# Optimizing a Trainium2 kernel written in Bass

```python
import numpy as np
import jax
import jax.numpy as jnp

def _softmax(x, axis=-1):
    return jax.nn.softmax(x, axis=axis)

def _gelu(x):
    return jax.nn.gelu(x, approximate=True)

def _silu(x):
    return jax.nn.silu(x)

def _sigmoid(x):
    return jax.nn.sigmoid(x)

def _layernorm(x, axis=-1, eps=1e-05):
    m = jnp.mean(x, axis=axis, keepdims=True)
    v = jnp.var(x, axis=axis, keepdims=True)
    return (x - m) / jnp.sqrt(v + eps)

def _scatter_add(tgt, idx, src, axis=0):
    return tgt.at[idx].add(src)

def _segment_sum(src, seg, n):
    return jax.ops.segment_sum(src, seg, n)
kernel_name = 'mk_hybrid_d1_jaxref_r8_b95f43'

def setup_inputs(seed: int=0):
    np.random.seed(seed)
    _w = jnp.asarray

    def _L0_attn_a_setup():
        import jax, jax.numpy as jnp
        import numpy as np
        H = 128
        NH = 32
        D = H // NH
        M = 2
        BMIN, BMAX = (0.85, 0.9995)
        EPS = 1e-06
        ROPE_BASE = 10000.0
        LN_EPS = 1e-05

        def _rope(u, cos, sin):
            half = D // 2
            u1, u2 = (u[..., :half], u[..., half:])
            return jnp.concatenate([u1 * cos - u2 * sin, u1 * sin + u2 * cos], axis=-1)

        def _forward(x, Wq, Wk, Wv, Wbeta, bbeta, Wmix, bmix, Wout, bout, ln_g, ln_b):
            b, t, _ = x.shape
            q = (x @ Wq.T).reshape(b, t, NH, D)
            k = (x @ Wk.T).reshape(b, t, NH, D)
            v = (x @ Wv.T).reshape(b, t, NH, D)
            half = D // 2
            inv_freq = 1.0 / ROPE_BASE ** (jnp.arange(half, dtype=jnp.float32) / half)
            freqs = jnp.arange(t, dtype=jnp.float32)[:, None] * inv_freq
            cos = jnp.cos(freqs)[None, :, None, :]
            sin = jnp.sin(freqs)[None, :, None, :]
            q = _rope(q, cos, sin)
            k = _rope(k, cos, sin)
            phi_q = jax.nn.elu(q) + 1.0
            phi_k = jax.nn.elu(k) + 1.0
            beta = jnp.clip(jax.nn.sigmoid((x @ Wbeta.T + bbeta).reshape(b, t, NH, M)), BMIN, BMAX)
            mix = jax.nn.softmax((x @ Wmix.T + bmix).reshape(b, t, NH, M), axis=-1)

            def step(carry, xs):
                S, K = carry
                pq, pk, vt, bt, mt = xs
                K = K * bt[..., None] + pk[:, :, None, :]
                S = S * bt[..., None, None] + pk[:, :, None, :, None] * vt[:, :, None, None, :]
                num = jnp.einsum('bhd,bhmdc->bhmc', pq, S)
                den = jnp.einsum('bhd,bhmd->bhm', pq, K) + EPS
                y = jnp.sum(num / den[..., None] * mt[..., None], axis=2)
                return ((S, K), y)
            S0 = jnp.zeros((b, NH, M, D, D), x.dtype)
            K0 = jnp.zeros((b, NH, M, D), x.dtype)
            tf = lambda a: jnp.moveaxis(a, 1, 0)
            _, ys = jax.lax.scan(step, (S0, K0), (tf(phi_q), tf(phi_k), tf(v), tf(beta), tf(mix)))
            y = jnp.moveaxis(ys, 0, 1).reshape(b, t, H) @ Wout.T + bout
            z = x + y
            mu = z.mean(-1, keepdims=True)
            var = ((z - mu) ** 2).mean(-1, keepdims=True)
            return (z - mu) / jnp.sqrt(var + LN_EPS) * ln_g + ln_b
        key = jax.random.key(seed)
        ks = jax.random.split(key, 8)
        b, t = (4, 128)
        x = jax.random.normal(ks[0], (b, t, H), jnp.float32)
        sc = (6.0 / (H + H)) ** 0.5
        Wq = jax.random.uniform(ks[1], (H, H), jnp.float32, -sc, sc)
        Wk = jax.random.uniform(ks[2], (H, H), jnp.float32, -sc, sc)
        Wv = jax.random.uniform(ks[3], (H, H), jnp.float32, -sc, sc)
        Wout = jax.random.uniform(ks[4], (H, H), jnp.float32, -sc, sc)
        bout = jnp.zeros((H,), jnp.float32)
        scb = (6.0 / (H + NH * M)) ** 0.5
        Wbeta = jax.random.uniform(ks[5], (NH * M, H), jnp.float32, -scb, scb)
        targets = jnp.linspace(BMIN, BMAX, M)
        bbeta = jnp.tile(jnp.log(targets / (1.0 - targets)), NH)
        Wmix = jnp.zeros((NH * M, H), jnp.float32)
        bmix = jnp.zeros((NH * M,), jnp.float32)
        ln_g = jnp.ones((H,), jnp.float32)
        ln_b = jnp.zeros((H,), jnp.float32)
        return dict(x=x, Wq=Wq, Wk=Wk, Wv=Wv, Wbeta=Wbeta, bbeta=bbeta, Wmix=Wmix, bmix=bmix, Wout=Wout, bout=bout, ln_g=ln_g, ln_b=ln_b)
    _L0_attn_a_in = _L0_attn_a_setup()

    def _L0_attn_b_setup():
        import math
        import jax, jax.numpy as jnp
        import numpy as np
        B, T, C = (2, 256, 128)
        HEADS = 16
        HD = C // HEADS

        def _rope_tables(seq_len, dim):
            pos = jnp.arange(seq_len, dtype=jnp.float32)
            freqs = 1.0 / 10000.0 ** (jnp.arange(0, dim, 2, dtype=jnp.float32) / dim)
            ang = pos[:, None] * freqs[None, :]
            return (jnp.sin(ang)[None, :, None, :], jnp.cos(ang)[None, :, None, :])

        def _apply_rope(t, sin, cos, dim):
            t1, t2 = (t[..., :dim // 2], t[..., dim // 2:])
            return jnp.concatenate([t1 * cos + t2 * sin, t1 * sin - t2 * cos], axis=-1)
        key = jax.random.key(seed)
        ks = jax.random.split(key, 5)
        s = 0.02
        return {'x': jax.random.normal(ks[0], (B, T, C), jnp.float32), 'Wq': jax.random.normal(ks[1], (C, C), jnp.float32) * s, 'bq': jnp.zeros((C,), jnp.float32), 'Wk': jax.random.normal(ks[2], (C, HD), jnp.float32) * s, 'bk': jnp.zeros((HD,), jnp.float32), 'Wv': jax.random.normal(ks[3], (C, HD), jnp.float32) * s, 'bv': jnp.zeros((HD,), jnp.float32), 'Wo': jax.random.normal(ks[4], (C, C), jnp.float32) * s, 'bo': jnp.zeros((C,), jnp.float32)}
    _L0_attn_b_in = _L0_attn_b_setup()

    def _L0_ffn_setup():
        import jax, jax.numpy as jnp
        import numpy as np
        NUM_EXPERTS = 8
        HIDDEN = 128
        FFN = 512
        BATCH = 2
        SEQ = 256
        key = jax.random.key(seed)
        k_x, k_g, k_u, k_d = jax.random.split(key, 4)
        scale_in = 1.0 / np.sqrt(HIDDEN)
        scale_mid = 1.0 / np.sqrt(FFN)
        return {'hidden_states': jax.random.normal(k_x, (BATCH, SEQ, HIDDEN), dtype=jnp.float32), 'Wg': jax.random.normal(k_g, (NUM_EXPERTS, HIDDEN, FFN), dtype=jnp.float32) * scale_in, 'Wu': jax.random.normal(k_u, (NUM_EXPERTS, HIDDEN, FFN), dtype=jnp.float32) * scale_in, 'Wd': jax.random.normal(k_d, (NUM_EXPERTS, FFN, HIDDEN), dtype=jnp.float32) * scale_mid}
    _L0_ffn_in = _L0_ffn_setup()
    _d = {'L0_attn_a_x': _L0_attn_a_in['x'], 'L0_attn_a_Wq': _L0_attn_a_in['Wq'], 'L0_attn_a_Wk': _L0_attn_a_in['Wk'], 'L0_attn_a_Wv': _L0_attn_a_in['Wv'], 'L0_attn_a_Wbeta': _L0_attn_a_in['Wbeta'], 'L0_attn_a_bbeta': _L0_attn_a_in['bbeta'], 'L0_attn_a_Wmix': _L0_attn_a_in['Wmix'], 'L0_attn_a_bmix': _L0_attn_a_in['bmix'], 'L0_attn_a_Wout': _L0_attn_a_in['Wout'], 'L0_attn_a_bout': _L0_attn_a_in['bout'], 'L0_attn_a_ln_g': _L0_attn_a_in['ln_g'], 'L0_attn_a_ln_b': _L0_attn_a_in['ln_b'], 'L0_attn_b_Wq': _L0_attn_b_in['Wq'], 'L0_attn_b_bq': _L0_attn_b_in['bq'], 'L0_attn_b_Wk': _L0_attn_b_in['Wk'], 'L0_attn_b_bk': _L0_attn_b_in['bk'], 'L0_attn_b_Wv': _L0_attn_b_in['Wv'], 'L0_attn_b_bv': _L0_attn_b_in['bv'], 'L0_attn_b_Wo': _L0_attn_b_in['Wo'], 'L0_attn_b_bo': _L0_attn_b_in['bo'], 'L0_ffn_Wg': _L0_ffn_in['Wg'], 'L0_ffn_Wu': _L0_ffn_in['Wu'], 'L0_ffn_Wd': _L0_ffn_in['Wd']}
    _x0 = _d['L0_attn_a_x']
    _d['L0_attn_a_x'] = jax.random.normal(jax.random.fold_in(jax.random.key(seed), 1), (16, 256, 128), dtype=_x0.dtype)
    del _x0
    return _d

def reference(L0_attn_a_x, L0_attn_a_Wq, L0_attn_a_Wk, L0_attn_a_Wv, L0_attn_a_Wbeta, L0_attn_a_bbeta, L0_attn_a_Wmix, L0_attn_a_bmix, L0_attn_a_Wout, L0_attn_a_bout, L0_attn_a_ln_g, L0_attn_a_ln_b, L0_attn_b_Wq, L0_attn_b_bq, L0_attn_b_Wk, L0_attn_b_bk, L0_attn_b_Wv, L0_attn_b_bv, L0_attn_b_Wo, L0_attn_b_bo, L0_ffn_Wg, L0_ffn_Wu, L0_ffn_Wd):

    def _L0_attn_a_ref(x, Wq, Wk, Wv, Wbeta, bbeta, Wmix, bmix, Wout, bout, ln_g, ln_b):
        import jax, jax.numpy as jnp
        import numpy as np
        H = 128
        NH = 32
        D = H // NH
        M = 2
        BMIN, BMAX = (0.85, 0.9995)
        EPS = 1e-06
        ROPE_BASE = 10000.0
        LN_EPS = 1e-05

        def _rope(u, cos, sin):
            half = D // 2
            u1, u2 = (u[..., :half], u[..., half:])
            return jnp.concatenate([u1 * cos - u2 * sin, u1 * sin + u2 * cos], axis=-1)

        def _forward(x, Wq, Wk, Wv, Wbeta, bbeta, Wmix, bmix, Wout, bout, ln_g, ln_b):
            b, t, _ = x.shape
            q = (x @ Wq.T).reshape(b, t, NH, D)
            k = (x @ Wk.T).reshape(b, t, NH, D)
            v = (x @ Wv.T).reshape(b, t, NH, D)
            half = D // 2
            inv_freq = 1.0 / ROPE_BASE ** (jnp.arange(half, dtype=jnp.float32) / half)
            freqs = jnp.arange(t, dtype=jnp.float32)[:, None] * inv_freq
            cos = jnp.cos(freqs)[None, :, None, :]
            sin = jnp.sin(freqs)[None, :, None, :]
            q = _rope(q, cos, sin)
            k = _rope(k, cos, sin)
            phi_q = jax.nn.elu(q) + 1.0
            phi_k = jax.nn.elu(k) + 1.0
            beta = jnp.clip(jax.nn.sigmoid((x @ Wbeta.T + bbeta).reshape(b, t, NH, M)), BMIN, BMAX)
            mix = jax.nn.softmax((x @ Wmix.T + bmix).reshape(b, t, NH, M), axis=-1)

            def step(carry, xs):
                S, K = carry
                pq, pk, vt, bt, mt = xs
                K = K * bt[..., None] + pk[:, :, None, :]
                S = S * bt[..., None, None] + pk[:, :, None, :, None] * vt[:, :, None, None, :]
                num = jnp.einsum('bhd,bhmdc->bhmc', pq, S)
                den = jnp.einsum('bhd,bhmd->bhm', pq, K) + EPS
                y = jnp.sum(num / den[..., None] * mt[..., None], axis=2)
                return ((S, K), y)
            S0 = jnp.zeros((b, NH, M, D, D), x.dtype)
            K0 = jnp.zeros((b, NH, M, D), x.dtype)
            tf = lambda a: jnp.moveaxis(a, 1, 0)
            _, ys = jax.lax.scan(step, (S0, K0), (tf(phi_q), tf(phi_k), tf(v), tf(beta), tf(mix)))
            y = jnp.moveaxis(ys, 0, 1).reshape(b, t, H) @ Wout.T + bout
            z = x + y
            mu = z.mean(-1, keepdims=True)
            var = ((z - mu) ** 2).mean(-1, keepdims=True)
            return (z - mu) / jnp.sqrt(var + LN_EPS) * ln_g + ln_b
        return _forward(x, Wq, Wk, Wv, Wbeta, bbeta, Wmix, bmix, Wout, bout, ln_g, ln_b)

    def _L0_attn_b_ref(x, Wq, bq, Wk, bk, Wv, bv, Wo, bo):
        import math
        import jax, jax.numpy as jnp
        import numpy as np
        B, T, C = (2, 256, 128)
        HEADS = 16
        HD = C // HEADS

        def _rope_tables(seq_len, dim):
            pos = jnp.arange(seq_len, dtype=jnp.float32)
            freqs = 1.0 / 10000.0 ** (jnp.arange(0, dim, 2, dtype=jnp.float32) / dim)
            ang = pos[:, None] * freqs[None, :]
            return (jnp.sin(ang)[None, :, None, :], jnp.cos(ang)[None, :, None, :])

        def _apply_rope(t, sin, cos, dim):
            t1, t2 = (t[..., :dim // 2], t[..., dim // 2:])
            return jnp.concatenate([t1 * cos + t2 * sin, t1 * sin - t2 * cos], axis=-1)
        Bx, Tx, Cx = x.shape
        q = (x @ Wq + bq).reshape(Bx, Tx, HEADS, HD)
        k = (x @ Wk + bk)[:, :, None, :]
        v = (x @ Wv + bv)[:, :, None, :]
        sin, cos = _rope_tables(Tx, HD)
        q = _apply_rope(q, sin, cos, HD)
        k = _apply_rope(k, sin, cos, HD)
        att = jnp.einsum('bthd,bThd->bhtT', q, k) / math.sqrt(HD)
        causal = jnp.triu(jnp.ones((Tx, Tx), bool), 1)
        att = jnp.where(causal, -jnp.inf, att)
        att = jax.nn.softmax(att, axis=-1)
        out = jnp.einsum('bhtT,bThd->bthd', att, v).reshape(Bx, Tx, Cx)
        return out @ Wo + bo

    def _L0_ffn_ref(hidden_states, Wg, Wu, Wd):
        import jax, jax.numpy as jnp
        import numpy as np
        NUM_EXPERTS = 8
        HIDDEN = 128
        FFN = 512
        BATCH = 2
        SEQ = 256
        B, S, H = hidden_states.shape
        x = hidden_states.reshape(-1, H)

        def expert_step(acc, w):
            wg, wu, wd = w
            h = jax.nn.silu(x @ wg) * (x @ wu)
            return (acc + h @ wd, None)
        acc, _ = jax.lax.scan(expert_step, jnp.zeros_like(x), (Wg, Wu, Wd))
        return acc.reshape(B, S, H)
    x = L0_attn_a_x
    x = x + _L0_attn_a_ref(_layernorm(x, axis=-1), L0_attn_a_Wq, L0_attn_a_Wk, L0_attn_a_Wv, L0_attn_a_Wbeta, L0_attn_a_bbeta, L0_attn_a_Wmix, L0_attn_a_bmix, L0_attn_a_Wout, L0_attn_a_bout, L0_attn_a_ln_g, L0_attn_a_ln_b)
    x = x + _L0_ffn_ref(_layernorm(x, axis=-1), L0_ffn_Wg, L0_ffn_Wu, L0_ffn_Wd)
    x = x + _L0_attn_b_ref(_layernorm(x, axis=-1), L0_attn_b_Wq, L0_attn_b_bq, L0_attn_b_Wk, L0_attn_b_bk, L0_attn_b_Wv, L0_attn_b_bv, L0_attn_b_Wo, L0_attn_b_bo)
    x = x + _L0_ffn_ref(_layernorm(x, axis=-1), L0_ffn_Wg, L0_ffn_Wu, L0_ffn_Wd)
    return x

_drawn_inputs = setup_inputs


def setup_inputs(seed=0):
    import zlib

    import numpy as np

    out = dict(_drawn_inputs(seed))
    spreads = {'L0_attn_a_Wmix': (0.0, 0.374),
     'L0_attn_a_bmix': (0.0, 2.0),
     'L0_attn_a_bout': (0.0, 0.1),
     'L0_attn_a_ln_g': (1.0, 0.2),
     'L0_attn_a_ln_b': (0.0, 0.1),
     'L0_attn_b_bq': (0.0, 0.8),
     'L0_attn_b_bk': (0.0, 0.8),
     'L0_attn_b_bv': (0.0, 0.8),
     'L0_attn_b_bo': (0.0, 0.1)}
    factors = {'L0_attn_a_Wbeta': 6.6,
     'L0_attn_b_Wq': 8.0,
     'L0_attn_b_Wk': 8.0,
     'L0_attn_b_Wv': 8.0,
     'L0_attn_b_Wo': 5.39}
    for name, (base, spread) in spreads.items():
        noise = np.random.default_rng([zlib.crc32(name.encode()), seed]).standard_normal(out[name].shape)
        drawn = base * np.exp(spread * noise) if base else spread * noise
        out[name] = jnp.asarray(drawn.astype(out[name].dtype))
    for name, factor in factors.items():
        out[name] = (out[name] * factor).astype(out[name].dtype)
    return out
```

```python
from collections import namedtuple
from contextlib import ExitStack

import numpy as np
import concourse.bass as bass
from concourse import mybir

F32 = mybir.dt.float32
F32R = mybir.dt.float32r
BF16 = mybir.dt.bfloat16
ALU = mybir.AluOpType
ACT = mybir.ActivationFunctionType
AX = mybir.AxisListType

P = 128
NSEQ, SEQ, C = 16, 256, 128
TOK = 512
SUB = TOK // P
NT = NSEQ * SEQ // TOK
SPT = TOK // SEQ
HA, DA, MA = 32, 4, 2
HB, DB = 16, 8
NE, FFN = 8, 512
FC = FFN // P
LN_EPS = 1e-5
DEN_EPS = 1e-6
BMIN, BMAX = 0.85, 0.9995
NG, NJ = 4, 4
RG = 32
MASKED = -1e30


def constants():
    c = {}
    eye = np.eye(P, dtype=np.float32)
    c["ident"] = eye
    pos = np.arange(SEQ, dtype=np.float32)
    inv = (1.0 / 10000.0 ** (np.arange(DA // 2, dtype=np.float32) / (DA // 2))).astype(np.float32)
    d = np.arange(P) // HA
    ang = pos[None, :] * inv[d % (DA // 2)][:, None]
    c["cos_a"] = np.cos(ang)
    c["sin_a"] = np.sin(ang) * np.where(d < DA // 2, -1.0, 1.0)[:, None]
    inv = (1.0 / 10000.0 ** (np.arange(0, DB, 2, dtype=np.float32) / DB)).astype(np.float32)
    d = np.arange(P) % DB
    ang = pos[None, :] * inv[d % (DB // 2)][:, None]
    c["cos_b"] = np.cos(ang) * np.where(d < DB // 2, 1.0, -1.0)[:, None]
    c["sin_b"] = np.sin(ang)
    h = np.arange(P) % HA
    q = np.arange(P) // HA
    same = (h[:, None] == h[None, :]).astype(np.float32)
    for s in range(4):
        c[f"sum_{s}"] = same * (q[None, :] == s)
    for s in range(4):
        c[f"rep_{s}"] = same * (q[:, None] == s)
    for j in range(NJ):
        hi = np.zeros((P, P), np.float32)
        lo = np.zeros((P, P), np.float32)
        for g in range(NG):
            for x in range(DB):
                src = (NJ * g + j) * DB + x
                hi[src, RG * g + x] = hi[src, RG * g + DB + x] = lo[src, RG * g + 2 * DB + x] = 1
        c[f"qhi_{j}"], c[f"qlo_{j}"] = hi, lo
    hi = np.zeros((P, P), np.float32)
    lo = np.zeros((P, P), np.float32)
    for g in range(NG):
        for x in range(DB):
            hi[x, RG * g + x] = hi[x, RG * g + 2 * DB + x] = lo[x, RG * g + DB + x] = 1
    c["khi"], c["klo"] = hi, lo
    ones = np.zeros((P, P), np.float32)
    for g in range(NG):
        ones[0, RG * g + 3 * DB:RG * g + 3 * DB + 2] = 1
    c["kone"] = ones
    r = np.arange(P)
    c["mask_rows"] = np.where(r[None, :] > r[:, None], MASKED, 0.0)
    c["mask_cols"] = np.where(r[:, None] > r[None, :], MASKED, 0.0)
    c["sign"] = np.where((np.arange(P) // HA) % MA == 0, 1.0, -1.0)[:, None]
    return {k: np.asarray(v, np.float32) for k, v in c.items()}


_C = constants()
CPOS, _at = {}, 0
for _k, _v in _C.items():
    CPOS[_k] = (_at, _v.shape[1])
    _at += _v.shape[1]
CWIDTH = _at


class Tile:

    def __init__(self, n, p):
        self.n, self.p = n, p

    def __add__(self, k):
        return Tile(self.n + k, (self.p + k) % 2)

    def real(self):
        return not isinstance(self.n, int) or 0 <= self.n < NT


def after(eng, sem, n):
    if not (isinstance(n, int) and n <= 0):
        eng.wait_ge(sem, n)


def run_steps(eng, step):
    for n in (-1, 0, 1):
        step(Tile(n, n % 2))
    with eng.Fori(1, NT // 2 - 1) as i:
        step(Tile(2 * i, 0))
        step(Tile(2 * i + 1, 1))
    for n in (NT - 2, NT - 1, NT):
        step(Tile(n, n % 2))


def program(nc, a_x, a_Wq, a_Wk, a_Wv, a_Wbeta, a_bbeta, a_Wmix, a_bmix, a_Wout, a_bout, a_ln_g, a_ln_b,
            b_Wq, b_bq, b_Wk, b_bk, b_Wv, b_bv, b_Wo, b_bo, f_Wg, f_Wu, f_Wd, consts, out):
    ctx = ExitStack()
    with ctx:
        def sb(name, shape, dt=F32):
            return ctx.enter_context(nc.sbuf_tensor(name, shape, dt))

        def sem(name):
            return ctx.enter_context(nc.semaphore(name))

        def sems(prefix, names):
            return namedtuple(prefix, names)(*[sem(f"{prefix}_{n}") for n in names.split()])

        def spread(ap, n):
            return bass.AP(ap.tensor, ap.offset, [ap.ap[0], [0, n], ap.ap[1]])

        def spread_in(ap, n):
            return bass.AP(ap.tensor, ap.offset, [*ap.ap, [0, n]])

        def r3(ap, n):
            return ap.rearrange("p (a b) -> p a b", a=n)

        single = {i: ctx.enter_context(nc.psum_tensor(f"bank{i}", [P, 512], F32)) for i in (0, 1, 6, 7)}
        pair = [ctx.enter_context(nc.psum_tensor(f"pair{i}", [P, 2, 512], F32)) for i in range(2)]
        bank = [single[i][:, :] if i in single else pair[i // 2 - 1][:, i % 2, :] for i in range(8)]

        X = sb("X", [P, NT, SUB, C])
        CST = sb("CST", [P, CWIDTH])

        def cst(name):
            at, w = CPOS[name]
            return CST[:, at:at + w]

        ident = cst("ident")
        SELR = sb("SELR", [P, 2 * NJ + 4, P], F32R)
        MASKB = sb("MASKB", [P, 3, P], BF16)
        ONES = sb("ONES", [P, P])
        ONESR = sb("ONESR", [1, TOK], F32R)
        HALF = sb("HALF", [P, SUB])
        WOUT = sb("WOUT", [P, C])
        WBH = sb("WBH", [P, 4, P], F32R)
        WBL = sb("WBL", [P, 4, P], F32R)
        WVH = sb("WVH", [P, DB], F32R)
        WVL = sb("WVL", [P, DB], F32R)
        WOB = sb("WOB", [P, C])
        BROW = sb("BROW", [1, 2 * C + DB])
        GB = sb("GB", [P, 2, C])
        BQK = sb("BQK", [P, 4])
        BBETA = sb("BBETA", [P, MA])
        BMIX = sb("BMIX", [P, MA])
        BMIXD = sb("BMIXD", [P, 2])
        XN = sb("XN", [P, 2, SUB, C])
        ST = sb("ST", [P, 2, SUB, 6])
        MV = sb("MV", [P, 2, SUB, 2])
        VE = sb("VE", [P, 2, SUB])
        RSTD = sb("RSTD", [P, 2, SUB])
        ST2 = sb("ST2", [P, SUB, 6])
        MV2 = sb("MV2", [P, SUB, 2])
        VE2 = sb("VE2", [P, SUB])
        RSTD2 = sb("RSTD2", [P, SUB])

        ARENA = sb("ARENA", [P, 20224])
        ARENA_R = sb("ARENA_R", [P, 18432], F32R)
        at = {F32: 0, F32R: 0}

        def take(*shape, dt=F32):
            n = int(np.prod(shape))
            a = {F32: ARENA, F32R: ARENA_R}[dt]
            ap = a[:, at[dt]:at[dt] + n]
            at[dt] += n
            names = "abcd"[:len(shape)]
            return ap.rearrange(f"p ({' '.join(names)}) -> p {' '.join(names)}", **dict(zip(names, shape)))

        def rewind():
            at[F32] = at[F32R] = 0

        WRAW = take(6, P)
        WT = take(6, P)
        LA = take(12, P)
        WB = take(4, P)
        WQB, WKB, WVB = take(C), take(DB), take(DB)
        rewind()
        S = take(MA, 5, TOK)
        KV = take(5, TOK)
        R1 = take(2, TOK)
        R2 = take(2, TOK)
        U = take(2, TOK)
        EX = take(2, TOK)
        PQ = take(2, TOK)
        TB = take(MA, TOK)
        BETA = take(MA, TOK)
        MIX = take(2, SEQ)
        DP, RC, WGT = take(SEQ), take(SEQ), take(SEQ)
        RS = take(MA, TOK)
        AY = take(MA, TOK)
        Y = take(2, TOK)
        Z = take(SUB, C)
        ZN = take(SUB, C)
        XH = take(2, TOK, dt=F32R)
        XL = take(2, TOK, dt=F32R)
        LAH = take(12, P, dt=F32R)
        LAL = take(12, P, dt=F32R)
        rewind()
        B1 = take(2, TOK)
        B2 = take(2, TOK)
        QK = take(2, TOK)
        PT = take(2, HB * SEQ + HB * P)
        OB = take(2, 2, C)
        OT = take(2, 2 * C)
        VA = take(2, SUB, DB + 1)
        NM = take(2, 2, HB)
        RO = take(2, HB)
        take(2, TOK, dt=F32R), take(2, TOK, dt=F32R)
        QKH = take(2, TOK, dt=F32R)
        QKL = take(2, TOK, dt=F32R)
        QST = take(2, NJ, TOK, dt=F32R)
        KST = take(2, TOK, dt=F32R)
        NMP = take(2, 2, NJ, P, dt=F32R)
        Q2 = take(2, NJ, SEQ, dt=F32R)
        rewind()
        YACC = take(NT, TOK)
        WS = take(2, 3, FFN)
        SG = take(2, TOK)
        HF = take(FC, TOK)
        YS = take(2, TOK)
        XTH = take(NT, TOK, dt=F32R)
        XTL = take(NT, TOK, dt=F32R)
        WH = take(2, 3, FFN, dt=F32R)
        WL = take(2, 3, FFN, dt=F32R)
        HH = take(FC, TOK, dt=F32R)
        HL = take(FC, TOK, dt=F32R)

        ld = sems("ld", "x0 x1 x consts wa wb bias")
        pr = sems("prep", "wt wtc la lah lal ones selr wb wbh wbl wout bmix nmp vone")
        PROJ = ["k", "ks", "q", "qs", "b0", "b1", "mx", "v0", "v1", "v2", "v3"]
        PBANK = {n: 1 + i % 3 for i, n in enumerate(PROJ)}
        a_ready = {n: sem(f"a_{n}_ready") for n in PROJ}
        a_used = {n: sem(f"a_{n}_used") for n in PROJ}
        A = sems("a", "u_k u_q ex_k ex_q re_k re_q phi_k phi_q clip scaled beta scan prod0 prod1 num den dp rc wgt rep "
                      "rs ay y z zsum st2 mv2 ve2 rstd2 zn zg zb done")
        NORM = "st mv ve rstd xn tp hi lo"
        norm_sems = sems("norm", NORM)

        def norm_of(phase, names="", *more):
            return namedtuple("phase", f"{NORM} base {names}")(*norm_sems, phase * NT, *more)

        n_a, n_b = norm_of(0), norm_of(2)
        BPROJ = ["q", "qs", "k", "ks"]
        b_ready = {n: sem(f"b_{n}_ready") for n in BPROJ}
        b_used = {n: sem(f"b_{n}_used") for n in BPROJ}
        B = sems("b", "u_q u_k hi lo v_ready v_used st_ready st_used kst_ready kst_used row_ready row_used nmh nml "
                      "q2_ready q2_used t_ready t_used pv ro o ot otc out done")
        FSEMS = "wload0 wload1 wh wl gate up sil mul hh hl d acc ys back done zero"
        f = [norm_of(2 * i + 1, FSEMS, *sems(f"f{i}", FSEMS)) for i in range(2)]
        stored = sem("stored")
        carried = sem("carried")

        def carry(eng):
            eng.sem_inc(carried, 1)

        x_tok = a_x.rearrange("b t c -> (b t) c").rearrange("(n s p) c -> p n s c", n=NT, p=P)
        o_tok = out.rearrange("b t c -> (b t) c").rearrange("(n s p) c -> p n s c", n=NT, p=P)

        block = ctx.enter_context(nc.Block())

        def seqs(ap):
            return ap.rearrange("p (a t) -> p a t", a=SPT)

        def by_sub(ap):
            return ap.rearrange("p (s c) -> p s c", s=SUB)

        def split_product(pe, dst, wh, wl, xh, xl, start=True, stop=True):
            pe.matmul(dst, wh, xh, start=start, stop=False)
            pe.matmul(dst, wh, xl, start=False, stop=False)
            return pe.matmul(dst, wl, xh, start=False, stop=stop)

        def pairs(eng, step, n=NT):
            step(Tile(0, 0))
            step(Tile(1, 1))
            with eng.Fori(1, n // 2) as i:
                step(Tile(2 * i, 0))
                step(Tile(2 * i + 1, 1))

        def norm_stats(v, s, t):
            n = s.base + t.n
            after(v, s.mv, SUB * (n - 1))
            for i in range(SUB):
                v.bn_stats(ST[:, t.p, i, :], X[:, t.n, i, :]).then_inc(s.st, 1)
            after(v, s.st, SUB * (n + 1))
            after(v, s.ve, n - 1)
            after(v, s.xn, SUB * (n - 1))
            carry(v)
            for i in range(SUB):
                v.bn_aggr(MV[:, t.p, i, :], ST[:, t.p, i, :]).then_inc(s.mv, 1)

        def norm_rstd(g, s, t):
            n = s.base + t.n
            after(g, s.mv, SUB * (n + 1))
            after(g, s.rstd, n - 1)
            carry(g)
            g.tensor_scalar(VE[:, t.p, :], MV[:, t.p, :, 1], LN_EPS, None, ALU.add).then_inc(s.ve, 1)
            after(g, s.ve, n + 1)
            after(g, s.xn, SUB * (n - 1))
            g.tensor_tensor(RSTD[:, t.p, :], VE[:, t.p, :], HALF[:, :], ALU.pow).then_inc(s.rstd, 1)

        def norm_apply(v, s, t):
            n = s.base + t.n
            after(v, s.rstd, n + 1)
            after(v, s.tp, n - 1)
            for i in range(SUB):
                v.tensor_scalar(XN[:, t.p, i, :], X[:, t.n, i, :], MV[:, t.p, i, 0:1], RSTD[:, t.p, i:i + 1],
                                ALU.subtract, ALU.mult).then_inc(s.xn, 1)

        def norm_turn(pe, s, t, dst):
            n = s.base + t.n
            after(pe, s.xn, SUB * (n + 1))
            for i in range(SUB):
                m = pe.transpose(dst[:, i * P:(i + 1) * P], XN[:, t.p, i, :], ident)
            m.then_inc(s.tp, 1)

        def norm_hi(act, s, t, src, hi):
            after(act, s.tp, s.base + t.n + 1)
            act.activation(hi, src, ACT.Copy).then_inc(s.hi, 1)

        def norm_lo(v, s, t, src, hi, lo):
            after(v, s.hi, s.base + t.n + 1)
            v.tensor_tensor(lo, src, hi.bitcast(F32), ALU.subtract).then_inc(s.lo, 1)

        BIAS_LOADS = 2 * DA + 5 + 1 + 3 * 2 * HB
        ffn_starts = ((A.done, NT), (B.done, NSEQ))

        @block.sync
        def _(sp):
            for n in range(NT):
                sp.dma_start(X[:, n, :, :], x_tok[:, n]).then_inc((ld.x0, ld.x1)[n] if n < 2 else ld.x, 16)
                if n == 0:
                    sp.dma_start(CST[:, :], consts).then_inc(ld.consts, 16)
                    for i, w in enumerate((a_Wq, a_Wk, a_Wv, a_Wbeta, a_Wmix, a_Wout)):
                        sp.dma_start(WRAW[0:w.shape[0], i, :], w).then_inc(ld.wa, 16)
            for d in range(DA):
                rows = slice(d * HA, (d + 1) * HA)
                sp.dma_start(BBETA[rows, :], a_bbeta.rearrange("(h m) -> h m", m=MA)).then_inc(ld.bias, 16)
                sp.dma_start(BMIX[rows, :], a_bmix.rearrange("(h m) -> h m", m=MA)).then_inc(ld.bias, 16)
            sp.dma_start(WQB[:, :], b_Wq).then_inc(ld.wb, 16)
            sp.dma_start(WKB[:, :], b_Wk).then_inc(ld.wb, 16)
            sp.dma_start(WVB[:, :], b_Wv).then_inc(ld.wb, 16)
            sp.dma_start(WOB[:, :], b_Wo).then_inc(ld.wb, 16)
            row = lambda v: v.rearrange("(a n) -> a n", a=1)
            sp.dma_start(BROW[:, 0:C], row(a_bout)).then_inc(ld.bias, 16)
            sp.dma_start(BROW[:, C:2 * C], row(b_bo)).then_inc(ld.bias, 16)
            sp.dma_start(BROW[:, 2 * C:], row(b_bv)).then_inc(ld.bias, 16)
            sp.dma_start(GB[:, 0, :], row(a_ln_g).broadcast_to([P, C])).then_inc(ld.bias, 16)
            sp.dma_start(GB[:, 1, :], row(a_ln_b).broadcast_to([P, C])).then_inc(ld.bias, 16)
            col = lambda v: v.rearrange("(n a) -> n a", a=1)
            half = DB // 2
            sp.dma_start(BQK[:, 0:1], col(b_bq)).then_inc(ld.bias, 16)
            for h in range(HB):
                for lo in (0, half):
                    dst = slice(h * DB + lo, h * DB + lo + half)
                    src = slice(h * DB + half - lo, h * DB + 2 * half - lo)
                    sp.dma_start(BQK[dst, 1:2], col(b_bq)[src]).then_inc(ld.bias, 16)
                    sp.dma_start(BQK[dst, 2:3], col(b_bk)[lo:lo + half]).then_inc(ld.bias, 16)
                    sp.dma_start(BQK[dst, 3:4], col(b_bk)[half - lo:2 * half - lo]).then_inc(ld.bias, 16)
            for i in range(2):
                s = f[i]
                wload = (s.wload0, s.wload1)
                sp.wait_ge(*ffn_starts[i])

                def load(x, u):
                    after(sp, s.wl, x - 1)
                    carry(sp)
                    sp.dma_start(WS[:, u, 0, :], f_Wg[x]).then_inc(wload[u], 16)
                    sp.dma_start(WS[:, u, 1, :], f_Wu[x]).then_inc(wload[u], 16)
                    sp.dma_start(WS[:, u, 2, :].rearrange("p (k c) -> p k c", k=FC),
                                 f_Wd[x].rearrange("(k p) c -> p k c", p=P)).then_inc(wload[u], 16)

                load(0, 0)
                load(1, 1)
                with sp.Fori(1, NE // 2) as h:
                    load(2 * h, 0)
                    load(2 * h + 1, 1)
            for n in range(NT):
                sp.wait_ge(f[1].done, n + 1)
                sp.dma_start(o_tok[:, n], X[:, n, :, :]).then_inc(stored, 16)
            sp.wait_ge(stored, 16 * NT)

        def ffn_pool(g, i):
            s = f[i]
            g.wait_ge(*ffn_starts[i])
            g.memset(YACC[:, :, :], 0.0).then_inc(s.zero, 1)
            pairs(g, lambda t: norm_rstd(g, s, t))

            def split(h, u):
                x = 2 * h + u
                g.wait_ge((s.wload0, s.wload1)[u], 48 * (h + 1))
                if not isinstance(x, int):
                    g.wait_ge(s.d, FC + FC * NT * (x - 1))
                carry(g)
                g.tensor_copy(WH[:, u, :, :], WS[:, u, :, :]).then_inc(s.wh, 1)
                g.wait_ge(s.wh, x + 1)
                g.tensor_tensor(WL[:, u, :, :], WS[:, u, :, :], WH[:, u, :, :].bitcast(F32),
                                ALU.subtract).then_inc(s.wl, 1)

            split(0, 0)
            split(0, 1)
            with g.Fori(1, NE // 2) as h:
                split(h, 0)
                split(h, 1)

        @block.gpsimd
        def _(g):
            g.memset(ONES[:, :], 1.0).then_inc(pr.ones, 1)
            g.memset(HALF[:, :], -0.5).then_inc(pr.ones, 1)
            g.wait_ge(ld.wa, 96)
            g.tensor_copy(LA[:, 0, :].rearrange("p (c h) -> p c h", c=DA),
                          WRAW[:, 5, :].rearrange("p (h c) -> p c h", c=DA)).then_inc(pr.wout, 1)
            g.wait_ge(pr.wtc, 6)
            g.memset(LA[:, 10:12, :], 0.0).then_inc(pr.la, 1)
            g.wait_ge(pr.la, 1)
            hd = lambda k: WT[:, k, :].rearrange("p (h d) -> p d h", d=DA)
            dh = lambda k: LA[:, k, :].rearrange("p (d h) -> p d h", d=DA)
            for k, w in ((0, 1), (2, 0)):
                g.tensor_copy(dh(k), hd(w)).then_inc(pr.la, 1)
                g.tensor_copy(dh(k + 1)[:, 0:2, :], hd(w)[:, 2:4, :]).then_inc(pr.la, 1)
                g.tensor_copy(dh(k + 1)[:, 2:4, :], hd(w)[:, 0:2, :]).then_inc(pr.la, 1)
            for c in range(DA):
                g.tensor_copy(dh(4 + c), spread(hd(2)[:, c, :], DA)).then_inc(pr.la, 1)
            for m in range(MA):
                hm = WT[:, 3, 0:HA * MA].rearrange("p (h m) -> p m h", m=MA)
                g.tensor_copy(dh(8 + m), spread(hm[:, m, :], DA)).then_inc(pr.la, 1)
            hm = WT[:, 4, 0:HA * MA].rearrange("p (h m) -> p m h", m=MA)
            for b in range(SPT):
                dst = LA[:, 10 + b, :].rearrange("p (b m h) -> p b m h", b=SPT, m=MA)
                for m in range(MA):
                    g.tensor_tensor(dst[:, b, m, :], hm[:, m, :], hm[:, 1 - m, :], ALU.subtract).then_inc(pr.la, 1)
            g.wait_ge(pr.la, 17)
            g.tensor_copy(LAH[:, :, :], LA[:, :, :]).then_inc(pr.lah, 1)
            g.wait_ge(pr.lah, 1)
            g.tensor_tensor(LAL[:, :, :], LA[:, :, :], LAH[:, :, :].bitcast(F32), ALU.subtract).then_inc(pr.lal, 1)
            g.tensor_scalar(WOUT[:, :], WT[:, 5, :], 0.5, None, ALU.mult).then_inc(pr.wout, 1)
            g.wait_ge(ld.wb, 64)
            hd = lambda k: WB[:, k, :].rearrange("p (h d) -> p h d", d=DB)
            wq = WQB[:, :].rearrange("p (h d) -> p h d", d=DB)
            half = DB // 2
            g.tensor_copy(WB[:, 0, :], WQB[:, :]).then_inc(pr.wb, 1)
            g.tensor_copy(hd(1)[:, :, 0:half], wq[:, :, half:DB]).then_inc(pr.wb, 1)
            g.tensor_copy(hd(1)[:, :, half:DB], wq[:, :, 0:half]).then_inc(pr.wb, 1)
            g.tensor_copy(hd(2), spread(WKB[:, :], HB)).then_inc(pr.wb, 1)
            g.tensor_copy(hd(3)[:, :, 0:half], spread(WKB[:, half:DB], HB)).then_inc(pr.wb, 1)
            g.tensor_copy(hd(3)[:, :, half:DB], spread(WKB[:, 0:half], HB)).then_inc(pr.wb, 1)
            g.wait_ge(pr.wb, 6)
            g.tensor_copy(WBH[:, :, :], WB[:, :, :]).then_inc(pr.wbh, 1)
            g.tensor_copy(WVH[:, :], WVB[:, :]).then_inc(pr.wbh, 1)
            g.wait_ge(pr.wbh, 2)
            g.tensor_tensor(WBL[:, :, :], WB[:, :, :], WBH[:, :, :].bitcast(F32), ALU.subtract).then_inc(pr.wbl, 1)
            g.tensor_tensor(WVL[:, :], WVB[:, :], WVH[:, :].bitcast(F32), ALU.subtract).then_inc(pr.wbl, 1)
            g.wait_ge(ld.consts, 16)
            at0 = CPOS["qhi_0"][0]
            for j in range(NJ):
                g.tensor_copy(SELR[:, j, :], cst(f"qhi_{j}")).then_inc(pr.selr, 1)
                g.tensor_copy(SELR[:, NJ + j, :], cst(f"qlo_{j}")).then_inc(pr.selr, 1)
            for k, name in enumerate(("khi", "klo", "kone", "ident")):
                g.tensor_copy(SELR[:, 2 * NJ + k, :], cst(name)).then_inc(pr.selr, 1)
            for k, name in enumerate(("mask_rows", "mask_cols", "ident")):
                g.tensor_copy(MASKB[:, k, :], cst(name)).then_inc(pr.selr, 1)
            g.tensor_copy(ONESR[:, 0:P], ONES[0:1, :]).then_inc(pr.selr, 1)
            for k in range(1, SUB):
                g.tensor_copy(ONESR[:, k * P:(k + 1) * P], ONES[0:1, :]).then_inc(pr.selr, 1)

            def step(t):
                nxt, old = t + 1, t + -1
                if nxt.real():
                    norm_rstd(g, n_a, nxt)
                if t.real():
                    for k, name in enumerate("kq"):
                        after(g, a_used[name], t.n + 1)
                        after(g, a_used[name + "s"], t.n + 1)
                        after(g, A.re_k if name == "k" else A.re_q, t.n)
                        after(g, A.phi_k if name == "k" else A.phi_q, t.n)
                        g.tensor_tensor(U[:, k, :], R1[:, k, :], R2[:, k, :],
                                        ALU.add).then_inc(A.u_k if name == "k" else A.u_q, 1)
                    after(g, a_used["b0"], t.n + 1)
                    after(g, a_used["b1"], t.n + 1)
                    carry(g)
                    g.tensor_scalar(TB[:, :, :], TB[:, :, :], 2 * BMAX - 1, 2 * BMIN - 1,
                                    ALU.min, ALU.max).then_inc(A.clip, 1)
                    after(g, A.clip, t.n + 1)
                    after(g, A.scan, 2 * 5 * t.n)
                    carry(g)
                    g.tensor_scalar(BETA[:, :, :], TB[:, :, :], 0.5, 0.5, ALU.mult, ALU.add).then_inc(A.scaled, 1)
                    after(g, A.scaled, t.n + 1)
                    carry(g)
                    g.memset(BETA[:, :, 0::SEQ], 0.0).then_inc(A.beta, 1)
                if old.real():
                    after(g, A.ay, 2 * (old.n + 1))
                    after(g, A.z, old.n - 1)
                    g.tensor_tensor(Y[:, old.p, :], AY[:, 0, :], AY[:, 1, :], ALU.add).then_inc(A.y, 1)
                    after(g, A.mv2, SUB * (old.n + 1))
                    after(g, A.rstd2, old.n)
                    carry(g)
                    g.tensor_scalar(VE2[:, :], MV2[:, :, 1], LN_EPS, None, ALU.add).then_inc(A.ve2, 1)
                    after(g, A.ve2, old.n + 1)
                    after(g, A.zn, SUB * old.n)
                    g.tensor_tensor(RSTD2[:, :], VE2[:, :], HALF[:, :], ALU.pow).then_inc(A.rstd2, 1)
                    after(g, A.zn, SUB * (old.n + 1))
                    g.tensor_tensor(ZN[:, :, :], ZN[:, :, :], spread(GB[:, 0, :], SUB), ALU.mult).then_inc(A.zg, 1)
                    after(g, A.zg, old.n + 1)
                    g.tensor_tensor(ZN[:, :, :], ZN[:, :, :], spread(GB[:, 1, :], SUB), ALU.add).then_inc(A.zb, 1)
                    after(g, A.zb, old.n + 1)
                    g.tensor_tensor(X[:, old.n, :, :], X[:, old.n, :, :], ZN[:, :, :], ALU.add).then_inc(A.done, 1)
                if t.real():
                    after(g, A.scan, 2 * 5 * (t.n + 1))
                    after(g, A.phi_q, t.n + 1)
                    g.tensor_tensor(S[:, 1, :, :], S[:, 1, :, :], spread(PQ[:, t.p, :], 5),
                                    ALU.mult).then_inc(A.prod1, 1)

            g.wait_ge(ld.bias, 16 * BIAS_LOADS)
            run_steps(g, step)
            ffn_pool(g, 0)

            g.wait_ge(f[0].done, NT)
            g.memset(VA[:, :, :, DB], 1.0).then_inc(pr.vone, 1)
            for k in range(2):
                g.tensor_scalar(NMP[:, k, :, :, :].rearrange("p a j r -> p (a j r)"), CST[:, 0:2 * NJ * P], 0.0, None,
                                ALU.mult).then_inc(pr.nmp, 1)

            def step_b(t):
                nxt = t + 1
                if nxt.real():
                    norm_rstd(g, n_b, nxt)
                    for k, name in enumerate("qk"):
                        after(g, b_used[name], nxt.n + 1)
                        after(g, b_used[name + "s"], nxt.n + 1)
                        after(g, B.hi, 2 * nxt.n)
                        after(g, B.lo, 2 * nxt.n)
                        g.tensor_tensor(QK[:, k, :], B1[:, k, :], B2[:, k, :],
                                        ALU.add).then_inc(B.u_q if k == 0 else B.u_k, 1)
            run_steps(g, step_b)
            ffn_pool(g, 1)

        def ffn_act(act, i):
            s = f[i]
            act.wait_ge(*ffn_starts[i])

            def norm(t):
                norm_hi(act, s, t, bank[6 + t.p], XTH[:, t.n, :])
            pairs(act, norm)
            act.sem_inc(s.sil, 2)

            def hi(m, k):
                act.wait_ge(s.mul, m * FC + k + 3)
                act.activation(HH[:, k, :], HF[:, k, :], ACT.Copy).then_inc(s.hh, 1)

            def tile(m):
                for k in range(FC):
                    act.wait_ge(s.gate, m * FC + k + 1)
                    act.wait_ge(s.mul, m * FC + k + 1)
                    act.activation(SG[:, k % 2, :], bank[k % 2], ACT.Silu).then_inc(s.sil, 1)
                    if k >= 1:
                        hi(m, k - 1)
                hi(m, FC - 1)

            with act.Fori(0, NE * NT // 2) as h:
                tile(2 * h)
                tile(2 * h + 1)

            def stage(t):
                after(act, s.acc, 2 + NT * NE)
                after(act, s.back, t.n - 1)
                act.activation(YS[:, t.p, :], YACC[:, t.n, :], ACT.Copy).then_inc(s.ys, 1)
            pairs(act, stage)

        @block.scalar
        def _(act):
            for k in range(6):
                w = P if k in (0, 1, 2, 5) else HA * MA
                act.wait_ge(pr.wt, k + 1)
                act.activation(WT[:, k, 0:w], bank[k][:, 0:w], ACT.Copy).then_inc(pr.wtc, 1)
            act.wait_ge(ld.bias, 16 * BIAS_LOADS)
            act.wait_ge(ld.consts, 16)
            act.activation(BBETA[:, :], BBETA[:, :], ACT.Copy, scale=0.5).then_inc(pr.bmix, 1)

            def step(t):
                nxt, old = t + 1, t + -1
                if t.real():
                    for k, name in enumerate("kq"):
                        u, ex, re, phi = ((A.u_k, A.ex_k, A.re_k, A.phi_k), (A.u_q, A.ex_q, A.re_q, A.phi_q))[k]
                        act.wait_ge(u, t.n + 1)
                        after(act, phi, t.n)
                        act.activation(EX[:, k, :], U[:, k, :], ACT.Exp).then_inc(ex, 1)
                        act.wait_ge(ex, t.n + 1)
                        act.activation(U[:, k, :], U[:, k, :], ACT.Relu).then_inc(re, 1)
                    for m in range(MA):
                        act.wait_ge(a_ready[f"b{m}"], t.n + 1)
                        after(act, A.scaled, t.n)
                        act.activation(TB[:, m, :], bank[PBANK[f"b{m}"]], ACT.Tanh, bias=BBETA[:, m:m + 1],
                                       scale=0.5).then_inc(a_used[f"b{m}"], 1)
                    act.wait_ge(a_ready["mx"], t.n + 1)
                    after(act, A.wgt, t.n - 1)
                    act.activation(MIX[:, t.p, :], bank[PBANK["mx"]][:, 0:SEQ], ACT.Tanh, bias=BMIXD[:, 1:2],
                                   scale=0.5).then_inc(a_used["mx"], 1)
                if old.real():
                    for m in range(MA):
                        act.wait_ge(A.rep, 2 * old.n + m + 1)
                        after(act, A.ay, 2 * old.n)
                        act.activation(RS[:, m, :], bank[7], ACT.Copy).then_inc(A.rs, 1)
                if nxt.real():
                    after(act, a_ready["v3"], nxt.n - 1)
                    norm_hi(act, n_a, nxt, bank[0], XH[:, nxt.p, :])

            act.wait_ge(pr.bmix, 3)
            run_steps(act, step)
            ffn_act(act, 0)

            def turned(n, p, b):
                act.wait_ge(B.ot, n + 1)
                after(act, B.out, n - 1)
                act.activation(OT[:, b, :], bank[7][:, 0:2 * C], ACT.Copy).then_inc(B.otc, 1)

            def slot(t, b, exps, outs):
                n = t.n * SPT + b
                if exps:
                    o = n - 1
                    ob = 1 - b
                    for h in range(2):
                        act.wait_ge(B.q2_ready, 2 * o + h + 1)
                        after(act, B.t_ready, 6 * (o - 1))
                        act.activation(Q2[:, ob, 2 * h:2 * h + 2, :],
                                       bank[6].rearrange("p (j t) -> p j t", j=2), ACT.Copy).then_inc(B.q2_used, 1)
                if outs:
                    turned(n - 2, None, b)
                if exps:
                    after(act, B.pv, o - 1)
                    for k in range(6):
                        act.wait_ge(B.t_ready, 6 * o + k + 1)
                        act.activation(PT[:, ob, k * 2 * TOK:(k + 1) * 2 * TOK].rearrange("p (a b) -> p a b", a=2),
                                       pair[k % 2][:, :, :], ACT.Exp, scale=DB ** -0.5).then_inc(B.t_used, 1)

            def step_b(t):
                nxt = t + 1
                for b in range(SPT):
                    n = t.n * SPT + b if isinstance(t.n, int) else None
                    slot(t, b, n is None or 0 <= n - 1 < NSEQ, n is None or 0 <= n - 2 < NSEQ)
                    if b == 0 and nxt.real():
                        after(act, B.v_ready, nxt.n - 1)
                        norm_hi(act, n_b, nxt, bank[6], XH[:, nxt.p, :])
                    if b == 1 and nxt.real():
                        for k in range(2):
                            act.wait_ge((B.u_q, B.u_k)[k], nxt.n + 1)
                            after(act, B.kst_ready, nxt.n)
                            act.activation(QKH[:, k, :], QK[:, k, :], ACT.Copy).then_inc(B.hi, 1)
                        for j in range(NJ):
                            act.wait_ge(B.st_ready, NJ * nxt.n + j + 1)
                            after(act, B.q2_ready, 4 * (nxt.n - 1))
                            after(act, B.row_ready, 24 * (nxt.n - 1))
                            act.activation(QST[:, nxt.p, j, :], bank[6], ACT.Copy).then_inc(B.st_used, 1)
                        act.wait_ge(B.kst_ready, nxt.n + 1)
                        after(act, B.t_ready, 12 * (nxt.n - 1))
                        act.activation(KST[:, nxt.p, :], bank[6], ACT.Copy).then_inc(B.kst_used, 1)

            act.wait_ge(f[0].done, NT)
            run_steps(act, step_b)
            ffn_act(act, 1)

        def ffn_pe(pe, i):
            s = f[i]
            pe.wait_ge(*ffn_starts[i])

            def norm(t):
                after(pe, s.lo, s.base + t.n - 1)
                norm_turn(pe, s, t, bank[6 + t.p])
            pairs(pe, norm)
            pe.sem_inc(s.d, FC)

            def gate_up(m, t, u, k):
                cols = slice(k * P, (k + 1) * P)
                pe.wait_ge(s.sil, m * FC + k + 1)
                split_product(pe, bank[k % 2], WH[:, u, 0, cols], WL[:, u, 0, cols],
                              XTH[:, t, :], XTL[:, t, :]).then_inc(s.gate, 1)
                pe.wait_ge(s.mul, m * FC + k + 1)
                split_product(pe, bank[2 + k % 2], WH[:, u, 1, cols], WL[:, u, 1, cols],
                              XTH[:, t, :], XTL[:, t, :]).then_inc(s.up, 1)

            def down(m, u, p, k):
                cols = slice(k * P, (k + 1) * P)
                if k == 0:
                    pe.wait_ge(s.acc, m + 1)
                pe.wait_ge(s.hl, m * FC + k + 1)
                split_product(pe, bank[4 + p], WH[:, u, 2, cols], WL[:, u, 2, cols], HH[:, k, :], HL[:, k, :],
                              start=(k == 0), stop=(k == FC - 1)).then_inc(s.d, 1)

            def tile(m, t, u, p, before):
                gate_up(m, t, u, 0)
                if before is not None:
                    down(m - 1, before, 1 - p, 2)
                gate_up(m, t, u, 1)
                if before is not None:
                    down(m - 1, before, 1 - p, 3)
                gate_up(m, t, u, 2)
                down(m, u, p, 0)
                gate_up(m, t, u, 3)
                down(m, u, p, 1)

            pe.wait_ge(s.lo, s.base + NT)
            with pe.Fori(0, NE // 2) as e:
                for u in range(2):
                    first = (2 * e + u) * NT
                    pe.wait_ge(s.wl, 2 * e + u + 1)
                    tile(first, 0, u, 0, None if u == 0 else 0)
                    tile(first + 1, 1, u, 1, u)
                    with pe.Fori(1, NT // 2) as h:
                        tile(first + 2 * h, 2 * h, u, 0, u)
                        tile(first + 2 * h + 1, 2 * h + 1, u, 1, u)
                last = (2 * e + 2) * NT - 1
                down(last, 1, 1, 2)
                down(last, 1, 1, 3)

            def back(t):
                after(pe, s.ys, t.n + 1)
                after(pe, s.done, t.n - 1)
                for k in range(SUB):
                    m = pe.transpose(bank[6 + t.p][:, k * P:(k + 1) * P], YS[:, t.p, k * P:(k + 1) * P], ident)
                m.then_inc(s.back, 1)
            pairs(pe, back)

        @block.tensor
        def _(pe):
            pe.wait_ge(ld.consts, 16)
            pe.wait_ge(ld.wa, 96)
            for k in range(6):
                w = P if k in (0, 1, 2, 5) else HA * MA
                src = WRAW[0:w, k, :]
                if k == 5:
                    pe.wait_ge(pr.wout, 1)
                    src = LA[:, 0, :]
                pe.transpose(bank[k][:, 0:w], src, ident[0:w, 0:w]).then_inc(pr.wt, 1)

            def project(t, names, last_use):
                for name in names:
                    bk = bank[PBANK[name]]
                    prev, back = last_use[name]
                    after(pe, a_used[prev], t.n + 1 - back)
                    if name == "mx":
                        for b in range(SPT):
                            cols = slice(b * SEQ, (b + 1) * SEQ)
                            m = split_product(pe, bk[:, 0:SEQ], LAH[:, 10 + b, :], LAL[:, 10 + b, :],
                                              XH[:, t.p, cols], XL[:, t.p, cols], start=(b == 0), stop=(b == SPT - 1))
                    else:
                        k = {"k": 0, "ks": 1, "q": 2, "qs": 3, "v0": 4, "v1": 5, "v2": 6, "v3": 7, "b0": 8, "b1": 9}[name]
                        m = split_product(pe, bk, LAH[:, k, :], LAL[:, k, :], XH[:, t.p, :], XL[:, t.p, :])
                    m.then_inc(a_ready[name], 1)

            last_use = {n: (PROJ[i - 3], 0) for i, n in enumerate(PROJ) if i >= 3}
            for n in PROJ[:3]:
                last_use[n] = ([x for x in PROJ if PBANK[x] == PBANK[n]][-1], 1)

            def step(t):
                nxt, old = t + 1, t + -1
                if t.real():
                    pe.wait_ge(n_a.lo, t.n + 1)
                    project(t, PROJ[:7], last_use)
                if old.real():
                    after(pe, A.ay, 2 * old.n)
                    for m in range(MA):
                        pe.wait_ge((A.prod0, A.prod1)[m], old.n + 1)
                        for c in range(DA):
                            x = pe.matmul(bank[5 + m], cst(f"sum_{c}"), S[:, m, c, :], start=(c == 0), stop=(c == DA - 1))
                        x.then_inc(A.num, 1)
                    after(pe, A.zsum, old.n)
                    for b in range(SPT):
                        for m in range(MA):
                            x = pe.matmul(bank[4][:, 0:SEQ], cst(f"sum_{2 * b + m}"), S[:, m, 4, b * SEQ:(b + 1) * SEQ],
                                          start=(b + m == 0), stop=(b + m == 2))
                    x.then_inc(A.den, 1)
                if t.real():
                    project(t, PROJ[7:10], last_use)
                if old.real():
                    pe.wait_ge(A.wgt, old.n + 1)
                    for m in range(MA):
                        after(pe, A.rs, 2 * old.n + m)
                        for b in range(SPT):
                            x = pe.matmul(bank[7][:, b * SEQ:(b + 1) * SEQ], cst(f"rep_{2 * b + m}"), WGT[:, :],
                                          start=True, stop=True)
                        x.then_inc(A.rep, 1)
                if t.real():
                    project(t, PROJ[10:], last_use)
                if old.real():
                    pe.wait_ge(A.y, old.n + 1)
                    for k in range(SUB):
                        cols = slice(k * P, (k + 1) * P)
                        pe.matmul(bank[4][:, cols], Y[:, old.p, cols], WOUT[:, :], start=True, stop=False)
                        x = pe.matmul(bank[4][:, cols], ONES[0:1, :], BROW[:, 0:C], start=False, stop=True)
                    x.then_inc(A.z, 1)
                if nxt.real():
                    after(pe, n_a.lo, nxt.n)
                    norm_turn(pe, n_a, nxt, bank[0])

            pe.wait_ge(pr.lal, 1)
            pe.wait_ge(pr.wout, 2)
            pe.wait_ge(pr.ones, 2)
            pe.wait_ge(ld.bias, 16 * BIAS_LOADS)
            run_steps(pe, step)
            ffn_pe(pe, 0)

            SQ, SL, SK, SKL, SKONE, SID = 0, NJ, 2 * NJ, 2 * NJ + 1, 2 * NJ + 2, 2 * NJ + 3

            def rows(t, b, k):
                n = t.n * SPT + b
                g, half = (k, None) if k < NG else ((k - NG) // 2, (k - NG) % 2)
                q = QST[g * RG:(g + 1) * RG, t.p, :, b * SEQ:(b + 1) * SEQ]
                ks = KST[g * RG:(g + 1) * RG, t.p, b * SEQ:(b + 1) * SEQ]
                bk = bank[k % 2]
                after(pe, B.row_used, 12 * n + k - 1)
                if k < NG:
                    for j in range(NJ):
                        pe.matmul(bk[:, j * P:(j + 1) * P], q[:, j, 0:P], ks[:, 0:P], start=(j == 0), stop=False,
                                  skip_group_check=True)
                    m = pe.matmul(r3(bk, NJ), MASKB[:, 2, :], spread(MASKB[:, 0, :], NJ), start=False, stop=True,
                                  skip_group_check=True)
                else:
                    for j in range(2):
                        pe.matmul(bk[:, j * SEQ:(j + 1) * SEQ], q[:, 2 * half + j, P:SEQ], ks, start=(j == 0),
                                  stop=False, skip_group_check=True)
                    m = pe.matmul(r3(bk, 2)[:, :, P:SEQ], MASKB[:, 2, :], spread(MASKB[:, 0, :], 2), start=False,
                                  stop=True, skip_group_check=True)
                m.then_inc(B.row_ready, 1)

            def cols(o, p, ob, k):
                after(pe, B.t_used, 6 * o + k - 1)
                for x in range(2):
                    g = 2 * (k // 2) + x if k < 4 else 2 * (k - 4) + x
                    rg = slice(g * RG, (g + 1) * RG)
                    bk = pair[k % 2][:, x, :]
                    if k < 4:
                        ks = KST[rg, p, ob * SEQ:ob * SEQ + P]
                        pe.matmul(bk, ks, Q2[rg, ob, 2 * (k % 2):2 * (k % 2) + 2, :], start=True, stop=False,
                                  skip_group_check=True)
                    else:
                        ks = KST[rg, p, ob * SEQ + P:(ob + 1) * SEQ]
                        pe.matmul(bk, ks, Q2[rg, ob, :, P:SEQ], start=True, stop=False, skip_group_check=True)
                for x in range(2):
                    bk = pair[k % 2][:, x, :]
                    if k < 4:
                        m = pe.matmul(r3(bk, 2)[:, :, 0:P], MASKB[:, 2, :], spread(MASKB[:, 1, :], 2), start=False,
                                      stop=True, skip_group_check=True)
                    else:
                        m = pe.matmul(r3(bk, NJ), MASKB[:, 2, :], spread(MASKB[:, 1, :], NJ), start=False, stop=True,
                                      skip_group_check=True)
                m.then_inc(B.t_ready, 1)

            def turn_out(n, b):
                pe.wait_ge(B.o, n + 1)
                for a in range(2):
                    m = pe.transpose(bank[7][:, a * P:(a + 1) * P], OB[:, b, a, :], ident)
                m.then_inc(B.ot, 1)

            def project_out(n, b):
                pe.wait_ge(B.otc, n + 1)
                for a in range(2):
                    dst = bank[7][:, a * P:(a + 1) * P]
                    pe.matmul(dst, OT[:, b, a * P:(a + 1) * P], WOB[:, :], start=True, stop=False)
                    m = pe.matmul(dst, ONES[0:1, :], BROW[:, C:2 * C], start=False, stop=True)
                m.then_inc(B.out, 1)

            def stack2(o, p, ob):
                pe.wait_ge(B.nml, 2 * (o + 1))
                for h in range(2):
                    pe.wait_ge(B.q2_used, 2 * o + h) if not (isinstance(o, int) and 2 * o + h <= 0) else None
                    seq = slice(ob * SEQ, (ob + 1) * SEQ)
                    for x in range(2):
                        j = 2 * h + x
                        dst = bank[6][:, x * SEQ:(x + 1) * SEQ]
                        pe.matmul(dst, SELR[:, SID, :], QST[:, p, j, seq], start=True, stop=False)
                        for a in range(2):
                            m = pe.matmul(dst[:, a * P:(a + 1) * P], NMP[:, ob, a, j, :], SELR[:, SID, :],
                                          start=False, stop=(a == 1))
                    m.then_inc(B.q2_ready, 1)

            def step_b(t):
                nxt = t + 1
                fixed = isinstance(t.n, int)
                for b in range(SPT):
                    n = t.n * SPT + b
                    here = t.real()
                    has1 = not fixed or 0 <= n - 1 < NSEQ
                    has2 = not fixed or 0 <= n - 2 < NSEQ
                    ob, op = 1 - b, (t.p if b == 1 else 1 - t.p)
                    if has1:
                        if b == 1 and nxt.real():
                            pe.wait_ge(n_b.lo, n_b.base + nxt.n + 1)
                        if b == 0 and here:
                            pe.wait_ge(B.kst_used, t.n + 1)
                        stack2(n - 1, op, ob)
                    if has2:
                        turn_out(n - 2, b)
                    for k in range(12):
                        if here:
                            if k == 0 and b == 0:
                                pe.wait_ge(B.st_used, NJ * (t.n + 1))
                                pe.wait_ge(B.kst_used, t.n + 1)
                            rows(t, b, k)
                        if has1 and k % 2 == 1:
                            if k == 1:
                                pe.wait_ge(B.q2_used, 2 * n)
                            cols(n - 1, op, ob, k // 2)
                        if k == 5 and has2:
                            project_out(n - 2, b)
                    if b == 0 and nxt.real():
                        norm_turn(pe, n_b, nxt, bank[6])
                    if b == 1 and nxt.real():
                        pe.wait_ge(n_b.lo, n_b.base + nxt.n + 1)
                        for k, name in enumerate(BPROJ):
                            if k:
                                pe.wait_ge(b_used[BPROJ[k - 1]], nxt.n + 1)
                            split_product(pe, bank[6], WBH[:, k, :], WBL[:, k, :], XH[:, nxt.p, :],
                                          XL[:, nxt.p, :]).then_inc(b_ready[name], 1)
                        pe.wait_ge(b_used[BPROJ[-1]], nxt.n + 1)
                        for k in range(SUB):
                            dst = bank[6][:, k * DB:(k + 1) * DB]
                            c = slice(k * P, (k + 1) * P)
                            pe.matmul(dst, XH[:, nxt.p, c], WVH[:, :], start=True, stop=False)
                            pe.matmul(dst, XL[:, nxt.p, c], WVH[:, :], start=False, stop=False)
                            pe.matmul(dst, XH[:, nxt.p, c], WVL[:, :], start=False, stop=False)
                            m = pe.matmul(dst, ONES[0:1, :], BROW[:, 2 * C:], start=False, stop=True)
                        m.then_inc(B.v_ready, 1)
                        pe.wait_ge(B.v_used, nxt.n + 1)
                        for j in range(NJ):
                            if j == 0:
                                pe.wait_ge(B.hi, 2 * (nxt.n + 1))
                                pe.wait_ge(B.lo, 2 * (nxt.n + 1))
                            else:
                                pe.wait_ge(B.st_used, NJ * nxt.n + j)
                            pe.matmul(bank[6], SELR[:, SQ + j, :], QKH[:, 0, :], start=True, stop=False)
                            pe.matmul(bank[6], SELR[:, SL + j, :], QKL[:, 0, :], start=False,
                                      stop=True).then_inc(B.st_ready, 1)
                        pe.wait_ge(B.st_used, NJ * (nxt.n + 1))
                        pe.matmul(bank[6], SELR[:, SK, :], QKH[:, 1, :], start=True, stop=False)
                        pe.matmul(bank[6], SELR[:, SKL, :], QKL[:, 1, :], start=False, stop=False)
                        pe.matmul(bank[6], SELR[0:1, SKONE, :], ONESR[:, :], start=False,
                                  stop=True).then_inc(B.kst_ready, 1)
                    if has1:
                        pe.wait_ge(B.t_used, 6 * n)
                        values_wait = t.n + 1 if b == 1 else t.n
                        after(pe, B.v_used, values_wait)
                        do_values(n - 1, op, ob)

            def do_values(o, p, ob):
                after(pe, B.done, o)
                acc = bank[7][:, 0:2 * HB * (DB + 1)].rearrange("p (a h c) -> p a h c", a=2, h=HB)
                lo = PT[:, ob, 0:HB * SEQ].rearrange("p (y z x j t) -> p y z x j t", y=2, z=2, x=2, j=2)
                hi = PT[:, ob, HB * SEQ:].rearrange("p (h t) -> p h t", h=HB)
                for h in range(HB):
                    g, j = h // NJ, h % NJ
                    at_lo = lo[:, g // 2, j // 2, g % 2, j % 2, :]
                    pe.matmul(acc[:, 0, h, :], at_lo[:, 0:P], VA[:, p, 2 * ob, :], start=True, stop=True)
                    pe.matmul(acc[:, 1, h, :], at_lo[:, P:SEQ], VA[:, p, 2 * ob, :], start=True, stop=False)
                    m = pe.matmul(acc[:, 1, h, :], hi[:, h, :], VA[:, p, 2 * ob + 1, :], start=False, stop=True)
                m.then_inc(B.pv, 1)

            pe.wait_ge(f[0].done, NT)
            pe.wait_ge(pr.selr, 2 * NJ + 4 + 3 + SUB)
            pe.wait_ge(pr.wbl, 2)
            pe.wait_ge(pr.nmp, 2)
            pe.wait_ge(pr.vone, 1)
            run_steps(pe, step_b)
            ffn_pe(pe, 1)

        def ffn_dve(v, i):
            s = f[i]
            v.wait_ge(*ffn_starts[i])

            def norm(t):
                norm_stats(v, s, t)
                norm_apply(v, s, t)
                norm_lo(v, s, t, bank[6 + t.p], XTH[:, t.n, :], XTL[:, t.n, :])
            pairs(v, norm)
            v.sem_inc(s.mul, 2)
            v.sem_inc(s.acc, 2)
            v.wait_ge(s.zero, 1)

            def mul(m, k):
                v.wait_ge(s.up, m * FC + k + 1)
                v.wait_ge(s.sil, m * FC + k + 3)
                v.wait_ge(s.d, m * FC + k + 1)
                v.tensor_tensor(HF[:, k, :], SG[:, k % 2, :], bank[2 + k % 2], ALU.mult).then_inc(s.mul, 1)

            def lo(m, k):
                v.wait_ge(s.hh, m * FC + k + 1)
                v.tensor_tensor(HL[:, k, :], HF[:, k, :], HH[:, k, :].bitcast(F32), ALU.subtract).then_inc(s.hl, 1)

            def add(m, t, p):
                v.wait_ge(s.d, (m + 2) * FC)
                v.tensor_tensor(YACC[:, t, :], YACC[:, t, :], bank[4 + p], ALU.add).then_inc(s.acc, 1)

            def tile(m, p, before):
                mul(m, 0)
                mul(m, 1)
                lo(m, 0)
                if before is not None:
                    add(m - 1, before, 1 - p)
                mul(m, 2)
                lo(m, 1)
                mul(m, 3)
                lo(m, 2)
                lo(m, 3)

            with v.Fori(0, NE // 2) as e:
                for u in range(2):
                    first = (2 * e + u) * NT
                    tile(first, 0, None if u == 0 else NT - 1)
                    tile(first + 1, 1, 0)
                    with v.Fori(1, NT // 2) as h:
                        tile(first + 2 * h, 0, 2 * h - 1)
                        tile(first + 2 * h + 1, 1, 2 * h)
                add((2 * e + 2) * NT - 1, NT - 1, 1)

            def residual(t):
                after(v, s.back, t.n + 1)
                v.tensor_tensor(X[:, t.n, :, :], X[:, t.n, :, :], by_sub(bank[6 + t.p]), ALU.add).then_inc(s.done, 1)
            pairs(v, residual)

        @block.vector
        def _(v):
            v.wait_ge(ld.bias, 16 * BIAS_LOADS)
            v.wait_ge(ld.consts, 16)
            v.tensor_tensor(BMIXD[:, 0:1], BMIX[:, 0:1], BMIX[:, 1:2], ALU.subtract).then_inc(pr.bmix, 1)
            v.wait_ge(pr.bmix, 2)
            v.tensor_scalar(BMIXD[:, 1:2], BMIXD[:, 0:1], cst("sign"), 0.5, ALU.mult, ALU.mult).then_inc(pr.bmix, 1)

            def rope_part(t, k, name, table, dst):
                v.wait_ge(a_ready[name], t.n + 1)
                after(v, (A.u_k, A.u_q)[k], t.n)
                v.tensor_tensor(seqs(dst), seqs(bank[PBANK[name]]), spread(cst(table), SPT),
                                ALU.mult).then_inc(a_used[name], 1)

            def phi(t, k):
                v.wait_ge((A.re_k, A.re_q)[k], t.n + 1)
                if k == 0:
                    after(v, A.scan, 10 * t.n)
                else:
                    after(v, A.prod0, t.n - 1)
                    after(v, A.prod1, t.n - 1)
                v.scalar_tensor_tensor(KV[:, 4, :] if k == 0 else PQ[:, t.p, :], EX[:, k, :], 1.0, U[:, k, :],
                                       ALU.min, ALU.add).then_inc((A.phi_k, A.phi_q)[k], 1)

            def step(t):
                nxt, old = t + 1, t + -1
                if nxt.real():
                    if isinstance(nxt.n, int) and nxt.n < 2:
                        v.wait_ge((ld.x0, ld.x1)[nxt.n], 16)
                    else:
                        v.wait_ge(ld.x, 16 * (NT - 2))
                    norm_stats(v, n_a, nxt)
                if t.real():
                    rope_part(t, 0, "k", "cos_a", R1[:, 0, :])
                    rope_part(t, 0, "ks", "sin_a", R2[:, 0, :])
                    rope_part(t, 1, "q", "cos_a", R1[:, 1, :])
                    rope_part(t, 1, "qs", "sin_a", R2[:, 1, :])
                if old.real():
                    v.wait_ge(A.den, old.n + 1)
                    v.tensor_scalar(DP[:, :], bank[4][:, 0:SEQ], DEN_EPS, None, ALU.add).then_inc(A.dp, 1)
                    v.wait_ge(A.dp, old.n + 1)
                    v.reciprocal(RC[:, :], DP[:, :]).then_inc(A.rc, 1)
                    v.wait_ge(A.rc, old.n + 1)
                    v.wait_ge(a_used["mx"], old.n + 1)
                    v.scalar_tensor_tensor(WGT[:, :], MIX[:, old.p, :], 1.0, RC[:, :], ALU.add,
                                           ALU.mult).then_inc(A.wgt, 1)
                if t.real():
                    phi(t, 0)
                    phi(t, 1)
                if old.real():
                    for m in range(MA):
                        v.wait_ge(A.rs, 2 * old.n + m + 1)
                        after(v, A.y, old.n)
                        v.tensor_tensor(AY[:, m, :], RS[:, m, :], bank[5 + m], ALU.mult).then_inc(A.ay, 1)
                if t.real():
                    v.wait_ge(A.phi_k, t.n + 1)
                    for c in range(DA):
                        v.wait_ge(a_ready[f"v{c}"], t.n + 1)
                        v.tensor_tensor(KV[:, c, :], KV[:, 4, :], bank[PBANK[f"v{c}"]],
                                        ALU.mult).then_inc(a_used[f"v{c}"], 1)
                if old.real():
                    v.wait_ge(A.z, old.n + 1)
                    after(v, A.zn, SUB * old.n)
                    v.tensor_tensor(Z[:, :, :], XN[:, old.p, :, :], by_sub(bank[4]), ALU.add).then_inc(A.zsum, 1)
                    v.wait_ge(A.zsum, old.n + 1)
                    after(v, A.mv2, SUB * old.n)
                    for k in range(SUB):
                        v.bn_stats(ST2[:, k, :], Z[:, k, :]).then_inc(A.st2, 1)
                    v.wait_ge(A.st2, SUB * (old.n + 1))
                    carry(v)
                    for k in range(SUB):
                        v.bn_aggr(MV2[:, k, :], ST2[:, k, :]).then_inc(A.mv2, 1)
                if nxt.real():
                    after(v, A.zsum, nxt.n - 1)
                    norm_apply(v, n_a, nxt)
                if t.real():
                    v.wait_ge(A.beta, t.n + 1)
                    v.wait_ge(a_used["v3"], t.n + 1)
                    after(v, A.den, t.n)
                    for m in range(MA):
                        for c in range(5):
                            v.tensor_tensor_scan(S[:, m, c, :], BETA[:, m, :], KV[:, c, :], 0.0, ALU.mult,
                                                 ALU.add).then_inc(A.scan, 1)
                if old.real():
                    v.wait_ge(A.rstd2, old.n + 1)
                    after(v, A.done, old.n)
                    for k in range(SUB):
                        v.tensor_scalar(ZN[:, k, :], Z[:, k, :], MV2[:, k, 0:1], RSTD2[:, k:k + 1], ALU.subtract,
                                        ALU.mult).then_inc(A.zn, 1)
                if t.real():
                    v.wait_ge(A.scan, 10 * t.n + 5)
                    v.wait_ge(A.phi_q, t.n + 1)
                    v.tensor_tensor(S[:, 0, :, :], S[:, 0, :, :], spread(PQ[:, t.p, :], 5),
                                    ALU.mult).then_inc(A.prod0, 1)
                if nxt.real():
                    after(v, a_ready["v3"], nxt.n - 1)
                    norm_lo(v, n_a, nxt, bank[0], XH[:, nxt.p, :], XL[:, nxt.p, :])

            v.wait_ge(pr.ones, 2)
            run_steps(v, step)
            ffn_dve(v, 0)

            def maxima(t, b):
                n = t.n * SPT + b
                after(v, B.nml, 2 * (n - 1))
                for k in range(12):
                    v.wait_ge(B.row_ready, 12 * n + k + 1)
                    if k < NG:
                        dst, src = NM[:, b, 0, NJ * k:NJ * (k + 1)], r3(bank[k % 2], NJ)
                    else:
                        h = 2 * (k - NG)
                        dst, src = NM[:, b, 1, h:h + 2], r3(bank[k % 2], 2)
                    v.tensor_reduce(dst, src, AX.X, ALU.max, negate=True).then_inc(B.row_used, 1)
                v.wait_ge(B.row_used, 12 * (n + 1))
                after(v, B.q2_ready, 2 * (n - 1))
                dst = lambda a, r: NMP[:, b, a, :, :].rearrange("p j (g r) -> p g j r", g=NG)[:, :, :, r]
                src = lambda a: NM[:, b, a, :].rearrange("p (g j) -> p g j", g=NG)
                for a in range(2):
                    v.tensor_copy(dst(a, 3 * DB), src(a)).then_inc(B.nmh, 1)
                v.wait_ge(B.nmh, 2 * (n + 1))
                for a in range(2):
                    v.tensor_tensor(dst(a, 3 * DB + 1), src(a), dst(a, 3 * DB).bitcast(F32),
                                    ALU.subtract).then_inc(B.nml, 1)

            def normalise(o, ob):
                v.wait_ge(B.pv, o + 1)
                after(v, B.o, o)
                acc = bank[7][:, 0:2 * HB * (DB + 1)].rearrange("p (a h c) -> p (a h) c", a=2, h=HB)
                ro = RO[:, :, :].rearrange("p a h -> p (a h)")
                v.reciprocal(ro, acc[:, :, DB]).then_inc(B.ro, 1)
                v.wait_ge(B.ro, o + 1)
                after(v, B.ot, o - 1)
                v.tensor_tensor(OB[:, ob, :, :].rearrange("p a (h c) -> p (a h) c", h=HB), acc[:, :, 0:DB],
                                spread_in(ro, DB), ALU.mult).then_inc(B.o, 1)

            def residual_b(n, t_n, b):
                v.wait_ge(B.out, n + 1)
                xs = X[:, t_n, 2 * b:2 * b + 2, :]
                v.tensor_tensor(xs, xs, bank[7][:, 0:2 * C].rearrange("p (a c) -> p a c", a=2),
                                ALU.add).then_inc(B.done, 1)

            def rope_b(t, k, name, table, dst, bias):
                v.wait_ge(b_ready[name], t.n + 1)
                after(v, (B.u_q, B.u_k)[k], t.n)
                v.scalar_tensor_tensor(seqs(dst), seqs(bank[6]), bias, spread(cst(table), SPT), ALU.add,
                                       ALU.mult).then_inc(b_used[name], 1)

            def step_b(t):
                nxt = t + 1
                fixed = isinstance(t.n, int)
                for b in range(SPT):
                    n = t.n * SPT + b
                    has1 = not fixed or 0 <= n - 1 < NSEQ
                    has2 = not fixed or 0 <= n - 2 < NSEQ
                    if b == 0 and nxt.real():
                        norm_stats(v, n_b, nxt)
                        norm_apply(v, n_b, nxt)
                    if t.real():
                        maxima(t, b)
                    if has2:
                        residual_b(n - 2, t.n - 1, b)
                    if b == 0 and nxt.real():
                        after(v, B.v_ready, nxt.n - 1)
                        norm_lo(v, n_b, nxt, bank[6], XH[:, nxt.p, :], XL[:, nxt.p, :])
                    if b == 1 and nxt.real():
                        rope_b(nxt, 0, "q", "cos_b", B1[:, 0, :], BQK[:, 0:1])
                        rope_b(nxt, 0, "qs", "sin_b", B2[:, 0, :], BQK[:, 1:2])
                        rope_b(nxt, 1, "k", "cos_b", B1[:, 1, :], BQK[:, 2:3])
                        rope_b(nxt, 1, "ks", "sin_b", B2[:, 1, :], BQK[:, 3:4])
                        v.wait_ge(B.v_ready, nxt.n + 1)
                        after(v, B.pv, SPT * (nxt.n - 1))
                        v.tensor_copy(VA[:, nxt.p, :, 0:DB],
                                      bank[6][:, 0:SUB * DB].rearrange("p (s c) -> p s c", s=SUB)).then_inc(B.v_used, 1)
                        for k in range(2):
                            v.wait_ge(B.hi, 2 * nxt.n + k + 1)
                            after(v, B.kst_ready, nxt.n)
                            v.tensor_tensor(QKL[:, k, :], QK[:, k, :], QKH[:, k, :].bitcast(F32),
                                            ALU.subtract).then_inc(B.lo, 1)
                    if has1:
                        normalise(n - 1, 1 - b)

            v.wait_ge(f[0].done, NT)
            v.wait_ge(pr.nmp, 2)
            v.wait_ge(pr.vone, 1)
            run_steps(v, step_b)
            ffn_dve(v, 1)


_INS = ["L0_attn_a_" + n for n in "x Wq Wk Wv Wbeta bbeta Wmix bmix Wout bout ln_g ln_b".split()] + \
       ["L0_attn_b_" + n for n in "Wq bq Wk bk Wv bv Wo bo".split()] + ["L0_ffn_" + n for n in "Wg Wu Wd".split()]


def kernel(**inputs):
    import numpy as _np
    import concourse.bacc as _bacc
    from concourse import mybir as _mybir
    from concourse.bass_utils import run_bass_kernel_spmd as _run

    nc = _bacc.Bacc("TRN2", target_bir_lowering=False, num_devices=1)
    arrays, args = {}, []
    for name in _INS:
        a = _np.ascontiguousarray(inputs[name])
        arrays[f"in_{name}_dram"] = a
        args.append(nc.dram_tensor(f"in_{name}_dram", a.shape, _mybir.dt.from_np(a.dtype), kind="ExternalInput").ap())
    tables = _np.concatenate(list(_C.values()), axis=1)
    arrays["in_tables_dram"] = tables
    args.append(nc.dram_tensor("in_tables_dram", tables.shape, _mybir.dt.float32, kind="ExternalInput").ap())
    shape = inputs["L0_attn_a_x"].shape
    args.append(nc.dram_tensor("out_0_dram", shape, _mybir.dt.float32, kind="ExternalOutput").ap())
    program(nc, *args)
    r = _run(nc, [arrays], core_ids=[0])
    return r.results[0]["out_0_dram"]
```

```python
from collections import namedtuple
from contextlib import ExitStack

import numpy as np
import concourse.bass as bass
from concourse import mybir

F32 = mybir.dt.float32
F32R = mybir.dt.float32r
BF16 = mybir.dt.bfloat16
ALU = mybir.AluOpType
ACT = mybir.ActivationFunctionType
AX = mybir.AxisListType

P = 128
NSEQ, SEQ, C = 16, 256, 128
TOK = 512
SUB = TOK // P
NT = NSEQ * SEQ // TOK
SPT = TOK // SEQ
HA, DA, MA = 32, 4, 2
HB, DB = 16, 8
NE, FFN = 8, 512
FC = FFN // P
LN_EPS = 1e-5
DEN_EPS = 1e-6
BMIN, BMAX = 0.85, 0.9995
NG, NJ = 4, 4
RG = 32
MASKED = -1e30
UNITS = 12
RING = 4
T_LAG, PV_LAG = 2, 4
OUT_STEP = 5


def constants():
    c = {}
    eye = np.eye(P, dtype=np.float32)
    c["ident"] = eye
    pos = np.arange(SEQ, dtype=np.float32)
    inv = (1.0 / 10000.0 ** (np.arange(DA // 2, dtype=np.float32) / (DA // 2))).astype(np.float32)
    d = np.arange(P) // HA
    ang = pos[None, :] * inv[d % (DA // 2)][:, None]
    c["cos_a"] = np.cos(ang)
    c["sin_a"] = np.sin(ang) * np.where(d < DA // 2, -1.0, 1.0)[:, None]
    inv = (1.0 / 10000.0 ** (np.arange(0, DB, 2, dtype=np.float32) / DB)).astype(np.float32)
    d = np.arange(P) % DB
    ang = pos[None, :] * inv[d % (DB // 2)][:, None]
    c["cos_b"] = np.cos(ang) * np.where(d < DB // 2, 1.0, -1.0)[:, None]
    c["sin_b"] = np.sin(ang)
    h = np.arange(P) % HA
    q = np.arange(P) // HA
    same = (h[:, None] == h[None, :]).astype(np.float32)
    for s in range(4):
        c[f"sum_{s}"] = same * (q[None, :] == s)
    for s in range(4):
        c[f"rep_{s}"] = same * (q[:, None] == s)
    for j in range(NJ):
        hi = np.zeros((P, P), np.float32)
        lo = np.zeros((P, P), np.float32)
        for g in range(NG):
            for x in range(DB):
                src = (NJ * g + j) * DB + x
                hi[src, RG * g + x] = hi[src, RG * g + DB + x] = lo[src, RG * g + 2 * DB + x] = 1
        c[f"qhi_{j}"], c[f"qlo_{j}"] = hi, lo
    hi = np.zeros((P, P), np.float32)
    lo = np.zeros((P, P), np.float32)
    for g in range(NG):
        for x in range(DB):
            hi[x, RG * g + x] = hi[x, RG * g + 2 * DB + x] = lo[x, RG * g + DB + x] = 1
    c["khi"], c["klo"] = hi, lo
    ones = np.zeros((P, P), np.float32)
    for g in range(NG):
        ones[0, RG * g + 3 * DB:RG * g + 3 * DB + 2] = 1
    c["kone"] = ones
    r = np.arange(P)
    c["mask_rows"] = np.where(r[None, :] > r[:, None], MASKED, 0.0)
    c["mask_cols"] = np.where(r[:, None] > r[None, :], MASKED, 0.0)
    fold = np.zeros((P, NG * (DB + 1)), np.float32)
    for g in range(NG):
        for x in range(DB + 1):
            fold[RG * g + x, (DB + 1) * g + x] = 1
        for x in range(DB):
            fold[RG * g + DB + 1 + x, (DB + 1) * g + x] = 1
    c["fold"] = fold
    c["sign"] = np.where((np.arange(P) // HA) % MA == 0, 1.0, -1.0)[:, None]
    return {k: np.asarray(v, np.float32) for k, v in c.items()}


_C = constants()
CPOS, _at = {}, 0
for _k, _v in _C.items():
    CPOS[_k] = (_at, _v.shape[1])
    _at += _v.shape[1]
CWIDTH = _at


class Tile:

    def __init__(self, n, p):
        self.n, self.p = n, p

    def __add__(self, k):
        return Tile(self.n + k, (self.p + k) % 2)

    def real(self):
        return not isinstance(self.n, int) or 0 <= self.n < NT


def after(eng, sem, n):
    if not (isinstance(n, int) and n <= 0):
        eng.wait_ge(sem, n)


def run_steps(eng, step):
    for n in (-1, 0, 1):
        step(Tile(n, n % 2))
    with eng.Fori(1, NT // 2 - 1) as i:
        step(Tile(2 * i, 0))
        step(Tile(2 * i + 1, 1))
    for n in (NT - 2, NT - 1, NT):
        step(Tile(n, n % 2))


def program(nc, a_x, a_Wq, a_Wk, a_Wv, a_Wbeta, a_bbeta, a_Wmix, a_bmix, a_Wout, a_bout, a_ln_g, a_ln_b,
            b_Wq, b_bq, b_Wk, b_bk, b_Wv, b_bv, b_Wo, b_bo, f_Wg, f_Wu, f_Wd, consts, out):
    ctx = ExitStack()
    with ctx:
        def sb(name, shape, dt=F32):
            return ctx.enter_context(nc.sbuf_tensor(name, shape, dt))

        def sem(name):
            return ctx.enter_context(nc.semaphore(name))

        def sems(prefix, names):
            return namedtuple(prefix, names)(*[sem(f"{prefix}_{n}") for n in names.split()])

        def spread(ap, n):
            return bass.AP(ap.tensor, ap.offset, [ap.ap[0], [0, n], ap.ap[1]])

        def spread_in(ap, n):
            return bass.AP(ap.tensor, ap.offset, [*ap.ap, [0, n]])

        def r3(ap, n):
            return ap.rearrange("p (a b) -> p a b", a=n)

        single = {i: ctx.enter_context(nc.psum_tensor(f"bank{i}", [P, 512], F32)) for i in (0, 1, 6, 7)}
        pair = [ctx.enter_context(nc.psum_tensor(f"pair{i}", [P, 2, 512], F32)) for i in range(2)]
        bank = [single[i][:, :] if i in single else pair[i // 2 - 1][:, i % 2, :] for i in range(8)]

        X = sb("X", [P, NT, SUB, C])
        CST = sb("CST", [P, CWIDTH])

        def cst(name):
            at, w = CPOS[name]
            return CST[:, at:at + w]

        ident = cst("ident")
        SELR = sb("SELR", [P, 2 * NJ + 4, P], F32R)
        MASKB = sb("MASKB", [P, 3, P], BF16)
        ONES = sb("ONES", [P, P])
        ONESR = sb("ONESR", [1, TOK], F32R)
        HALF = sb("HALF", [P, SUB])
        WOUT = sb("WOUT", [P, C])
        WBH = sb("WBH", [P, 4, P], F32R)
        WBL = sb("WBL", [P, 4, P], F32R)
        WVH = sb("WVH", [P, DB], F32R)
        WVL = sb("WVL", [P, DB], F32R)
        WOB = sb("WOB", [P, C])
        BROW = sb("BROW", [1, 2 * C + DB])
        GB = sb("GB", [P, 2, C])
        BQK = sb("BQK", [P, 4])
        BBETA = sb("BBETA", [P, MA])
        BMIX = sb("BMIX", [P, MA])
        BMIXD = sb("BMIXD", [P, 2])
        XN = sb("XN", [P, 2, SUB, C])
        ST = sb("ST", [P, 2, SUB, 6])
        MV = sb("MV", [P, 2, SUB, 2])
        VE = sb("VE", [P, 2, SUB])
        RSTD = sb("RSTD", [P, 2, SUB])
        ST2 = sb("ST2", [P, SUB, 6])
        MV2 = sb("MV2", [P, SUB, 2])
        VE2 = sb("VE2", [P, SUB])
        RSTD2 = sb("RSTD2", [P, SUB])

        ARENA = sb("ARENA", [P, 20224])
        ARENA_R = sb("ARENA_R", [P, 19200], F32R)
        at = {F32: 0, F32R: 0}

        def take(*shape, dt=F32):
            n = int(np.prod(shape))
            a = {F32: ARENA, F32R: ARENA_R}[dt]
            ap = a[:, at[dt]:at[dt] + n]
            at[dt] += n
            names = "abcd"[:len(shape)]
            return ap.rearrange(f"p ({' '.join(names)}) -> p {' '.join(names)}", **dict(zip(names, shape)))

        def rewind():
            at[F32] = at[F32R] = 0

        WRAW = take(6, P)
        WT = take(6, P)
        LA = take(12, P)
        WB = take(4, P)
        WQB, WKB, WVB = take(C), take(DB), take(DB)
        rewind()
        S = take(MA, 5, TOK)
        KV = take(5, TOK)
        R1 = take(2, TOK)
        R2 = take(2, TOK)
        U = take(2, TOK)
        EX = take(2, TOK)
        PQ = take(2, TOK)
        TB = take(MA, TOK)
        BETA = take(MA, TOK)
        MIX = take(2, SEQ)
        DP, RC, WGT = take(SEQ), take(SEQ), take(SEQ)
        RS = take(MA, TOK)
        AY = take(MA, TOK)
        Y = take(2, TOK)
        Z = take(SUB, C)
        ZN = take(SUB, C)
        XH = take(2, TOK, dt=F32R)
        XL = take(2, TOK, dt=F32R)
        LAH = take(12, P, dt=F32R)
        LAL = take(12, P, dt=F32R)
        rewind()
        B1 = take(2, TOK)
        B2 = take(2, TOK)
        QK = take(2, TOK)
        PT = take(RING, TOK)
        OS = take(2, 2, TOK)
        OB = take(2, 2, C)
        OT = take(2, 2 * C)
        NM = take(2, 2, HB)
        RO = take(2, HB)
        take(2, TOK, dt=F32R), take(2, TOK, dt=F32R)
        QKH = take(2, TOK, dt=F32R)
        QKL = take(2, TOK, dt=F32R)
        QST = take(2, NJ, TOK, dt=F32R)
        KST = take(2, TOK, dt=F32R)
        NMP = take(2, 2, NJ, P, dt=F32R)
        Q2 = take(2, NJ, SEQ, dt=F32R)
        PH = take(RING, TOK, dt=F32R)
        PL = take(RING, TOK, dt=F32R)
        VS = take(2, SUB, 2 * P - RG, dt=F32R)
        rewind()
        YACC = take(NT, TOK)
        WS = take(2, 3, FFN)
        SG = take(2, TOK)
        HF = take(FC, TOK)
        YS = take(2, TOK)
        XTH = take(NT, TOK, dt=F32R)
        XTL = take(NT, TOK, dt=F32R)
        WH = take(2, 3, FFN, dt=F32R)
        WL = take(2, 3, FFN, dt=F32R)
        HH = take(FC, TOK, dt=F32R)
        HL = take(FC, TOK, dt=F32R)

        ld = sems("ld", "x0 x1 x consts wa wb bias")
        pr = sems("prep", "wt wtc la lah lal ones selr wb wbh wbl wout bmix zero vone")
        PROJ = ["k", "ks", "q", "qs", "b0", "b1", "mx", "v0", "v1", "v2", "v3"]
        PBANK = {n: 1 + i % 3 for i, n in enumerate(PROJ)}
        a_ready = {n: sem(f"a_{n}_ready") for n in PROJ}
        a_used = {n: sem(f"a_{n}_used") for n in PROJ}
        A = sems("a", "u_k u_q ex_k ex_q re_k re_q phi_k phi_q clip scaled beta scan prod0 prod1 num den dp rc wgt rep "
                      "rs ay y z zsum st2 mv2 ve2 rstd2 zn zg zb done")
        NORM = "st mv ve rstd xn tp hi lo"
        norm_sems = sems("norm", NORM)

        def norm_of(phase, names="", *more):
            return namedtuple("phase", f"{NORM} base {names}")(*norm_sems, phase * NT, *more)

        n_a, n_b = norm_of(0), norm_of(2)
        BPROJ = ["q", "qs", "k", "ks"]
        b_ready = {n: sem(f"b_{n}_ready") for n in BPROJ}
        b_used = {n: sem(f"b_{n}_used") for n in BPROJ}
        B = sems("b", "u_q u_k hi lo v_ready v_used st_ready st_used kst_ready kst_used row_ready row_used nmh nml "
                      "q2_ready q2_used t_ready t_used pl vhi pv os fold ro o ot otc out done")
        FSEMS = "wload0 wload1 wh wl gate up sil mul hh hl d acc ys back done zero"
        f = [norm_of(2 * i + 1, FSEMS, *sems(f"f{i}", FSEMS)) for i in range(2)]
        stored = sem("stored")
        carried = sem("carried")

        def carry(eng):
            eng.sem_inc(carried, 1)

        x_tok = a_x.rearrange("b t c -> (b t) c").rearrange("(n s p) c -> p n s c", n=NT, p=P)
        o_tok = out.rearrange("b t c -> (b t) c").rearrange("(n s p) c -> p n s c", n=NT, p=P)

        block = ctx.enter_context(nc.Block())

        def seqs(ap):
            return ap.rearrange("p (a t) -> p a t", a=SPT)

        def by_sub(ap):
            return ap.rearrange("p (s c) -> p s c", s=SUB)

        def split_product(pe, dst, wh, wl, xh, xl, start=True, stop=True):
            pe.matmul(dst, wh, xh, start=start, stop=False)
            pe.matmul(dst, wh, xl, start=False, stop=False)
            return pe.matmul(dst, wl, xh, start=False, stop=stop)

        def pairs(eng, step, n=NT):
            step(Tile(0, 0))
            step(Tile(1, 1))
            with eng.Fori(1, n // 2) as i:
                step(Tile(2 * i, 0))
                step(Tile(2 * i + 1, 1))

        def norm_stats(v, s, t):
            n = s.base + t.n
            after(v, s.mv, SUB * (n - 1))
            for i in range(SUB):
                v.bn_stats(ST[:, t.p, i, :], X[:, t.n, i, :]).then_inc(s.st, 1)
            after(v, s.st, SUB * (n + 1))
            after(v, s.ve, n - 1)
            after(v, s.xn, SUB * (n - 1))
            carry(v)
            for i in range(SUB):
                v.bn_aggr(MV[:, t.p, i, :], ST[:, t.p, i, :]).then_inc(s.mv, 1)

        def norm_rstd(g, s, t):
            n = s.base + t.n
            after(g, s.mv, SUB * (n + 1))
            after(g, s.rstd, n - 1)
            carry(g)
            g.tensor_scalar(VE[:, t.p, :], MV[:, t.p, :, 1], LN_EPS, None, ALU.add).then_inc(s.ve, 1)
            after(g, s.ve, n + 1)
            after(g, s.xn, SUB * (n - 1))
            g.tensor_tensor(RSTD[:, t.p, :], VE[:, t.p, :], HALF[:, :], ALU.pow).then_inc(s.rstd, 1)

        def norm_apply(v, s, t):
            n = s.base + t.n
            after(v, s.rstd, n + 1)
            after(v, s.tp, n - 1)
            for i in range(SUB):
                v.tensor_scalar(XN[:, t.p, i, :], X[:, t.n, i, :], MV[:, t.p, i, 0:1], RSTD[:, t.p, i:i + 1],
                                ALU.subtract, ALU.mult).then_inc(s.xn, 1)

        def norm_turn(pe, s, t, dst):
            n = s.base + t.n
            after(pe, s.xn, SUB * (n + 1))
            for i in range(SUB):
                m = pe.transpose(dst[:, i * P:(i + 1) * P], XN[:, t.p, i, :], ident)
            m.then_inc(s.tp, 1)

        def norm_hi(act, s, t, src, hi):
            after(act, s.tp, s.base + t.n + 1)
            act.activation(hi, src, ACT.Copy).then_inc(s.hi, 1)

        def norm_lo(v, s, t, src, hi, lo):
            after(v, s.hi, s.base + t.n + 1)
            v.tensor_tensor(lo, src, hi.bitcast(F32), ALU.subtract).then_inc(s.lo, 1)

        def run_slots(eng, slot):
            def step_b(t):
                for b in range(SPT):
                    slot(t, b)
            run_steps(eng, step_b)

        def live(t, b, back):
            return not isinstance(t.n, int) or 0 <= t.n * SPT + b - back < NSEQ

        def unit_at(t, b, k, lag):
            n, u = t.n * SPT + b, k - lag
            if u >= 0:
                return (n - 1, t.p if b == 1 else 1 - t.p, 1 - b, u) if live(t, b, 1) else None
            return (n - 2, 1 - t.p, b, u + UNITS) if live(t, b, 2) else None

        VAT = P - RG


        BIAS_LOADS = 2 * DA + 5 + 1 + 3 * 2 * HB
        ffn_starts = ((A.done, NT), (B.done, NSEQ))

        @block.sync
        def _(sp):
            for n in range(NT):
                sp.dma_start(X[:, n, :, :], x_tok[:, n]).then_inc((ld.x0, ld.x1)[n] if n < 2 else ld.x, 16)
                if n == 0:
                    sp.dma_start(CST[:, :], consts).then_inc(ld.consts, 16)
                    for i, w in enumerate((a_Wq, a_Wk, a_Wv, a_Wbeta, a_Wmix, a_Wout)):
                        sp.dma_start(WRAW[0:w.shape[0], i, :], w).then_inc(ld.wa, 16)
            for d in range(DA):
                rows = slice(d * HA, (d + 1) * HA)
                sp.dma_start(BBETA[rows, :], a_bbeta.rearrange("(h m) -> h m", m=MA)).then_inc(ld.bias, 16)
                sp.dma_start(BMIX[rows, :], a_bmix.rearrange("(h m) -> h m", m=MA)).then_inc(ld.bias, 16)
            sp.dma_start(WQB[:, :], b_Wq).then_inc(ld.wb, 16)
            sp.dma_start(WKB[:, :], b_Wk).then_inc(ld.wb, 16)
            sp.dma_start(WVB[:, :], b_Wv).then_inc(ld.wb, 16)
            sp.dma_start(WOB[:, :], b_Wo).then_inc(ld.wb, 16)
            row = lambda v: v.rearrange("(a n) -> a n", a=1)
            sp.dma_start(BROW[:, 0:C], row(a_bout)).then_inc(ld.bias, 16)
            sp.dma_start(BROW[:, C:2 * C], row(b_bo)).then_inc(ld.bias, 16)
            sp.dma_start(BROW[:, 2 * C:], row(b_bv)).then_inc(ld.bias, 16)
            sp.dma_start(GB[:, 0, :], row(a_ln_g).broadcast_to([P, C])).then_inc(ld.bias, 16)
            sp.dma_start(GB[:, 1, :], row(a_ln_b).broadcast_to([P, C])).then_inc(ld.bias, 16)
            col = lambda v: v.rearrange("(n a) -> n a", a=1)
            half = DB // 2
            sp.dma_start(BQK[:, 0:1], col(b_bq)).then_inc(ld.bias, 16)
            for h in range(HB):
                for lo in (0, half):
                    dst = slice(h * DB + lo, h * DB + lo + half)
                    src = slice(h * DB + half - lo, h * DB + 2 * half - lo)
                    sp.dma_start(BQK[dst, 1:2], col(b_bq)[src]).then_inc(ld.bias, 16)
                    sp.dma_start(BQK[dst, 2:3], col(b_bk)[lo:lo + half]).then_inc(ld.bias, 16)
                    sp.dma_start(BQK[dst, 3:4], col(b_bk)[half - lo:2 * half - lo]).then_inc(ld.bias, 16)
            for i in range(2):
                s = f[i]
                wload = (s.wload0, s.wload1)
                sp.wait_ge(*ffn_starts[i])

                def load(x, u):
                    after(sp, s.wl, x - 1)
                    carry(sp)
                    sp.dma_start(WS[:, u, 0, :], f_Wg[x]).then_inc(wload[u], 16)
                    sp.dma_start(WS[:, u, 1, :], f_Wu[x]).then_inc(wload[u], 16)
                    sp.dma_start(WS[:, u, 2, :].rearrange("p (k c) -> p k c", k=FC),
                                 f_Wd[x].rearrange("(k p) c -> p k c", p=P)).then_inc(wload[u], 16)

                load(0, 0)
                load(1, 1)
                with sp.Fori(1, NE // 2) as h:
                    load(2 * h, 0)
                    load(2 * h + 1, 1)
            for n in range(NT):
                sp.wait_ge(f[1].done, n + 1)
                sp.dma_start(o_tok[:, n], X[:, n, :, :]).then_inc(stored, 16)
            sp.wait_ge(stored, 16 * NT)

        def ffn_pool(g, i):
            s = f[i]
            g.wait_ge(*ffn_starts[i])
            g.memset(YACC[:, :, :], 0.0).then_inc(s.zero, 1)
            pairs(g, lambda t: norm_rstd(g, s, t))

            def split(h, u):
                x = 2 * h + u
                g.wait_ge((s.wload0, s.wload1)[u], 48 * (h + 1))
                if not isinstance(x, int):
                    g.wait_ge(s.d, FC + FC * NT * (x - 1))
                carry(g)
                g.tensor_copy(WH[:, u, :, :], WS[:, u, :, :]).then_inc(s.wh, 1)
                g.wait_ge(s.wh, x + 1)
                g.tensor_tensor(WL[:, u, :, :], WS[:, u, :, :], WH[:, u, :, :].bitcast(F32),
                                ALU.subtract).then_inc(s.wl, 1)

            split(0, 0)
            split(0, 1)
            with g.Fori(1, NE // 2) as h:
                split(h, 0)
                split(h, 1)

        @block.gpsimd
        def _(g):
            g.memset(ONES[:, :], 1.0).then_inc(pr.ones, 1)
            g.memset(HALF[:, :], -0.5).then_inc(pr.ones, 1)
            g.wait_ge(ld.wa, 96)
            g.tensor_copy(LA[:, 0, :].rearrange("p (c h) -> p c h", c=DA),
                          WRAW[:, 5, :].rearrange("p (h c) -> p c h", c=DA)).then_inc(pr.wout, 1)
            g.wait_ge(pr.wtc, 6)
            g.memset(LA[:, 10:12, :], 0.0).then_inc(pr.la, 1)
            g.wait_ge(pr.la, 1)
            hd = lambda k: WT[:, k, :].rearrange("p (h d) -> p d h", d=DA)
            dh = lambda k: LA[:, k, :].rearrange("p (d h) -> p d h", d=DA)
            for k, w in ((0, 1), (2, 0)):
                g.tensor_copy(dh(k), hd(w)).then_inc(pr.la, 1)
                g.tensor_copy(dh(k + 1)[:, 0:2, :], hd(w)[:, 2:4, :]).then_inc(pr.la, 1)
                g.tensor_copy(dh(k + 1)[:, 2:4, :], hd(w)[:, 0:2, :]).then_inc(pr.la, 1)
            for c in range(DA):
                g.tensor_copy(dh(4 + c), spread(hd(2)[:, c, :], DA)).then_inc(pr.la, 1)
            for m in range(MA):
                hm = WT[:, 3, 0:HA * MA].rearrange("p (h m) -> p m h", m=MA)
                g.tensor_copy(dh(8 + m), spread(hm[:, m, :], DA)).then_inc(pr.la, 1)
            hm = WT[:, 4, 0:HA * MA].rearrange("p (h m) -> p m h", m=MA)
            for b in range(SPT):
                dst = LA[:, 10 + b, :].rearrange("p (b m h) -> p b m h", b=SPT, m=MA)
                for m in range(MA):
                    g.tensor_tensor(dst[:, b, m, :], hm[:, m, :], hm[:, 1 - m, :], ALU.subtract).then_inc(pr.la, 1)
            g.wait_ge(pr.la, 17)
            g.tensor_copy(LAH[:, :, :], LA[:, :, :]).then_inc(pr.lah, 1)
            g.wait_ge(pr.lah, 1)
            g.tensor_tensor(LAL[:, :, :], LA[:, :, :], LAH[:, :, :].bitcast(F32), ALU.subtract).then_inc(pr.lal, 1)
            g.tensor_scalar(WOUT[:, :], WT[:, 5, :], 0.5, None, ALU.mult).then_inc(pr.wout, 1)
            g.wait_ge(ld.wb, 64)
            hd = lambda k: WB[:, k, :].rearrange("p (h d) -> p h d", d=DB)
            wq = WQB[:, :].rearrange("p (h d) -> p h d", d=DB)
            half = DB // 2
            g.tensor_copy(WB[:, 0, :], WQB[:, :]).then_inc(pr.wb, 1)
            g.tensor_copy(hd(1)[:, :, 0:half], wq[:, :, half:DB]).then_inc(pr.wb, 1)
            g.tensor_copy(hd(1)[:, :, half:DB], wq[:, :, 0:half]).then_inc(pr.wb, 1)
            g.tensor_copy(hd(2), spread(WKB[:, :], HB)).then_inc(pr.wb, 1)
            g.tensor_copy(hd(3)[:, :, 0:half], spread(WKB[:, half:DB], HB)).then_inc(pr.wb, 1)
            g.tensor_copy(hd(3)[:, :, half:DB], spread(WKB[:, 0:half], HB)).then_inc(pr.wb, 1)
            g.wait_ge(pr.wb, 6)
            g.tensor_copy(WBH[:, :, :], WB[:, :, :]).then_inc(pr.wbh, 1)
            g.tensor_copy(WVH[:, :], WVB[:, :]).then_inc(pr.wbh, 1)
            g.wait_ge(pr.wbh, 2)
            g.tensor_tensor(WBL[:, :, :], WB[:, :, :], WBH[:, :, :].bitcast(F32), ALU.subtract).then_inc(pr.wbl, 1)
            g.tensor_tensor(WVL[:, :], WVB[:, :], WVH[:, :].bitcast(F32), ALU.subtract).then_inc(pr.wbl, 1)
            g.wait_ge(ld.consts, 16)
            at0 = CPOS["qhi_0"][0]
            for j in range(NJ):
                g.tensor_copy(SELR[:, j, :], cst(f"qhi_{j}")).then_inc(pr.selr, 1)
                g.tensor_copy(SELR[:, NJ + j, :], cst(f"qlo_{j}")).then_inc(pr.selr, 1)
            for k, name in enumerate(("khi", "klo", "kone", "ident")):
                g.tensor_copy(SELR[:, 2 * NJ + k, :], cst(name)).then_inc(pr.selr, 1)
            for k, name in enumerate(("mask_rows", "mask_cols", "ident")):
                g.tensor_copy(MASKB[:, k, :], cst(name)).then_inc(pr.selr, 1)
            g.tensor_copy(ONESR[:, 0:P], ONES[0:1, :]).then_inc(pr.selr, 1)
            for k in range(1, SUB):
                g.tensor_copy(ONESR[:, k * P:(k + 1) * P], ONES[0:1, :]).then_inc(pr.selr, 1)

            def step(t):
                nxt, old = t + 1, t + -1
                if nxt.real():
                    norm_rstd(g, n_a, nxt)
                if t.real():
                    for k, name in enumerate("kq"):
                        after(g, a_used[name], t.n + 1)
                        after(g, a_used[name + "s"], t.n + 1)
                        after(g, A.re_k if name == "k" else A.re_q, t.n)
                        after(g, A.phi_k if name == "k" else A.phi_q, t.n)
                        g.tensor_tensor(U[:, k, :], R1[:, k, :], R2[:, k, :],
                                        ALU.add).then_inc(A.u_k if name == "k" else A.u_q, 1)
                    after(g, a_used["b0"], t.n + 1)
                    after(g, a_used["b1"], t.n + 1)
                    carry(g)
                    g.tensor_scalar(TB[:, :, :], TB[:, :, :], 2 * BMAX - 1, 2 * BMIN - 1,
                                    ALU.min, ALU.max).then_inc(A.clip, 1)
                    after(g, A.clip, t.n + 1)
                    after(g, A.scan, 2 * 5 * t.n)
                    carry(g)
                    g.tensor_scalar(BETA[:, :, :], TB[:, :, :], 0.5, 0.5, ALU.mult, ALU.add).then_inc(A.scaled, 1)
                    after(g, A.scaled, t.n + 1)
                    carry(g)
                    g.memset(BETA[:, :, 0::SEQ], 0.0).then_inc(A.beta, 1)
                if old.real():
                    after(g, A.ay, 2 * (old.n + 1))
                    after(g, A.z, old.n - 1)
                    g.tensor_tensor(Y[:, old.p, :], AY[:, 0, :], AY[:, 1, :], ALU.add).then_inc(A.y, 1)
                    after(g, A.mv2, SUB * (old.n + 1))
                    after(g, A.rstd2, old.n)
                    carry(g)
                    g.tensor_scalar(VE2[:, :], MV2[:, :, 1], LN_EPS, None, ALU.add).then_inc(A.ve2, 1)
                    after(g, A.ve2, old.n + 1)
                    after(g, A.zn, SUB * old.n)
                    g.tensor_tensor(RSTD2[:, :], VE2[:, :], HALF[:, :], ALU.pow).then_inc(A.rstd2, 1)
                    after(g, A.zn, SUB * (old.n + 1))
                    g.tensor_tensor(ZN[:, :, :], ZN[:, :, :], spread(GB[:, 0, :], SUB), ALU.mult).then_inc(A.zg, 1)
                    after(g, A.zg, old.n + 1)
                    g.tensor_tensor(ZN[:, :, :], ZN[:, :, :], spread(GB[:, 1, :], SUB), ALU.add).then_inc(A.zb, 1)
                    after(g, A.zb, old.n + 1)
                    g.tensor_tensor(X[:, old.n, :, :], X[:, old.n, :, :], ZN[:, :, :], ALU.add).then_inc(A.done, 1)
                if t.real():
                    after(g, A.scan, 2 * 5 * (t.n + 1))
                    after(g, A.phi_q, t.n + 1)
                    g.tensor_tensor(S[:, 1, :, :], S[:, 1, :, :], spread(PQ[:, t.p, :], 5),
                                    ALU.mult).then_inc(A.prod1, 1)

            g.wait_ge(ld.bias, 16 * BIAS_LOADS)
            run_steps(g, step)
            ffn_pool(g, 0)

            g.wait_ge(f[0].done, NT)

            def slot(t, b):
                nxt = t + 1
                for k in range(UNITS):
                    unit = unit_at(t, b, k, T_LAG)
                    if unit:
                        o, _, _, u = unit
                        q = UNITS * o + u
                        after(g, B.t_used, 2 * (q + 1))
                        after(g, B.pv, q - RING + 1)
                        g.tensor_tensor(PL[:, u % RING, :], PT[:, u % RING, :], PH[:, u % RING, :].bitcast(F32),
                                        ALU.subtract).then_inc(B.pl, 1)
                    if nxt.real() and (b, k) == (0, 1):
                        norm_rstd(g, n_b, nxt)
                    if nxt.real() and (b, k) in ((0, 9), (1, 1)):
                        i, name = (0, "q") if b == 0 else (1, "k")
                        after(g, b_used[name], nxt.n + 1)
                        after(g, b_used[name + "s"], nxt.n + 1)
                        after(g, B.hi, 2 * nxt.n)
                        after(g, B.lo, 2 * nxt.n)
                        g.tensor_tensor(QK[:, i, :], B1[:, i, :], B2[:, i, :],
                                        ALU.add).then_inc(B.u_q if i == 0 else B.u_k, 1)
            run_slots(g, slot)
            ffn_pool(g, 1)

        def ffn_act(act, i):
            s = f[i]
            act.wait_ge(*ffn_starts[i])

            def norm(t):
                norm_hi(act, s, t, bank[6 + t.p], XTH[:, t.n, :])
            pairs(act, norm)
            act.sem_inc(s.sil, 2)

            def hi(m, k):
                act.wait_ge(s.mul, m * FC + k + 3)
                act.activation(HH[:, k, :], HF[:, k, :], ACT.Copy).then_inc(s.hh, 1)

            def tile(m):
                for k in range(FC):
                    act.wait_ge(s.gate, m * FC + k + 1)
                    act.wait_ge(s.mul, m * FC + k + 1)
                    act.activation(SG[:, k % 2, :], bank[k % 2], ACT.Silu).then_inc(s.sil, 1)
                    if k >= 1:
                        hi(m, k - 1)
                hi(m, FC - 1)

            with act.Fori(0, NE * NT // 2) as h:
                tile(2 * h)
                tile(2 * h + 1)

            def stage(t):
                after(act, s.acc, 2 + NT * NE)
                after(act, s.back, t.n - 1)
                act.activation(YS[:, t.p, :], YACC[:, t.n, :], ACT.Copy).then_inc(s.ys, 1)
            pairs(act, stage)

        @block.scalar
        def _(act):
            for k in range(6):
                w = P if k in (0, 1, 2, 5) else HA * MA
                act.wait_ge(pr.wt, k + 1)
                act.activation(WT[:, k, 0:w], bank[k][:, 0:w], ACT.Copy).then_inc(pr.wtc, 1)
            act.wait_ge(ld.bias, 16 * BIAS_LOADS)
            act.wait_ge(ld.consts, 16)
            act.activation(BBETA[:, :], BBETA[:, :], ACT.Copy, scale=0.5).then_inc(pr.bmix, 1)

            def step(t):
                nxt, old = t + 1, t + -1
                if t.real():
                    for k, name in enumerate("kq"):
                        u, ex, re, phi = ((A.u_k, A.ex_k, A.re_k, A.phi_k), (A.u_q, A.ex_q, A.re_q, A.phi_q))[k]
                        act.wait_ge(u, t.n + 1)
                        after(act, phi, t.n)
                        act.activation(EX[:, k, :], U[:, k, :], ACT.Exp).then_inc(ex, 1)
                        act.wait_ge(ex, t.n + 1)
                        act.activation(U[:, k, :], U[:, k, :], ACT.Relu).then_inc(re, 1)
                    for m in range(MA):
                        act.wait_ge(a_ready[f"b{m}"], t.n + 1)
                        after(act, A.scaled, t.n)
                        act.activation(TB[:, m, :], bank[PBANK[f"b{m}"]], ACT.Tanh, bias=BBETA[:, m:m + 1],
                                       scale=0.5).then_inc(a_used[f"b{m}"], 1)
                    act.wait_ge(a_ready["mx"], t.n + 1)
                    after(act, A.wgt, t.n - 1)
                    act.activation(MIX[:, t.p, :], bank[PBANK["mx"]][:, 0:SEQ], ACT.Tanh, bias=BMIXD[:, 1:2],
                                   scale=0.5).then_inc(a_used["mx"], 1)
                if old.real():
                    for m in range(MA):
                        act.wait_ge(A.rep, 2 * old.n + m + 1)
                        after(act, A.ay, 2 * old.n)
                        act.activation(RS[:, m, :], bank[7], ACT.Copy).then_inc(A.rs, 1)
                if nxt.real():
                    after(act, a_ready["v3"], nxt.n - 1)
                    norm_hi(act, n_a, nxt, bank[0], XH[:, nxt.p, :])

            act.wait_ge(pr.bmix, 3)
            run_steps(act, step)
            ffn_act(act, 0)

            def slot(t, b):
                nxt = t + 1
                n = t.n * SPT + b
                for k in range(UNITS):
                    if k == T_LAG - 1 and live(t, b, 1):
                        o, ob = n - 1, 1 - b
                        for h in range(2):
                            act.wait_ge(B.q2_ready, 2 * o + h + 1)
                            after(act, B.t_ready, UNITS * (o - 1))
                            act.activation(Q2[:, ob, 2 * h:2 * h + 2, :],
                                           r3(bank[6 + h], 2), ACT.Copy).then_inc(B.q2_used, 1)
                    if k == PV_LAG and live(t, b, 2):
                        for z in range(2):
                            act.wait_ge(B.pv, UNITS * (n - 1))
                            after(act, B.fold, n - 3)
                            act.activation(OS[:, b, z, :], bank[4 + z], ACT.Copy).then_inc(B.os, 1)
                    unit = unit_at(t, b, k, T_LAG)
                    if unit:
                        o, _, _, u = unit
                        q = UNITS * o + u
                        for dst in (PH, PT):
                            act.wait_ge(B.t_ready, q + 1)
                            after(act, B.pv, q - RING + 1)
                            after(act, B.pl, q - RING + 1)
                            act.activation(dst[:, u % RING, :], bank[2 + u % 2], ACT.Exp,
                                           scale=DB ** -0.5).then_inc(B.t_used, 1)
                    if k == OUT_STEP + 3 and live(t, b, 2):
                        act.wait_ge(B.ot, n - 1)
                        after(act, B.out, n - 3)
                        act.activation(OT[:, b, :], bank[7][:, 0:2 * C], ACT.Copy).then_inc(B.otc, 1)
                    if not nxt.real():
                        continue
                    if (b, k) == (0, 4):
                        after(act, B.v_ready, nxt.n - 1)
                        norm_hi(act, n_b, nxt, bank[6], XH[:, nxt.p, :])
                    if (b, k) in ((1, 0), (1, 4)):
                        i = k // 4
                        act.wait_ge((B.u_q, B.u_k)[i], nxt.n + 1)
                        after(act, B.kst_ready, nxt.n)
                        act.activation(QKH[:, i, :], QK[:, i, :], ACT.Copy).then_inc(B.hi, 1)
                    if b == 1 and 5 <= k < 5 + NJ:
                        j = k - 5
                        act.wait_ge(B.st_ready, NJ * nxt.n + j + 1)
                        after(act, B.q2_ready, 4 * (nxt.n - 1))
                        after(act, B.row_ready, 2 * UNITS * (nxt.n - 1))
                        act.activation(QST[:, nxt.p, j, :], bank[6], ACT.Copy).then_inc(B.st_used, 1)
                    if (b, k) == (1, 10):
                        act.wait_ge(B.kst_ready, nxt.n + 1)
                        after(act, B.t_ready, 2 * UNITS * (nxt.n - 1))
                        act.activation(KST[:, nxt.p, :], bank[6], ACT.Copy).then_inc(B.kst_used, 1)

            act.wait_ge(f[0].done, NT)
            for dst in [NMP[:, i, :, :, :].rearrange("p a j r -> p (a j r)") for i in range(2)] + \
                       [VS[:, i, :, :].rearrange("p s r -> p (s r)") for i in range(2)]:
                act.activation(dst, CST[:, 0:dst.shape[1]], ACT.Copy, scale=0.0).then_inc(pr.zero, 1)
            act.wait_ge(pr.zero, 4)
            for i in range(2):
                act.activation(VS[:, i, :, VAT + DB], ONES[:, 0:SUB], ACT.Copy).then_inc(pr.vone, 1)
            run_slots(act, slot)
            ffn_act(act, 1)

        def ffn_pe(pe, i):
            s = f[i]
            pe.wait_ge(*ffn_starts[i])

            def norm(t):
                after(pe, s.lo, s.base + t.n - 1)
                norm_turn(pe, s, t, bank[6 + t.p])
            pairs(pe, norm)
            pe.sem_inc(s.d, FC)

            def gate_up(m, t, u, k):
                cols = slice(k * P, (k + 1) * P)
                pe.wait_ge(s.sil, m * FC + k + 1)
                split_product(pe, bank[k % 2], WH[:, u, 0, cols], WL[:, u, 0, cols],
                              XTH[:, t, :], XTL[:, t, :]).then_inc(s.gate, 1)
                pe.wait_ge(s.mul, m * FC + k + 1)
                split_product(pe, bank[2 + k % 2], WH[:, u, 1, cols], WL[:, u, 1, cols],
                              XTH[:, t, :], XTL[:, t, :]).then_inc(s.up, 1)

            def down(m, u, p, k):
                cols = slice(k * P, (k + 1) * P)
                if k == 0:
                    pe.wait_ge(s.acc, m + 1)
                pe.wait_ge(s.hl, m * FC + k + 1)
                split_product(pe, bank[4 + p], WH[:, u, 2, cols], WL[:, u, 2, cols], HH[:, k, :], HL[:, k, :],
                              start=(k == 0), stop=(k == FC - 1)).then_inc(s.d, 1)

            def tile(m, t, u, p, before):
                gate_up(m, t, u, 0)
                if before is not None:
                    down(m - 1, before, 1 - p, 2)
                gate_up(m, t, u, 1)
                if before is not None:
                    down(m - 1, before, 1 - p, 3)
                gate_up(m, t, u, 2)
                down(m, u, p, 0)
                gate_up(m, t, u, 3)
                down(m, u, p, 1)

            pe.wait_ge(s.lo, s.base + NT)
            with pe.Fori(0, NE // 2) as e:
                for u in range(2):
                    first = (2 * e + u) * NT
                    pe.wait_ge(s.wl, 2 * e + u + 1)
                    tile(first, 0, u, 0, None if u == 0 else 0)
                    tile(first + 1, 1, u, 1, u)
                    with pe.Fori(1, NT // 2) as h:
                        tile(first + 2 * h, 2 * h, u, 0, u)
                        tile(first + 2 * h + 1, 2 * h + 1, u, 1, u)
                last = (2 * e + 2) * NT - 1
                down(last, 1, 1, 2)
                down(last, 1, 1, 3)

            def back(t):
                after(pe, s.ys, t.n + 1)
                after(pe, s.done, t.n - 1)
                for k in range(SUB):
                    m = pe.transpose(bank[6 + t.p][:, k * P:(k + 1) * P], YS[:, t.p, k * P:(k + 1) * P], ident)
                m.then_inc(s.back, 1)
            pairs(pe, back)

        @block.tensor
        def _(pe):
            pe.wait_ge(ld.consts, 16)
            pe.wait_ge(ld.wa, 96)
            for k in range(6):
                w = P if k in (0, 1, 2, 5) else HA * MA
                src = WRAW[0:w, k, :]
                if k == 5:
                    pe.wait_ge(pr.wout, 1)
                    src = LA[:, 0, :]
                pe.transpose(bank[k][:, 0:w], src, ident[0:w, 0:w]).then_inc(pr.wt, 1)

            def project(t, names, last_use):
                for name in names:
                    bk = bank[PBANK[name]]
                    prev, back = last_use[name]
                    after(pe, a_used[prev], t.n + 1 - back)
                    if name == "mx":
                        for b in range(SPT):
                            cols = slice(b * SEQ, (b + 1) * SEQ)
                            m = split_product(pe, bk[:, 0:SEQ], LAH[:, 10 + b, :], LAL[:, 10 + b, :],
                                              XH[:, t.p, cols], XL[:, t.p, cols], start=(b == 0), stop=(b == SPT - 1))
                    else:
                        k = {"k": 0, "ks": 1, "q": 2, "qs": 3, "v0": 4, "v1": 5, "v2": 6, "v3": 7, "b0": 8, "b1": 9}[name]
                        m = split_product(pe, bk, LAH[:, k, :], LAL[:, k, :], XH[:, t.p, :], XL[:, t.p, :])
                    m.then_inc(a_ready[name], 1)

            last_use = {n: (PROJ[i - 3], 0) for i, n in enumerate(PROJ) if i >= 3}
            for n in PROJ[:3]:
                last_use[n] = ([x for x in PROJ if PBANK[x] == PBANK[n]][-1], 1)

            def step(t):
                nxt, old = t + 1, t + -1
                if t.real():
                    pe.wait_ge(n_a.lo, t.n + 1)
                    project(t, PROJ[:7], last_use)
                if old.real():
                    after(pe, A.ay, 2 * old.n)
                    for m in range(MA):
                        pe.wait_ge((A.prod0, A.prod1)[m], old.n + 1)
                        for c in range(DA):
                            x = pe.matmul(bank[5 + m], cst(f"sum_{c}"), S[:, m, c, :], start=(c == 0), stop=(c == DA - 1))
                        x.then_inc(A.num, 1)
                    after(pe, A.zsum, old.n)
                    for b in range(SPT):
                        for m in range(MA):
                            x = pe.matmul(bank[4][:, 0:SEQ], cst(f"sum_{2 * b + m}"), S[:, m, 4, b * SEQ:(b + 1) * SEQ],
                                          start=(b + m == 0), stop=(b + m == 2))
                    x.then_inc(A.den, 1)
                if t.real():
                    project(t, PROJ[7:10], last_use)
                if old.real():
                    pe.wait_ge(A.wgt, old.n + 1)
                    for m in range(MA):
                        after(pe, A.rs, 2 * old.n + m)
                        for b in range(SPT):
                            x = pe.matmul(bank[7][:, b * SEQ:(b + 1) * SEQ], cst(f"rep_{2 * b + m}"), WGT[:, :],
                                          start=True, stop=True)
                        x.then_inc(A.rep, 1)
                if t.real():
                    project(t, PROJ[10:], last_use)
                if old.real():
                    pe.wait_ge(A.y, old.n + 1)
                    for k in range(SUB):
                        cols = slice(k * P, (k + 1) * P)
                        pe.matmul(bank[4][:, cols], Y[:, old.p, cols], WOUT[:, :], start=True, stop=False)
                        x = pe.matmul(bank[4][:, cols], ONES[0:1, :], BROW[:, 0:C], start=False, stop=True)
                    x.then_inc(A.z, 1)
                if nxt.real():
                    after(pe, n_a.lo, nxt.n)
                    norm_turn(pe, n_a, nxt, bank[0])

            pe.wait_ge(pr.lal, 1)
            pe.wait_ge(pr.wout, 2)
            pe.wait_ge(pr.ones, 2)
            pe.wait_ge(ld.bias, 16 * BIAS_LOADS)
            run_steps(pe, step)
            ffn_pe(pe, 0)

            SQ, SL, SK, SKL, SKONE, SID = 0, NJ, 2 * NJ, 2 * NJ + 1, 2 * NJ + 2, 2 * NJ + 3

            def rows(t, b, k):
                n = t.n * SPT + b
                g, half = (k, None) if k < NG else ((k - NG) // 2, (k - NG) % 2)
                q = QST[g * RG:(g + 1) * RG, t.p, :, b * SEQ:(b + 1) * SEQ]
                ks = KST[g * RG:(g + 1) * RG, t.p, b * SEQ:(b + 1) * SEQ]
                bk = bank[k % 2]
                after(pe, B.row_used, 12 * n + k - 1)
                if k < NG:
                    for j in range(NJ):
                        pe.matmul(bk[:, j * P:(j + 1) * P], q[:, j, 0:P], ks[:, 0:P], start=(j == 0), stop=False,
                                  skip_group_check=True)
                    m = pe.matmul(r3(bk, NJ), MASKB[:, 2, :], spread(MASKB[:, 0, :], NJ), start=False, stop=True,
                                  skip_group_check=True)
                else:
                    for j in range(2):
                        pe.matmul(bk[:, j * SEQ:(j + 1) * SEQ], q[:, 2 * half + j, P:SEQ], ks, start=(j == 0),
                                  stop=False, skip_group_check=True)
                    m = pe.matmul(r3(bk, 2)[:, :, P:SEQ], MASKB[:, 2, :], spread(MASKB[:, 0, :], 2), start=False,
                                  stop=True, skip_group_check=True)
                m.then_inc(B.row_ready, 1)

            def cols(o, p, ob, u):
                g = u // 2 if u < 8 else u - 8
                rg = slice(g * RG, (g + 1) * RG)
                bk = bank[2 + u % 2]
                after(pe, B.t_used, 2 * (UNITS * o + u - 1))
                if u < 8:
                    pe.matmul(bk, KST[rg, p, ob * SEQ:ob * SEQ + P], Q2[rg, ob, 2 * (u % 2):2 * (u % 2) + 2, :],
                              start=True, stop=False, skip_group_check=True)
                    m = pe.matmul(r3(bk, 2)[:, :, 0:P], MASKB[:, 2, :], spread(MASKB[:, 1, :], 2), start=False,
                                  stop=True, skip_group_check=True)
                else:
                    pe.matmul(bk, KST[rg, p, ob * SEQ + P:(ob + 1) * SEQ], Q2[rg, ob, :, P:SEQ], start=True,
                              stop=False, skip_group_check=True)
                    m = pe.matmul(r3(bk, NJ), MASKB[:, 2, :], spread(MASKB[:, 1, :], NJ), start=False, stop=True,
                                  skip_group_check=True)
                m.then_inc(B.t_ready, 1)

            def values(o, p, ob, u):
                if u < 2:
                    after(pe, B.os, 2 * o - 1 + u)
                pe.wait_ge(B.pl, UNITS * o + u + 1)
                at = VAT - RG * (u // 2 if u < 8 else u - 8)
                for i in range(2):
                    x = (PH, PL)[i][:, u % RING, :]
                    if u < 8:
                        m = pe.matmul(bank[4 + u % 2], VS[:, p, 2 * ob, at:at + P], x, start=(u < 2 and i == 0),
                                      stop=False, skip_group_check=True)
                    else:
                        for z in range(2):
                            m = pe.matmul(r3(bank[4 + z], 2)[:, :, P:SEQ], VS[:, p, 2 * ob + 1, at:at + P],
                                          r3(x, NJ)[:, 2 * z:2 * z + 2, :], start=False, stop=(u == UNITS - 1),
                                          skip_group_check=True)
                m.then_inc(B.pv, 1)

            def fold(o, ob, more):
                pe.wait_ge(B.os, 2 * (o + 1))
                after(pe, B.done, o)
                if more:
                    pe.wait_ge(B.q2_used, 2 * (o + 2))
                for a in range(2):
                    for j in range(NJ):
                        dst = bank[7][:, a * HB * (DB + 1):(a + 1) * HB * (DB + 1)]
                        dst = dst.rearrange("p (g j c) -> p g j c", g=NG, j=NJ)[:, :, j, :]
                        at = (j % 2) * SEQ + a * P
                        m = pe.matmul(dst, OS[:, ob, j // 2, at:at + P], r3(cst("fold"), NG), start=True, stop=True)
                m.then_inc(B.fold, 1)

            def turn_out(o, ob):
                pe.wait_ge(B.o, o + 1)
                for a in range(2):
                    m = pe.transpose(bank[7][:, a * P:(a + 1) * P], OB[:, ob, a, :], ident)
                m.then_inc(B.ot, 1)

            def project_out(o, ob):
                pe.wait_ge(B.otc, o + 1)
                for a in range(2):
                    dst = bank[7][:, a * P:(a + 1) * P]
                    pe.matmul(dst, OT[:, ob, a * P:(a + 1) * P], WOB[:, :], start=True, stop=False)
                    m = pe.matmul(dst, ONES[0:1, :], BROW[:, C:2 * C], start=False, stop=True)
                m.then_inc(B.out, 1)

            def stack2(o, p, ob, h):
                pe.wait_ge(B.nml, 2 * (o + 1))
                for x in range(2):
                    j = 2 * h + x
                    dst = bank[6 + h][:, x * SEQ:(x + 1) * SEQ]
                    pe.matmul(dst, SELR[:, SID, :], QST[:, p, j, ob * SEQ:(ob + 1) * SEQ], start=True, stop=False)
                    for a in range(2):
                        m = pe.matmul(dst[:, a * P:(a + 1) * P], NMP[:, ob, a, j, :], SELR[:, SID, :],
                                      start=False, stop=(a == 1))
                m.then_inc(B.q2_ready, 1)

            def project_b(nxt, i):
                pe.wait_ge(n_b.lo, n_b.base + nxt.n + 1)
                if i:
                    pe.wait_ge(b_used[BPROJ[i - 1]], nxt.n + 1)
                split_product(pe, bank[6], WBH[:, i, :], WBL[:, i, :], XH[:, nxt.p, :],
                              XL[:, nxt.p, :]).then_inc(b_ready[BPROJ[i]], 1)

            def project_v(nxt):
                pe.wait_ge(b_used[BPROJ[-1]], nxt.n + 1)
                for k in range(SUB):
                    dst = bank[6][:, k * DB:(k + 1) * DB]
                    c = slice(k * P, (k + 1) * P)
                    pe.matmul(dst, XH[:, nxt.p, c], WVH[:, :], start=True, stop=False)
                    pe.matmul(dst, XH[:, nxt.p, c], WVL[:, :], start=False, stop=False)
                    pe.matmul(dst, XL[:, nxt.p, c], WVH[:, :], start=False, stop=False)
                    m = pe.matmul(dst, ONES[0:1, :], BROW[:, 2 * C:], start=False, stop=True)
                m.then_inc(B.v_ready, 1)

            def query_stack(nxt, j):
                pe.wait_ge(B.v_used, nxt.n + 1) if j == 0 else pe.wait_ge(B.st_used, NJ * nxt.n + j)
                pe.wait_ge(B.lo, 2 * nxt.n + 1)
                pe.matmul(bank[6], SELR[:, SQ + j, :], QKH[:, 0, :], start=True, stop=False)
                pe.matmul(bank[6], SELR[:, SL + j, :], QKL[:, 0, :], start=False, stop=True).then_inc(B.st_ready, 1)

            def key_stack(nxt):
                pe.wait_ge(B.st_used, NJ * (nxt.n + 1))
                pe.wait_ge(B.lo, 2 * (nxt.n + 1))
                pe.matmul(bank[6], SELR[:, SK, :], QKH[:, 1, :], start=True, stop=False)
                pe.matmul(bank[6], SELR[:, SKL, :], QKL[:, 1, :], start=False, stop=False)
                pe.matmul(bank[6], SELR[0:1, SKONE, :], ONESR[:, :], start=False, stop=True).then_inc(B.kst_ready, 1)

            def slot(t, b):
                nxt = t + 1
                n = t.n * SPT + b
                has1, has2 = live(t, b, 1), live(t, b, 2)
                for k in range(UNITS):
                    if t.real():
                        if (b, k) == (0, 0):
                            pe.wait_ge(B.kst_used, t.n + 1)
                            pe.wait_ge(B.st_used, NJ * (t.n + 1))
                        rows(t, b, k)
                    unit = unit_at(t, b, k, T_LAG)
                    if unit:
                        if k == T_LAG:
                            pe.wait_ge(B.q2_used, 2 * n)
                        cols(*unit)
                    if k == T_LAG - 1 and has1:
                        op = t.p if b == 1 else 1 - t.p
                        if b == 0 and t.real():
                            pe.wait_ge(B.kst_used, t.n + 1)
                        if b == 1 and nxt.real():
                            pe.wait_ge(b_used[BPROJ[-1]], nxt.n + 1)
                        stack2(n - 1, op, 1 - b, 0)
                        after(pe, B.done, n - 2)
                        stack2(n - 1, op, 1 - b, 1)
                    if nxt.real():
                        if k == 3 and has1:
                            pe.wait_ge(B.q2_used, 2 * n - 1)
                        if (b, k) == (0, 3):
                            if t.real():
                                pe.wait_ge(B.kst_used, t.n + 1)
                            norm_turn(pe, n_b, nxt, bank[6])
                        if b == 0 and k >= 5 and k % 2 == 1:
                            project_b(nxt, (k - 5) // 2)
                        if (b, k) == (1, 3):
                            project_v(nxt)
                        if b == 1 and 5 <= k < 5 + NJ:
                            query_stack(nxt, k - 5)
                        if (b, k) == (1, 10):
                            key_stack(nxt)
                    unit = unit_at(t, b, k, PV_LAG)
                    if unit:
                        values(*unit)
                    if has2:
                        if k == OUT_STEP:
                            fold(n - 2, b, has1)
                        if k == OUT_STEP + 2:
                            turn_out(n - 2, b)
                        if k == OUT_STEP + 4:
                            project_out(n - 2, b)

            pe.wait_ge(f[0].done, NT)
            pe.wait_ge(pr.selr, 2 * NJ + 4 + 3 + SUB)
            pe.wait_ge(pr.wbl, 2)
            pe.wait_ge(pr.zero, 4)
            pe.wait_ge(pr.vone, 2)
            run_slots(pe, slot)
            ffn_pe(pe, 1)

        def ffn_dve(v, i):
            s = f[i]
            v.wait_ge(*ffn_starts[i])

            def norm(t):
                norm_stats(v, s, t)
                norm_apply(v, s, t)
                norm_lo(v, s, t, bank[6 + t.p], XTH[:, t.n, :], XTL[:, t.n, :])
            pairs(v, norm)
            v.sem_inc(s.mul, 2)
            v.sem_inc(s.acc, 2)
            v.wait_ge(s.zero, 1)

            def mul(m, k):
                v.wait_ge(s.up, m * FC + k + 1)
                v.wait_ge(s.sil, m * FC + k + 3)
                v.wait_ge(s.d, m * FC + k + 1)
                v.tensor_tensor(HF[:, k, :], SG[:, k % 2, :], bank[2 + k % 2], ALU.mult).then_inc(s.mul, 1)

            def lo(m, k):
                v.wait_ge(s.hh, m * FC + k + 1)
                v.tensor_tensor(HL[:, k, :], HF[:, k, :], HH[:, k, :].bitcast(F32), ALU.subtract).then_inc(s.hl, 1)

            def add(m, t, p):
                v.wait_ge(s.d, (m + 2) * FC)
                v.tensor_tensor(YACC[:, t, :], YACC[:, t, :], bank[4 + p], ALU.add).then_inc(s.acc, 1)

            def tile(m, p, before):
                mul(m, 0)
                mul(m, 1)
                lo(m, 0)
                if before is not None:
                    add(m - 1, before, 1 - p)
                mul(m, 2)
                lo(m, 1)
                mul(m, 3)
                lo(m, 2)
                lo(m, 3)

            with v.Fori(0, NE // 2) as e:
                for u in range(2):
                    first = (2 * e + u) * NT
                    tile(first, 0, None if u == 0 else NT - 1)
                    tile(first + 1, 1, 0)
                    with v.Fori(1, NT // 2) as h:
                        tile(first + 2 * h, 0, 2 * h - 1)
                        tile(first + 2 * h + 1, 1, 2 * h)
                add((2 * e + 2) * NT - 1, NT - 1, 1)

            def residual(t):
                after(v, s.back, t.n + 1)
                v.tensor_tensor(X[:, t.n, :, :], X[:, t.n, :, :], by_sub(bank[6 + t.p]), ALU.add).then_inc(s.done, 1)
            pairs(v, residual)

        @block.vector
        def _(v):
            v.wait_ge(ld.bias, 16 * BIAS_LOADS)
            v.wait_ge(ld.consts, 16)
            v.tensor_tensor(BMIXD[:, 0:1], BMIX[:, 0:1], BMIX[:, 1:2], ALU.subtract).then_inc(pr.bmix, 1)
            v.wait_ge(pr.bmix, 2)
            v.tensor_scalar(BMIXD[:, 1:2], BMIXD[:, 0:1], cst("sign"), 0.5, ALU.mult, ALU.mult).then_inc(pr.bmix, 1)

            def rope_part(t, k, name, table, dst):
                v.wait_ge(a_ready[name], t.n + 1)
                after(v, (A.u_k, A.u_q)[k], t.n)
                v.tensor_tensor(seqs(dst), seqs(bank[PBANK[name]]), spread(cst(table), SPT),
                                ALU.mult).then_inc(a_used[name], 1)

            def phi(t, k):
                v.wait_ge((A.re_k, A.re_q)[k], t.n + 1)
                if k == 0:
                    after(v, A.scan, 10 * t.n)
                else:
                    after(v, A.prod0, t.n - 1)
                    after(v, A.prod1, t.n - 1)
                v.scalar_tensor_tensor(KV[:, 4, :] if k == 0 else PQ[:, t.p, :], EX[:, k, :], 1.0, U[:, k, :],
                                       ALU.min, ALU.add).then_inc((A.phi_k, A.phi_q)[k], 1)

            def step(t):
                nxt, old = t + 1, t + -1
                if nxt.real():
                    if isinstance(nxt.n, int) and nxt.n < 2:
                        v.wait_ge((ld.x0, ld.x1)[nxt.n], 16)
                    else:
                        v.wait_ge(ld.x, 16 * (NT - 2))
                    norm_stats(v, n_a, nxt)
                if t.real():
                    rope_part(t, 0, "k", "cos_a", R1[:, 0, :])
                    rope_part(t, 0, "ks", "sin_a", R2[:, 0, :])
                    rope_part(t, 1, "q", "cos_a", R1[:, 1, :])
                    rope_part(t, 1, "qs", "sin_a", R2[:, 1, :])
                if old.real():
                    v.wait_ge(A.den, old.n + 1)
                    v.tensor_scalar(DP[:, :], bank[4][:, 0:SEQ], DEN_EPS, None, ALU.add).then_inc(A.dp, 1)
                    v.wait_ge(A.dp, old.n + 1)
                    v.reciprocal(RC[:, :], DP[:, :]).then_inc(A.rc, 1)
                    v.wait_ge(A.rc, old.n + 1)
                    v.wait_ge(a_used["mx"], old.n + 1)
                    v.scalar_tensor_tensor(WGT[:, :], MIX[:, old.p, :], 1.0, RC[:, :], ALU.add,
                                           ALU.mult).then_inc(A.wgt, 1)
                if t.real():
                    phi(t, 0)
                    phi(t, 1)
                if old.real():
                    for m in range(MA):
                        v.wait_ge(A.rs, 2 * old.n + m + 1)
                        after(v, A.y, old.n)
                        v.tensor_tensor(AY[:, m, :], RS[:, m, :], bank[5 + m], ALU.mult).then_inc(A.ay, 1)
                if t.real():
                    v.wait_ge(A.phi_k, t.n + 1)
                    for c in range(DA):
                        v.wait_ge(a_ready[f"v{c}"], t.n + 1)
                        v.tensor_tensor(KV[:, c, :], KV[:, 4, :], bank[PBANK[f"v{c}"]],
                                        ALU.mult).then_inc(a_used[f"v{c}"], 1)
                if old.real():
                    v.wait_ge(A.z, old.n + 1)
                    after(v, A.zn, SUB * old.n)
                    v.tensor_tensor(Z[:, :, :], XN[:, old.p, :, :], by_sub(bank[4]), ALU.add).then_inc(A.zsum, 1)
                    v.wait_ge(A.zsum, old.n + 1)
                    after(v, A.mv2, SUB * old.n)
                    for k in range(SUB):
                        v.bn_stats(ST2[:, k, :], Z[:, k, :]).then_inc(A.st2, 1)
                    v.wait_ge(A.st2, SUB * (old.n + 1))
                    carry(v)
                    for k in range(SUB):
                        v.bn_aggr(MV2[:, k, :], ST2[:, k, :]).then_inc(A.mv2, 1)
                if nxt.real():
                    after(v, A.zsum, nxt.n - 1)
                    norm_apply(v, n_a, nxt)
                if t.real():
                    v.wait_ge(A.beta, t.n + 1)
                    v.wait_ge(a_used["v3"], t.n + 1)
                    after(v, A.den, t.n)
                    for m in range(MA):
                        for c in range(5):
                            v.tensor_tensor_scan(S[:, m, c, :], BETA[:, m, :], KV[:, c, :], 0.0, ALU.mult,
                                                 ALU.add).then_inc(A.scan, 1)
                if old.real():
                    v.wait_ge(A.rstd2, old.n + 1)
                    after(v, A.done, old.n)
                    for k in range(SUB):
                        v.tensor_scalar(ZN[:, k, :], Z[:, k, :], MV2[:, k, 0:1], RSTD2[:, k:k + 1], ALU.subtract,
                                        ALU.mult).then_inc(A.zn, 1)
                if t.real():
                    v.wait_ge(A.scan, 10 * t.n + 5)
                    v.wait_ge(A.phi_q, t.n + 1)
                    v.tensor_tensor(S[:, 0, :, :], S[:, 0, :, :], spread(PQ[:, t.p, :], 5),
                                    ALU.mult).then_inc(A.prod0, 1)
                if nxt.real():
                    after(v, a_ready["v3"], nxt.n - 1)
                    norm_lo(v, n_a, nxt, bank[0], XH[:, nxt.p, :], XL[:, nxt.p, :])

            v.wait_ge(pr.ones, 2)
            run_steps(v, step)
            ffn_dve(v, 0)

            def maximum(t, b, k):
                n = t.n * SPT + b
                after(v, B.nml, 2 * (n - 1))
                v.wait_ge(B.row_ready, UNITS * n + k + 1)
                if k < NG:
                    dst, src = NM[:, b, 0, NJ * k:NJ * (k + 1)], r3(bank[k % 2], NJ)
                else:
                    h = 2 * (k - NG)
                    dst, src = NM[:, b, 1, h:h + 2], r3(bank[k % 2], 2)
                v.tensor_reduce(dst, src, AX.X, ALU.max, negate=True).then_inc(B.row_used, 1)

            def split_maxima(t, b):
                n = t.n * SPT + b
                v.wait_ge(B.row_used, UNITS * (n + 1))
                after(v, B.q2_ready, 2 * (n - 1))
                dst = lambda a, r: NMP[:, b, a, :, :].rearrange("p j (g r) -> p g j r", g=NG)[:, :, :, r]
                src = lambda a: NM[:, b, a, :].rearrange("p (g j) -> p g j", g=NG)
                for a in range(2):
                    v.tensor_copy(dst(a, 3 * DB), src(a)).then_inc(B.nmh, 1)
                v.wait_ge(B.nmh, 2 * (n + 1))
                for a in range(2):
                    v.tensor_tensor(dst(a, 3 * DB + 1), src(a), dst(a, 3 * DB).bitcast(F32),
                                    ALU.subtract).then_inc(B.nml, 1)

            def normalise(o, ob):
                v.wait_ge(B.fold, o + 1)
                after(v, B.o, o)
                acc = bank[7][:, 0:2 * HB * (DB + 1)].rearrange("p (a h c) -> p (a h) c", a=2, h=HB)
                ro = RO[:, :, :].rearrange("p a h -> p (a h)")
                v.reciprocal(ro, acc[:, :, DB]).then_inc(B.ro, 1)
                v.wait_ge(B.ro, o + 1)
                after(v, B.ot, o - 1)
                v.tensor_tensor(OB[:, ob, :, :].rearrange("p a (h c) -> p (a h) c", h=HB), acc[:, :, 0:DB],
                                spread_in(ro, DB), ALU.mult).then_inc(B.o, 1)

            def residual_b(n, t_n, b):
                v.wait_ge(B.out, n + 1)
                xs = X[:, t_n, 2 * b:2 * b + 2, :]
                v.tensor_tensor(xs, xs, bank[7][:, 0:2 * C].rearrange("p (a c) -> p a c", a=2),
                                ALU.add).then_inc(B.done, 1)

            def rope_b(t, k, name, table, dst, bias):
                v.wait_ge(b_ready[name], t.n + 1)
                after(v, (B.u_q, B.u_k)[k], t.n)
                v.scalar_tensor_tensor(seqs(dst), seqs(bank[6]), bias, spread(cst(table), SPT), ALU.add,
                                       ALU.mult).then_inc(b_used[name], 1)

            def split_b(nxt, i):
                v.wait_ge(B.hi, 2 * nxt.n + i + 1)
                after(v, B.kst_ready, nxt.n)
                v.tensor_tensor(QKL[:, i, :], QK[:, i, :], QKH[:, i, :].bitcast(F32), ALU.subtract).then_inc(B.lo, 1)

            def split_v(nxt):
                src = bank[6][:, 0:SUB * DB].rearrange("p (s c) -> p s c", s=SUB)
                part = lambda c: VS[:, nxt.p, :, VAT + c:VAT + c + DB]
                v.wait_ge(B.v_ready, nxt.n + 1)
                after(v, B.pv, 2 * UNITS * (nxt.n - 1))
                v.tensor_copy(part(0), src).then_inc(B.vhi, 1)
                v.wait_ge(B.vhi, nxt.n + 1)
                v.tensor_tensor(part(DB + 1), src, part(0).bitcast(F32),
                                ALU.subtract).then_inc(B.v_used, 1)

            def slot(t, b):
                nxt = t + 1
                n = t.n * SPT + b
                for k in range(UNITS):
                    if t.real():
                        maximum(t, b, k)
                    if live(t, b, 2):
                        if k == OUT_STEP + 1:
                            normalise(n - 2, b)
                        if k == OUT_STEP + 5:
                            residual_b(n - 2, t.n - 1, b)
                    if not nxt.real():
                        continue
                    if (b, k) == (0, 0):
                        norm_stats(v, n_b, nxt)
                    if (b, k) == (0, 2):
                        norm_apply(v, n_b, nxt)
                    if (b, k) == (0, 4):
                        after(v, B.v_ready, nxt.n - 1)
                        norm_lo(v, n_b, nxt, bank[6], XH[:, nxt.p, :], XL[:, nxt.p, :])
                    if (b, k) == (0, 6):
                        rope_b(nxt, 0, "q", "cos_b", B1[:, 0, :], BQK[:, 0:1])
                    if (b, k) == (0, 8):
                        rope_b(nxt, 0, "qs", "sin_b", B2[:, 0, :], BQK[:, 1:2])
                    if (b, k) == (0, 10):
                        rope_b(nxt, 1, "k", "cos_b", B1[:, 1, :], BQK[:, 2:3])
                    if (b, k) == (1, 0):
                        rope_b(nxt, 1, "ks", "sin_b", B2[:, 1, :], BQK[:, 3:4])
                    if (b, k) == (1, 2):
                        split_b(nxt, 0)
                    if (b, k) == (1, 4):
                        split_v(nxt)
                    if (b, k) == (1, 5):
                        split_b(nxt, 1)
                if t.real():
                    split_maxima(t, b)

            v.wait_ge(f[0].done, NT)
            v.wait_ge(pr.zero, 4)
            v.wait_ge(pr.vone, 2)
            run_slots(v, slot)
            ffn_dve(v, 1)


_INS = ["L0_attn_a_" + n for n in "x Wq Wk Wv Wbeta bbeta Wmix bmix Wout bout ln_g ln_b".split()] + \
       ["L0_attn_b_" + n for n in "Wq bq Wk bk Wv bv Wo bo".split()] + ["L0_ffn_" + n for n in "Wg Wu Wd".split()]


def kernel(**inputs):
    import numpy as _np
    import concourse.bacc as _bacc
    from concourse import mybir as _mybir
    from concourse.bass_utils import run_bass_kernel_spmd as _run

    nc = _bacc.Bacc("TRN2", target_bir_lowering=False, num_devices=1)
    arrays, args = {}, []
    for name in _INS:
        a = _np.ascontiguousarray(inputs[name])
        arrays[f"in_{name}_dram"] = a
        args.append(nc.dram_tensor(f"in_{name}_dram", a.shape, _mybir.dt.from_np(a.dtype), kind="ExternalInput").ap())
    tables = _np.concatenate(list(_C.values()), axis=1)
    arrays["in_tables_dram"] = tables
    args.append(nc.dram_tensor("in_tables_dram", tables.shape, _mybir.dt.float32, kind="ExternalInput").ap())
    shape = inputs["L0_attn_a_x"].shape
    args.append(nc.dram_tensor("out_0_dram", shape, _mybir.dt.float32, kind="ExternalOutput").ap())
    program(nc, *args)
    r = _run(nc, [arrays], core_ids=[0])
    return r.results[0]["out_0_dram"]
```

```python
from collections import namedtuple
from contextlib import ExitStack

import numpy as np
import concourse.bass as bass
from concourse import mybir

F32 = mybir.dt.float32
F32R = mybir.dt.float32r
BF16 = mybir.dt.bfloat16
ALU = mybir.AluOpType
ACT = mybir.ActivationFunctionType
AX = mybir.AxisListType

P = 128
NSEQ, SEQ, C = 16, 256, 128
TOK = 512
SUB = TOK // P
NT = NSEQ * SEQ // TOK
SPT = TOK // SEQ
HA, DA, MA = 32, 4, 2
HB, DB = 16, 8
NE, FFN = 8, 512
FC = FFN // P
LN_EPS = 1e-5
DEN_EPS = 1e-6
BMIN, BMAX = 0.85, 0.9995
NG, NJ = 4, 4
RG = 32
MASKED = -1e30
UNITS = 12
RING = 4
T_LAG, PV_LAG = 2, 5
OUT_STEP = 5


def constants():
    c = {}
    eye = np.eye(P, dtype=np.float32)
    c["ident"] = eye
    pos = np.arange(SEQ, dtype=np.float32)
    inv = (1.0 / 10000.0 ** (np.arange(DA // 2, dtype=np.float32) / (DA // 2))).astype(np.float32)
    d = np.arange(P) // HA
    ang = pos[None, :] * inv[d % (DA // 2)][:, None]
    c["cos_a"] = np.cos(ang)
    c["sin_a"] = np.sin(ang) * np.where(d < DA // 2, -1.0, 1.0)[:, None]
    h = np.arange(P) % HA
    q = np.arange(P) // HA
    same = (h[:, None] == h[None, :]).astype(np.float32)
    for s in range(4):
        c[f"sum_{s}"] = same * (q[None, :] == s)
    for s in range(4):
        c[f"rep_{s}"] = same * (q[:, None] == s)
    c["sign"] = np.where((np.arange(P) // HA) % MA == 0, 1.0, -1.0)[:, None]
    inv = (1.0 / 10000.0 ** (np.arange(0, DB, 2, dtype=np.float32) / DB)).astype(np.float32)
    d = np.arange(P) % DB
    ang = pos[None, :] * inv[d % (DB // 2)][:, None]
    c["cos_b"] = np.cos(ang) * np.where(d < DB // 2, 1.0, -1.0)[:, None]
    c["sin_b"] = np.sin(ang)
    for j in range(NJ):
        hi = np.zeros((P, P), np.float32)
        lo = np.zeros((P, P), np.float32)
        for g in range(NG):
            for x in range(DB):
                src = (NJ * g + j) * DB + x
                hi[src, RG * g + x] = hi[src, RG * g + DB + x] = lo[src, RG * g + 2 * DB + x] = 1
        c[f"qhi_{j}"], c[f"qlo_{j}"] = hi, lo
    hi = np.zeros((P, P), np.float32)
    lo = np.zeros((P, P), np.float32)
    for g in range(NG):
        for x in range(DB):
            hi[x, RG * g + x] = hi[x, RG * g + 2 * DB + x] = lo[x, RG * g + DB + x] = 1
    c["khi"], c["klo"] = hi, lo
    ones = np.zeros((P, P), np.float32)
    for g in range(NG):
        ones[0, RG * g + 3 * DB:RG * g + 3 * DB + 2] = 1
    c["kone"] = ones
    r = np.arange(P)
    c["mask_rows"] = np.where(r[None, :] > r[:, None], MASKED, 0.0)
    c["mask_cols"] = np.where(r[:, None] > r[None, :], MASKED, 0.0)
    return {k: np.asarray(v, np.float32) for k, v in c.items()}


_C = constants()
CPOS, _at = {}, 0
for _k, _v in _C.items():
    CPOS[_k] = (_at, _v.shape[1])
    _at += _v.shape[1]
CWIDTH = _at
CB = CPOS["cos_b"][0]


class Tile:

    def __init__(self, n, p):
        self.n, self.p = n, p

    def __add__(self, k):
        return Tile(self.n + k, (self.p + k) % 2)

    def real(self):
        return not isinstance(self.n, int) or 0 <= self.n < NT


def after(eng, sem, n):
    if not (isinstance(n, int) and n <= 0):
        eng.wait_ge(sem, n)


def run_steps(eng, step):
    for n in (-1, 0, 1):
        step(Tile(n, n % 2))
    with eng.Fori(1, NT // 2 - 1) as i:
        step(Tile(2 * i, 0))
        step(Tile(2 * i + 1, 1))
    for n in (NT - 2, NT - 1, NT):
        step(Tile(n, n % 2))


def program(nc, a_x, a_Wq, a_Wk, a_Wv, a_Wbeta, a_bbeta, a_Wmix, a_bmix, a_Wout, a_bout, a_ln_g, a_ln_b,
            b_Wq, b_bq, b_Wk, b_bk, b_Wv, b_bv, b_Wo, b_bo, f_Wg, f_Wu, f_Wd, consts, out):
    ctx = ExitStack()
    with ctx:
        def sb(name, shape, dt=F32):
            return ctx.enter_context(nc.sbuf_tensor(name, shape, dt))

        def sem(name):
            return ctx.enter_context(nc.semaphore(name))

        def sems(prefix, names):
            return namedtuple(prefix, names)(*[sem(f"{prefix}_{n}") for n in names.split()])

        def spread(ap, n):
            return bass.AP(ap.tensor, ap.offset, [ap.ap[0], [0, n], ap.ap[1]])

        def r3(ap, n):
            return ap.rearrange("p (a b) -> p a b", a=n)

        single = {i: ctx.enter_context(nc.psum_tensor(f"bank{i}", [P, 512], F32)) for i in (0, 1, 6, 7)}
        pair = [ctx.enter_context(nc.psum_tensor(f"pair{i}", [P, 2, 512], F32)) for i in range(2)]
        bank = [single[i][:, :] if i in single else pair[i // 2 - 1][:, i % 2, :] for i in range(8)]

        X = sb("X", [P, NT, SUB, C])
        CST = sb("CST", [P, CWIDTH])

        def cst(name):
            at, w = CPOS[name]
            return CST[:, at:at + w]

        ident = cst("ident")
        SELR = sb("SELR", [P, 2 * NJ + 4, P], F32R)
        MASKB = sb("MASKB", [P, 3, P], BF16)
        ONES = sb("ONES", [P, P])
        ONESR = sb("ONESR", [1, TOK], F32R)
        HALF = sb("HALF", [P, SUB])
        WOUT = sb("WOUT", [P, C])
        WBH = sb("WBH", [P, 4, P], F32R)
        WBL = sb("WBL", [P, 4, P], F32R)
        WVH = sb("WVH", [P, DB], F32R)
        WVL = sb("WVL", [P, DB], F32R)
        WOB = sb("WOB", [P, C])
        BROW = sb("BROW", [1, 2 * C + DB])
        GB = sb("GB", [P, 2, C])
        BQK = sb("BQK", [P, 4])
        BAH = sb("BAH", [HA, 2, MA])
        BA = sb("BA", [P, 2, MA])
        BMIXD = sb("BMIXD", [P, 2])
        XN = sb("XN", [P, 2, SUB, C])
        ST = sb("ST", [P, 2, SUB, 6])
        MV = sb("MV", [P, 2, SUB, 2])
        VE = sb("VE", [P, 2, SUB])
        RSTD = sb("RSTD", [P, 2, SUB])
        ST2 = sb("ST2", [P, SUB, 6])
        MV2 = sb("MV2", [P, SUB, 2])
        VE2 = sb("VE2", [P, SUB])
        RSTD2 = sb("RSTD2", [P, SUB])

        ARENA = sb("ARENA", [P, 20224])
        ARENA_R = sb("ARENA_R", [P, 19200], F32R)
        at = {F32: 0, F32R: 0}

        def take(*shape, dt=F32):
            n = int(np.prod(shape))
            a = {F32: ARENA, F32R: ARENA_R}[dt]
            ap = a[:, at[dt]:at[dt] + n]
            at[dt] += n
            names = "abcde"[:len(shape)]
            return ap.rearrange(f"p ({' '.join(names)}) -> p {' '.join(names)}", **dict(zip(names, shape)))

        def rewind():
            at[F32] = at[F32R] = 0

        WRAW = take(6, P)
        WT = take(6, P)
        LA = take(12, P)
        rewind()
        S = take(MA, 5, TOK)
        KV = take(5, TOK)
        R1 = take(2, TOK)
        R2 = take(2, TOK)
        U = take(2, TOK)
        EX = take(2, TOK)
        PQ = take(2, TOK)
        TB = take(MA, TOK)
        BETA = take(MA, TOK)
        MIX = take(2, SEQ)
        DP, RC, WGT = take(SEQ), take(SEQ), take(SEQ)
        RS = take(MA, TOK)
        AY = take(MA, TOK)
        Y = take(2, TOK)
        Z = take(SUB, C)
        ZN = take(SUB, C)
        XH = take(2, TOK, dt=F32R)
        XL = take(2, TOK, dt=F32R)
        LAH = take(12, P, dt=F32R)
        LAL = take(12, P, dt=F32R)
        rewind()
        B1 = take(2, TOK)
        B2 = take(2, TOK)
        QK = take(2, TOK)
        PT = take(RING, TOK)
        OS = take(2, 2, TOK)
        OC = take(2, 2, NG, NJ, DB)
        OB = take(2, 2, C)
        OT = take(2, 2 * C)
        take(2, TOK, dt=F32R), take(2, TOK, dt=F32R)
        QKH = take(2, TOK, dt=F32R)
        QKL = take(2, TOK, dt=F32R)
        QST = take(2, NJ, TOK, dt=F32R)
        KST = take(2, TOK, dt=F32R)
        NMP = take(2, 2, NJ, P, dt=F32R)
        Q2 = take(2, NJ, SEQ, dt=F32R)
        PH = take(RING, TOK, dt=F32R)
        PL = take(RING, TOK, dt=F32R)
        VS = take(2, SUB, 2 * P - RG, dt=F32R)
        rewind()
        YACC = take(NT, TOK)
        SG = take(2, TOK)
        HF = take(FC, TOK)
        YS = take(2, TOK)
        take(TOK)
        WS = take(2, 3, FFN)
        WB = take(4, P)
        WQB, WKB, WVB = take(C), take(DB), take(DB)
        BRAW = take(C + DB)[0:1, :]
        BQKR = take(4, C)[0:1, :, :]
        XNF = take(NT, SUB, C)
        NM = take(2, 2, HB)
        RO = take(2, HB)
        XTH = take(NT, TOK, dt=F32R)
        XTL = take(NT, TOK, dt=F32R)
        WH = take(2, 3, FFN, dt=F32R)
        WL = take(2, 3, FFN, dt=F32R)
        HH = take(FC, TOK, dt=F32R)
        HL = take(FC, TOK, dt=F32R)

        ld = sems("ld", "x0 x1 x tables_a tables_b wa wb ba bb")
        pr = sems("prep", "wt wtc la ones selr wb wout ba bmix bqkr bqk zero")
        PROJ = ["k", "ks", "q", "qs", "b0", "b1", "mx", "v0", "v1", "v2", "v3"]
        PBANK = {n: 1 + i % 3 for i, n in enumerate(PROJ)}
        a_ready = {n: sem(f"a_{n}_ready") for n in PROJ}
        a_used = {n: sem(f"a_{n}_used") for n in PROJ}
        A = sems("a", "u_k u_q ex_k ex_q re_k re_q phi_k phi_q clip scaled beta scan prod0 prod1 num den dp rc wgt rep "
                      "rs ay y z zsum st2 mv2 ve2 rstd2 zn zg zb done")
        NORM = "st mv ve rstd xn tp hi lo"
        norm_sems = sems("norm", NORM)

        def norm_of(phase, names="", *more):
            return namedtuple("phase", f"{NORM} base {names}")(*norm_sems, phase * NT, *more)

        n_a, n_b = norm_of(0), norm_of(2)
        BPROJ = ["q", "qs", "k", "ks"]
        b_ready = {n: sem(f"b_{n}_ready") for n in BPROJ}
        b_used = {n: sem(f"b_{n}_used") for n in BPROJ}
        B = sems("b", "u_q u_k hi lo v_ready v_used st_ready st_used kst_ready kst_used row_ready row_used nmh nml "
                      "q2_ready q2_used t_ready t_used pl vhi pv os turn oc ro o ot otc out done")
        FSEMS = "wload0 wload1 wh wl gate up sil mul hh hl d acc ys back done zero"
        f = [norm_of(2 * i + 1, FSEMS, *sems(f"f{i}", FSEMS)) for i in range(2)]
        stored = sem("stored")
        carried = sem("carried")

        def carry(eng):
            eng.sem_inc(carried, 1)

        x_tok = a_x.rearrange("b t c -> (b t) c").rearrange("(n s p) c -> p n s c", n=NT, p=P)
        o_tok = out.rearrange("b t c -> (b t) c").rearrange("(n s p) c -> p n s c", n=NT, p=P)

        block = ctx.enter_context(nc.Block())

        def seqs(ap):
            return ap.rearrange("p (a t) -> p a t", a=SPT)

        def by_sub(ap):
            return ap.rearrange("p (s c) -> p s c", s=SUB)

        def split_product(pe, dst, wh, wl, xh, xl, start=True, stop=True):
            pe.matmul(dst, wh, xh, start=start, stop=False)
            pe.matmul(dst, wh, xl, start=False, stop=False)
            return pe.matmul(dst, wl, xh, start=False, stop=stop)

        def quads(eng, step, n=NT):
            for k in range(4):
                step(Tile(k, k % 2))
            with eng.Fori(2, n // 2) as i:
                step(Tile(2 * i, 0))
                step(Tile(2 * i + 1, 1))

        def norm_stats(v, s, t):
            n = s.base + t.n
            after(v, s.mv, SUB * (n - 1))
            for i in range(SUB):
                v.bn_stats(ST[:, t.p, i, :], X[:, t.n, i, :]).then_inc(s.st, 1)
            after(v, s.st, SUB * (n + 1))
            after(v, s.ve, n - 1)
            after(v, s.xn, SUB * (n - 1))
            carry(v)
            for i in range(SUB):
                v.bn_aggr(MV[:, t.p, i, :], ST[:, t.p, i, :]).then_inc(s.mv, 1)

        def norm_rstd(g, s, t):
            n = s.base + t.n
            after(g, s.mv, SUB * (n + 1))
            after(g, s.rstd, n - 1)
            carry(g)
            g.tensor_scalar(VE[:, t.p, :], MV[:, t.p, :, 1], LN_EPS, None, ALU.add).then_inc(s.ve, 1)
            after(g, s.ve, n + 1)
            after(g, s.xn, SUB * (n - 1))
            g.tensor_tensor(RSTD[:, t.p, :], VE[:, t.p, :], HALF[:, :], ALU.pow).then_inc(s.rstd, 1)

        def norm_apply(v, s, t, dst=XN):
            n = s.base + t.n
            after(v, s.rstd, n + 1)
            after(v, s.tp, n - 1)
            for i in range(SUB):
                v.tensor_scalar(dst[:, t.p, i, :], X[:, t.n, i, :], MV[:, t.p, i, 0:1], RSTD[:, t.p, i:i + 1],
                                ALU.subtract, ALU.mult).then_inc(s.xn, 1)

        def norm_turn(pe, s, t, dst, src=XN):
            n = s.base + t.n
            after(pe, s.xn, SUB * (n + 1))
            for i in range(SUB):
                m = pe.transpose(dst[:, i * P:(i + 1) * P], src[:, t.p, i, :], ident)
            m.then_inc(s.tp, 1)

        XF = XNF[:, 1:3, :, :]

        def meanwhile(t, stage, tiles):
            if isinstance(t.n, int) and t.n == NT:
                for n in tiles:
                    stage(Tile(n, n % 2))

        def first_norm_dve(v, t):
            nxt, old = t + 1, t + -1
            if nxt.real():
                v.wait_ge(A.done, nxt.n + 1)
                norm_stats(v, f[0], nxt)
            if t.real():
                norm_apply(v, f[0], t, XF)
            if old.real():
                norm_lo(v, f[0], old, bank[old.p], XTH[:, old.n, :], XTL[:, old.n, :])

        def first_norm_turn(pe, t):
            after(pe, f[0].lo, f[0].base + t.n - 1)
            norm_turn(pe, f[0], t, bank[t.p], XF)

        def early_stats(v, t):
            n = NT + t.n
            v.wait_ge(B.done, SPT * (t.n + 1))
            after(v, A.mv2, SUB * n)
            carry(v)
            for k in range(SUB):
                v.bn_stats(ST2[:, k, :], X[:, t.n, k, :]).then_inc(A.st2, 1)
            v.wait_ge(A.st2, SUB * (n + 1))
            v.wait_ge(A.ve2, n)
            v.wait_ge(A.zn, SUB * n)
            carry(v)
            for k in range(SUB):
                v.bn_aggr(MV2[:, k, :], ST2[:, k, :]).then_inc(A.mv2, 1)

        def early_rstd(g, t):
            n = NT + t.n
            g.wait_ge(A.mv2, SUB * (n + 1))
            g.wait_ge(A.rstd2, n)
            carry(g)
            g.tensor_scalar(VE2[:, :], MV2[:, :, 1], LN_EPS, None, ALU.add).then_inc(A.ve2, 1)
            g.wait_ge(A.ve2, n + 1)
            g.wait_ge(A.zn, SUB * n)
            g.tensor_tensor(RSTD2[:, :], VE2[:, :], HALF[:, :], ALU.pow).then_inc(A.rstd2, 1)

        def early_apply(v, t):
            v.wait_ge(A.rstd2, NT + t.n + 1)
            for k in range(SUB):
                v.tensor_scalar(XNF[:, t.n, k, :], X[:, t.n, k, :], MV2[:, k, 0:1], RSTD2[:, k:k + 1], ALU.subtract,
                                ALU.mult).then_inc(A.zn, 1)

        LAST = Tile(NT - 1, (NT - 1) % 2)

        def early_tile(t, b, k):
            if isinstance(t.n, int) and (t.n, b) == (NT, SPT - 1) and 0 <= k - PV_LAG < NT - 1:
                return Tile(k - PV_LAG, (k - PV_LAG) % 2)
            return None

        def early_turn(pe, t, dst):
            s = f[1]
            pe.wait_ge(A.zn, SUB * (NT + t.n + 1))
            for k in range(SUB):
                m = pe.transpose(dst[:, k * P:(k + 1) * P], XNF[:, t.n, k, :], ident)
            m.then_inc(s.tp, 1)

        def norm_hi(act, s, t, src, hi):
            after(act, s.tp, s.base + t.n + 1)
            act.activation(hi, src, ACT.Copy).then_inc(s.hi, 1)

        def norm_lo(v, s, t, src, hi, lo):
            after(v, s.hi, s.base + t.n + 1)
            v.tensor_tensor(lo, src, hi.bitcast(F32), ALU.subtract).then_inc(s.lo, 1)

        def run_slots(eng, slot):
            def step_b(t):
                for b in range(SPT):
                    slot(t, b)
            run_steps(eng, step_b)

        def live(t, b, back):
            return not isinstance(t.n, int) or 0 <= t.n * SPT + b - back < NSEQ

        def unit_at(t, b, k, lag):
            n, u = t.n * SPT + b, k - lag
            if u >= 0:
                return (n - 1, t.p if b == 1 else 1 - t.p, 1 - b, u) if live(t, b, 1) else None
            return (n - 2, 1 - t.p, b, u + UNITS) if live(t, b, 2) else None

        VAT = P - RG


        ffn_starts = ((A.done, NT), (B.done, NSEQ))

        def load_expert(sp, s, x, u):
            wload = (s.wload0, s.wload1)[u]
            after(sp, s.wl, x - 1)
            carry(sp)
            sp.dma_start(WS[:, u, 0, :], f_Wg[x]).then_inc(wload, 16)
            sp.dma_start(WS[:, u, 1, :], f_Wu[x]).then_inc(wload, 16)
            sp.dma_start(WS[:, u, 2, :].rearrange("p (k c) -> p k c", k=FC),
                         f_Wd[x].rearrange("(k p) c -> p k c", p=P)).then_inc(wload, 16)

        def first_hi(act, s, u):
            act.wait_ge((s.wload0, s.wload1)[u], 48)
            act.activation(WH[:, u, :, :], WS[:, u, :, :], ACT.Copy).then_inc(s.wh, 1)
            act.wait_ge(s.wh, u + 1)

        def split_lo(g, s, x, u):
            g.wait_ge(s.wh, x + 1)
            g.tensor_tensor(WL[:, u, :, :], WS[:, u, :, :], WH[:, u, :, :].bitcast(F32),
                            ALU.subtract).then_inc(s.wl, 1)

        @block.sync
        def _(sp):
            for i, w in enumerate((a_Wq, a_Wk, a_Wv, a_Wbeta, a_Wmix, a_Wout)):
                sp.dma_start(WRAW[0:w.shape[0], i, :], w).then_inc(ld.wa, 16)
            sp.dma_start(CST[:, 0:CB], consts[:, 0:CB]).then_inc(ld.tables_a, 16)
            sp.dma_start(X[:, 0, :, :], x_tok[:, 0]).then_inc(ld.x0, 16)
            row = lambda v: v.rearrange("(a n) -> a n", a=1)
            sp.dma_start(BAH[:, 0, :], a_bbeta.rearrange("(h m) -> h m", m=MA)).then_inc(ld.ba, 16)
            sp.dma_start(BAH[:, 1, :], a_bmix.rearrange("(h m) -> h m", m=MA)).then_inc(ld.ba, 16)
            sp.dma_start(BROW[:, 0:C], row(a_bout)).then_inc(ld.ba, 16)
            sp.dma_start(GB[:, 0, :], row(a_ln_g).broadcast_to([P, C])).then_inc(ld.ba, 16)
            sp.dma_start(GB[:, 1, :], row(a_ln_b).broadcast_to([P, C])).then_inc(ld.ba, 16)
            for n in range(1, NT):
                sp.dma_start(X[:, n, :, :], x_tok[:, n]).then_inc(ld.x1 if n == 1 else ld.x, 16)
            sp.dma_start(CST[:, CB:], consts[:, CB:]).then_inc(ld.tables_b, 16)
            sp.dma_start(BROW[:, C:2 * C], row(b_bo)).then_inc(ld.bb, 16)
            sp.dma_start(BROW[:, 2 * C:], row(b_bv)).then_inc(ld.bb, 16)
            sp.dma_start(WOB[:, :], b_Wo).then_inc(ld.bb, 16)
            sp.wait_ge(A.phi_k, NT)
            sp.wait_ge(A.phi_q, NT)
            load_expert(sp, f[0], 0, 0)
            load_expert(sp, f[0], 1, 1)
            sp.wait_ge(*ffn_starts[0])
            sp.dma_start(WQB[:, :], b_Wq).then_inc(ld.wb, 16)
            sp.dma_start(WKB[:, :], b_Wk).then_inc(ld.wb, 16)
            sp.dma_start(WVB[:, :], b_Wv).then_inc(ld.wb, 16)
            sp.dma_start(BRAW[:, 0:C], row(b_bq)).then_inc(ld.wb, 16)
            sp.dma_start(BRAW[:, C:], row(b_bk)).then_inc(ld.wb, 16)
            for s in f:
                if s is f[1]:
                    sp.wait_ge(f[0].wl, NE)
                    load_expert(sp, s, 0, 0)
                    load_expert(sp, s, 1, 1)
                with sp.Fori(1, NE // 2) as h:
                    load_expert(sp, s, 2 * h, 0)
                    load_expert(sp, s, 2 * h + 1, 1)
            for n in range(NT):
                sp.wait_ge(f[1].done, n + 1)
                sp.dma_start(o_tok[:, n], X[:, n, :, :]).then_inc(stored, 16)
            sp.wait_ge(stored, 16 * NT)

        def ffn_pool(g, i):
            s = f[i]
            g.wait_ge(*ffn_starts[i])
            if i == 1:
                early_rstd(g, LAST)

            def split(h, u):
                x = 2 * h + u
                g.wait_ge((s.wload0, s.wload1)[u], 48 * (h + 1))
                g.wait_ge(s.d, FC + FC * NT * (x - 1))
                carry(g)
                g.tensor_copy(WH[:, u, :, :], WS[:, u, :, :]).then_inc(s.wh, 1)
                split_lo(g, s, x, u)

            g.memset(YACC[:, :, :], 0.0).then_inc(s.zero, 1)
            split_lo(g, s, 1, 1)
            with g.Fori(1, NE // 2) as h:
                split(h, 0)
                split(h, 1)

        @block.gpsimd
        def _(g):
            g.memset(ONES[:, :], 1.0).then_inc(pr.ones, 1)
            g.memset(HALF[:, :], -0.5).then_inc(pr.ones, 1)
            def leave(old):
                after(g, A.zn, SUB * (old.n + 1))
                g.tensor_tensor(ZN[:, :, :], ZN[:, :, :], spread(GB[:, 0, :], SUB), ALU.mult).then_inc(A.zg, 1)
                after(g, A.zg, old.n + 1)
                g.tensor_tensor(ZN[:, :, :], ZN[:, :, :], spread(GB[:, 1, :], SUB), ALU.add).then_inc(A.zb, 1)
                after(g, A.zb, old.n + 1)
                g.tensor_tensor(X[:, old.n, :, :], X[:, old.n, :, :], ZN[:, :, :], ALU.add).then_inc(A.done, 1)

            def step(t):
                nxt, old = t + 1, t + -1
                if nxt.real():
                    norm_rstd(g, n_a, nxt)
                meanwhile(t, first_rstd, (0, 1, 2))
                if t.real():
                    for k, name in enumerate("kq"):
                        after(g, a_used[name], t.n + 1)
                        after(g, a_used[name + "s"], t.n + 1)
                        after(g, A.re_k if name == "k" else A.re_q, t.n)
                        after(g, A.phi_k if name == "k" else A.phi_q, t.n)
                        g.tensor_tensor(U[:, k, :], R1[:, k, :], R2[:, k, :],
                                        ALU.add).then_inc(A.u_k if name == "k" else A.u_q, 1)
                    after(g, a_used["b0"], t.n + 1)
                    after(g, a_used["b1"], t.n + 1)
                    carry(g)
                    g.tensor_scalar(TB[:, :, :], TB[:, :, :], 2 * BMAX - 1, 2 * BMIN - 1,
                                    ALU.min, ALU.max).then_inc(A.clip, 1)
                    after(g, A.clip, t.n + 1)
                    after(g, A.scan, 2 * 5 * t.n)
                    carry(g)
                    g.tensor_scalar(BETA[:, :, :], TB[:, :, :], 0.5, 0.5, ALU.mult, ALU.add).then_inc(A.scaled, 1)
                    after(g, A.scaled, t.n + 1)
                    carry(g)
                    g.memset(BETA[:, :, 0::SEQ], 0.0).then_inc(A.beta, 1)
                older = t + -2
                if older.real():
                    leave(older)
                if not t.real() and t.n == NT:
                    split_lo(g, f[0], 0, 0)
                if old.real():
                    after(g, A.ay, 2 * (old.n + 1))
                    after(g, A.z, old.n)
                    g.tensor_tensor(Y[:, old.p, :], AY[:, 0, :], AY[:, 1, :], ALU.add).then_inc(A.y, 1)
                meanwhile(t, first_rstd, (3,))
                if t.real():
                    after(g, A.scan, 2 * 5 * (t.n + 1))
                    after(g, A.phi_q, t.n + 1)
                    g.tensor_tensor(S[:, 1, :, :], S[:, 1, :, :], spread(PQ[:, t.p, :], 5),
                                    ALU.mult).then_inc(A.prod1, 1)
                if old.real():
                    after(g, A.mv2, SUB * (old.n + 1))
                    after(g, A.rstd2, old.n)
                    carry(g)
                    g.tensor_scalar(VE2[:, :], MV2[:, :, 1], LN_EPS, None, ALU.add).then_inc(A.ve2, 1)
                    after(g, A.ve2, old.n + 1)
                    after(g, A.zn, SUB * old.n)
                    g.tensor_tensor(RSTD2[:, :], VE2[:, :], HALF[:, :], ALU.pow).then_inc(A.rstd2, 1)
                meanwhile(t, first_rstd, (4, 5))

            def first_rstd(t):
                norm_rstd(g, f[0], t)

            g.wait_ge(ld.ba, 80)
            run_steps(g, step)
            leave(LAST)
            for n in (6, 7):
                first_rstd(Tile(n, n % 2))
            ffn_pool(g, 0)

            g.wait_ge(ld.wb, 80)
            hd = lambda k: WB[:, k, :].rearrange("p (h d) -> p h d", d=DB)
            wq = WQB[:, :].rearrange("p (h d) -> p h d", d=DB)
            half = DB // 2
            g.tensor_copy(WB[:, 0, :], WQB[:, :]).then_inc(pr.wb, 1)
            g.tensor_copy(hd(1)[:, :, 0:half], wq[:, :, half:DB]).then_inc(pr.wb, 1)
            g.tensor_copy(hd(1)[:, :, half:DB], wq[:, :, 0:half]).then_inc(pr.wb, 1)
            g.tensor_copy(hd(2), spread(WKB[:, :], HB)).then_inc(pr.wb, 1)
            g.tensor_copy(hd(3)[:, :, 0:half], spread(WKB[:, half:DB], HB)).then_inc(pr.wb, 1)
            g.tensor_copy(hd(3)[:, :, half:DB], spread(WKB[:, 0:half], HB)).then_inc(pr.wb, 1)
            g.wait_ge(pr.wb, 6)
            g.tensor_copy(WBH[:, :, :], WB[:, :, :]).then_inc(pr.wb, 1)
            g.tensor_copy(WVH[:, :], WVB[:, :]).then_inc(pr.wb, 1)
            g.wait_ge(pr.wb, 8)
            g.tensor_tensor(WBL[:, :, :], WB[:, :, :], WBH[:, :, :].bitcast(F32), ALU.subtract).then_inc(pr.wb, 1)
            g.tensor_tensor(WVL[:, :], WVB[:, :], WVH[:, :].bitcast(F32), ALU.subtract).then_inc(pr.wb, 1)
            g.wait_ge(ld.tables_b, 16)
            for j in range(NJ):
                g.tensor_copy(SELR[:, j, :], cst(f"qhi_{j}")).then_inc(pr.selr, 1)
                g.tensor_copy(SELR[:, NJ + j, :], cst(f"qlo_{j}")).then_inc(pr.selr, 1)
            for k, name in enumerate(("khi", "klo", "kone", "ident")):
                g.tensor_copy(SELR[:, 2 * NJ + k, :], cst(name)).then_inc(pr.selr, 1)
            for k, name in enumerate(("mask_rows", "mask_cols", "ident")):
                g.tensor_copy(MASKB[:, k, :], cst(name)).then_inc(pr.selr, 1)
            g.tensor_copy(ONESR[:, 0:P], ONES[0:1, :]).then_inc(pr.selr, 1)
            for k in range(1, SUB):
                g.tensor_copy(ONESR[:, k * P:(k + 1) * P], ONES[0:1, :]).then_inc(pr.selr, 1)

            g.wait_ge(ld.bb, 48)
            br = lambda k: BQKR[:, k, :].rearrange("p (h d) -> p h d", d=DB)
            bq = BRAW[:, 0:C].rearrange("p (h d) -> p h d", d=DB)
            g.tensor_copy(BQKR[:, 0, :], BRAW[:, 0:C]).then_inc(pr.bqkr, 1)
            g.tensor_copy(br(1)[:, :, 0:half], bq[:, :, half:DB]).then_inc(pr.bqkr, 1)
            g.tensor_copy(br(1)[:, :, half:DB], bq[:, :, 0:half]).then_inc(pr.bqkr, 1)
            g.tensor_copy(br(2), spread(BRAW[:, C:], HB)).then_inc(pr.bqkr, 1)
            g.tensor_copy(br(3)[:, :, 0:half], spread(BRAW[:, C + half:], HB)).then_inc(pr.bqkr, 1)
            g.tensor_copy(br(3)[:, :, half:DB], spread(BRAW[:, C:C + half], HB)).then_inc(pr.bqkr, 1)

            norm_rstd(g, n_b, Tile(0, 0))
            g.wait_ge(f[0].done, NT)

            def slot(t, b):
                nxt = t + 1
                for k in range(UNITS):
                    unit = unit_at(t, b, k, T_LAG)
                    if unit:
                        o, _, _, u = unit
                        q = UNITS * o + u
                        after(g, B.t_used, 2 * (q + 1))
                        after(g, B.pv, q - RING + 1)
                        g.tensor_tensor(PL[:, u % RING, :], PT[:, u % RING, :], PH[:, u % RING, :].bitcast(F32),
                                        ALU.subtract).then_inc(B.pl, 1)
                    if (t + 2).real() and (b, k) == (1, 11):
                        norm_rstd(g, n_b, t + 2)
                    if (t + -2).real() and (b, k) == (0, 5):
                        early_rstd(g, t + -2)
                    if isinstance(t.n, int) and (t.n, b, k) == (NT, 1, 4):
                        g.wait_ge(B.pv, UNITS * NSEQ)
                        split_lo(g, f[1], 0, 0)
                    if nxt.real() and (b, k) in ((0, 9), (1, 1)):
                        i, name = (0, "q") if b == 0 else (1, "k")
                        after(g, b_used[name], nxt.n + 1)
                        after(g, b_used[name + "s"], nxt.n + 1)
                        after(g, B.hi, 2 * nxt.n)
                        after(g, B.lo, 2 * nxt.n)
                        g.tensor_tensor(QK[:, i, :], B1[:, i, :], B2[:, i, :],
                                        ALU.add).then_inc(B.u_q if i == 0 else B.u_k, 1)
            run_slots(g, slot)
            ffn_pool(g, 1)

        def ffn_act(act, i):
            s = f[i]
            act.wait_ge(*ffn_starts[i])
            if i == 1:
                norm_hi(act, s, LAST, bank[6 + LAST.p], XTH[:, LAST.n, :])
            act.sem_inc(s.sil, 2)

            def hi(m, k):
                act.wait_ge(s.mul, m * FC + k + 3)
                act.activation(HH[:, k, :], HF[:, k, :], ACT.Copy).then_inc(s.hh, 1)

            def tile(m):
                for k in range(FC):
                    act.wait_ge(s.gate, m * FC + k + 1)
                    act.wait_ge(s.mul, m * FC + k + 1)
                    act.activation(SG[:, k % 2, :], bank[k % 2], ACT.Silu).then_inc(s.sil, 1)
                    if k >= 1:
                        hi(m, k - 1)
                hi(m, FC - 1)

            with act.Fori(0, (NE - 1) * NT // 2) as h:
                tile(2 * h)
                tile(2 * h + 1)

            def stage(t):
                after(act, s.acc, 2 + NT * (NE - 1) + t.n + 1)
                after(act, s.back, t.n - 1)
                act.activation(YS[:, t.p, :], YACC[:, t.n, :], ACT.Copy).then_inc(s.ys, 1)

            def last(t):
                tile((NE - 1) * NT + t.n)
                if (t + -1).real():
                    stage(t + -1)
            quads(act, last)
            stage(LAST)

        @block.scalar
        def _(act):
            for k in range(6):
                w = P if k in (0, 1, 2, 5) else HA * MA
                act.wait_ge(pr.wt, k + 1)
                act.activation(WT[:, k, 0:w], bank[k][:, 0:w], ACT.Copy).then_inc(pr.wtc, 1)
            act.wait_ge(pr.ba, 1)
            act.activation(BA[:, :, :], bank[6][:, 0:2 * MA].rearrange("p (a m) -> p a m", a=2), ACT.Copy,
                           scale=0.5).then_inc(pr.ba, 1)

            def step(t):
                nxt, old = t + 1, t + -1
                if t.real():
                    for k, name in enumerate("kq"):
                        u, ex, re, phi = ((A.u_k, A.ex_k, A.re_k, A.phi_k), (A.u_q, A.ex_q, A.re_q, A.phi_q))[k]
                        act.wait_ge(u, t.n + 1)
                        after(act, phi, t.n)
                        act.activation(EX[:, k, :], U[:, k, :], ACT.Exp).then_inc(ex, 1)
                        act.wait_ge(ex, t.n + 1)
                        act.activation(U[:, k, :], U[:, k, :], ACT.Relu).then_inc(re, 1)
                    for m in range(MA):
                        act.wait_ge(a_ready[f"b{m}"], t.n + 1)
                        after(act, A.scaled, t.n)
                        act.activation(TB[:, m, :], bank[PBANK[f"b{m}"]], ACT.Tanh, bias=BA[:, 0, m:m + 1],
                                       scale=0.5).then_inc(a_used[f"b{m}"], 1)
                    act.wait_ge(a_ready["mx"], t.n + 1)
                    after(act, A.wgt, t.n - 1)
                    act.activation(MIX[:, t.p, :], bank[PBANK["mx"]][:, 0:SEQ], ACT.Tanh, bias=BMIXD[:, 1:2],
                                   scale=0.5).then_inc(a_used["mx"], 1)
                meanwhile(t, lambda w: first_hi(act, f[0], w.n), (0,))
                meanwhile(t, first_norm, (0, 1))
                meanwhile(t, lambda w: first_hi(act, f[0], w.n), (1,))
                if old.real():
                    for m in range(MA):
                        act.wait_ge(A.rep, 2 * old.n + m + 1)
                        after(act, A.ay, 2 * old.n)
                        act.activation(RS[:, m, :], bank[7], ACT.Copy).then_inc(A.rs, 1)
                meanwhile(t, first_norm, range(2, NT))
                if nxt.real():
                    after(act, a_ready["v3"], nxt.n - 1)
                    norm_hi(act, n_a, nxt, bank[0], XH[:, nxt.p, :])

            def first_norm(t):
                norm_hi(act, f[0], t, bank[t.p], XTH[:, t.n, :])

            act.wait_ge(pr.bmix, 2)
            run_steps(act, step)
            ffn_act(act, 0)

            def prepare(nxt, b, k):
                if (b, k) == (0, 4):
                    after(act, B.v_ready, nxt.n - 1)
                    norm_hi(act, n_b, nxt, bank[6], XH[:, nxt.p, :])
                if (b, k) in ((1, 0), (1, 4)):
                    i = k // 4
                    act.wait_ge((B.u_q, B.u_k)[i], nxt.n + 1)
                    after(act, B.kst_ready, nxt.n)
                    act.activation(QKH[:, i, :], QK[:, i, :], ACT.Copy).then_inc(B.hi, 1)
                if b == 1 and 5 <= k < 5 + NJ:
                    j = k - 5
                    act.wait_ge(B.st_ready, NJ * nxt.n + j + 1)
                    after(act, B.q2_ready, 4 * (nxt.n - 1))
                    after(act, B.row_ready, 2 * UNITS * (nxt.n - 1))
                    act.activation(QST[:, nxt.p, j, :], bank[6], ACT.Copy).then_inc(B.st_used, 1)
                if (b, k) == (1, 10):
                    act.wait_ge(B.kst_ready, nxt.n + 1)
                    after(act, B.t_ready, 2 * UNITS * (nxt.n - 1))
                    act.activation(KST[:, nxt.p, :], bank[6], ACT.Copy).then_inc(B.kst_used, 1)

            def slot(t, b):
                nxt = t + 1
                n = t.n * SPT + b
                for k in range(UNITS):
                    if k == T_LAG - 1 and live(t, b, 1):
                        o, ob = n - 1, 1 - b
                        for h in range(2):
                            act.wait_ge(B.q2_ready, 2 * o + h + 1)
                            after(act, B.t_ready, UNITS * (o - 1))
                            act.activation(Q2[:, ob, 2 * h:2 * h + 2, :],
                                           r3(bank[6 + h], 2), ACT.Copy).then_inc(B.q2_used, 1)
                    if k == PV_LAG and live(t, b, 2):
                        for z in range(2):
                            act.wait_ge(B.pv, UNITS * (n - 1))
                            after(act, B.turn, 2 * (n - 3))
                            act.activation(OS[:, b, z, :], bank[4 + z], ACT.Copy).then_inc(B.os, 1)
                    early = early_tile(t, b, k)
                    if early:
                        norm_hi(act, f[1], early, bank[early.p], XTH[:, early.n, :])
                    if k == OUT_STEP + 4 and live(t, b, 2):
                        act.wait_ge(B.ot, n - 1)
                        after(act, B.out, n - 3)
                        act.activation(OT[:, b, :], bank[7][:, 0:2 * C], ACT.Copy).then_inc(B.otc, 1)
                    if isinstance(t.n, int) and (t.n, b, k) == (NT, 1, 3):
                        act.wait_ge(B.t_ready, UNITS * NSEQ)
                        act.wait_ge(B.q2_ready, 2 * NSEQ)
                        first_hi(act, f[1], 0)
                        first_hi(act, f[1], 1)
                    if nxt.real():
                        prepare(nxt, b, k)
                    unit = unit_at(t, b, k, T_LAG)
                    if unit:
                        o, _, _, u = unit
                        q = UNITS * o + u
                        for dst in (PH, PT):
                            act.wait_ge(B.t_ready, q + 1)
                            after(act, B.pv, q - RING + 1)
                            after(act, B.pl, q - RING + 1)
                            act.activation(dst[:, u % RING, :], bank[2 + u % 2], ACT.Exp,
                                           scale=DB ** -0.5).then_inc(B.t_used, 1)

            act.wait_ge(f[0].d, FC + FC * NT * NE)
            for dst in [NMP[:, i, :, :, :].rearrange("p a j r -> p (a j r)") for i in range(2)] + \
                       [VS[:, i, :, :].rearrange("p s r -> p (s r)") for i in range(2)]:
                act.activation(dst, CST[:, 0:dst.shape[1]], ACT.Copy, scale=0.0).then_inc(pr.zero, 1)
            act.wait_ge(pr.zero, 4)
            for i in range(2):
                act.activation(VS[:, i, :, VAT + DB], ONES[:, 0:SUB], ACT.Copy).then_inc(pr.zero, 1)
            act.wait_ge(f[0].done, NT)
            act.wait_ge(pr.bqk, 1)
            act.activation(BQK[:, :], bank[7][:, 0:4], ACT.Copy).then_inc(pr.bqk, 1)
            run_slots(act, slot)
            ffn_act(act, 1)

        def ffn_pe(pe, i):
            s = f[i]
            pe.wait_ge(*ffn_starts[i])

            if i == 1:
                early_turn(pe, LAST, bank[6 + LAST.p])
            pe.sem_inc(s.d, FC)

            def gate_up(m, t, u, k):
                cols = slice(k * P, (k + 1) * P)
                pe.wait_ge(s.sil, m * FC + k + 1)
                split_product(pe, bank[k % 2], WH[:, u, 0, cols], WL[:, u, 0, cols],
                              XTH[:, t, :], XTL[:, t, :]).then_inc(s.gate, 1)
                pe.wait_ge(s.mul, m * FC + k + 1)
                split_product(pe, bank[2 + k % 2], WH[:, u, 1, cols], WL[:, u, 1, cols],
                              XTH[:, t, :], XTL[:, t, :]).then_inc(s.up, 1)

            def down(m, u, p, k):
                cols = slice(k * P, (k + 1) * P)
                if k == 0:
                    pe.wait_ge(s.acc, m + 1)
                pe.wait_ge(s.hl, m * FC + k + 1)
                split_product(pe, bank[4 + p], WH[:, u, 2, cols], WL[:, u, 2, cols], HH[:, k, :], HL[:, k, :],
                              start=(k == 0), stop=(k == FC - 1)).then_inc(s.d, 1)

            def tile(m, t, u, p, before):
                gate_up(m, t, u, 0)
                if before is not None:
                    down(m - 1, before, 1 - p, 2)
                gate_up(m, t, u, 1)
                if before is not None:
                    down(m - 1, before, 1 - p, 3)
                gate_up(m, t, u, 2)
                down(m, u, p, 0)
                gate_up(m, t, u, 3)
                down(m, u, p, 1)

            def back(t):
                after(pe, s.ys, t.n + 1)
                after(pe, s.done, t.n - 1)
                for k in range(SUB):
                    m = pe.transpose(bank[6 + t.p][:, k * P:(k + 1) * P], YS[:, t.p, k * P:(k + 1) * P], ident)
                m.then_inc(s.back, 1)

            def expert(e, u, before):
                first = (2 * e + u) * NT
                pe.wait_ge(s.wl, 2 * e + u + 1)
                tile(first, 0, u, 0, before)
                tile(first + 1, 1, u, 1, u)
                with pe.Fori(1, NT // 2) as h:
                    tile(first + 2 * h, 2 * h, u, 0, u)
                    tile(first + 2 * h + 1, 2 * h + 1, u, 1, u)

            pe.wait_ge(s.lo, s.base + NT)
            expert(0, 0, None)
            expert(0, 1, 0)
            with pe.Fori(1, NE // 2 - 1) as e:
                expert(e, 0, 1)
                expert(e, 1, 0)
            expert(NE // 2 - 1, 0, 1)
            pe.wait_ge(s.wl, NE)

            def last(t):
                tile((NE - 1) * NT + t.n, t.n, 1, t.p, 0 if isinstance(t.n, int) and t.n == 0 else 1)
                if (t + -2).real():
                    back(t + -2)
            quads(pe, last)
            down(NE * NT - 1, 1, 1, 2)
            down(NE * NT - 1, 1, 1, 3)
            back(LAST + -1)
            back(LAST)

        @block.tensor
        def _(pe):
            pe.wait_ge(ld.tables_a, 16)
            pe.wait_ge(ld.wa, 96)
            for k in range(6):
                w = P if k in (0, 1, 2, 5) else HA * MA
                src = WRAW[0:w, k, :]
                if k == 5:
                    pe.wait_ge(pr.wout, 1)
                    src = LA[:, 0, :]
                pe.transpose(bank[k][:, 0:w], src, ident[0:w, 0:w]).then_inc(pr.wt, 1)

            def project(t, names, last_use):
                for name in names:
                    bk = bank[PBANK[name]]
                    prev, back = last_use[name]
                    after(pe, a_used[prev], t.n + 1 - back)
                    if name == "mx":
                        for b in range(SPT):
                            cols = slice(b * SEQ, (b + 1) * SEQ)
                            m = split_product(pe, bk[:, 0:SEQ], LAH[:, 10 + b, :], LAL[:, 10 + b, :],
                                              XH[:, t.p, cols], XL[:, t.p, cols], start=(b == 0), stop=(b == SPT - 1))
                    else:
                        k = {"k": 0, "ks": 1, "q": 2, "qs": 3, "v0": 4, "v1": 5, "v2": 6, "v3": 7, "b0": 8, "b1": 9}[name]
                        m = split_product(pe, bk, LAH[:, k, :], LAL[:, k, :], XH[:, t.p, :], XL[:, t.p, :])
                    m.then_inc(a_ready[name], 1)

            last_use = {n: (PROJ[i - 3], 0) for i, n in enumerate(PROJ) if i >= 3}
            for n in PROJ[:3]:
                last_use[n] = ([x for x in PROJ if PBANK[x] == PBANK[n]][-1], 1)

            def numerator(old, m):
                after(pe, A.ay, 2 * old.n)
                pe.wait_ge((A.prod0, A.prod1)[m], old.n + 1)
                for c in range(DA):
                    x = pe.matmul(bank[5 + m], cst(f"sum_{c}"), S[:, m, c, :], start=(c == 0), stop=(c == DA - 1))
                x.then_inc(A.num, 1)

            def denominators(old):
                pe.wait_ge(A.prod0, old.n + 1)
                pe.wait_ge(A.prod1, old.n + 1)
                after(pe, A.zsum, old.n)
                for b in range(SPT):
                    for m in range(MA):
                        x = pe.matmul(bank[4][:, 0:SEQ], cst(f"sum_{2 * b + m}"), S[:, m, 4, b * SEQ:(b + 1) * SEQ],
                                      start=(b + m == 0), stop=(b + m == 2))
                x.then_inc(A.den, 1)

            def weights(old, m):
                pe.wait_ge(A.wgt, old.n + 1)
                after(pe, A.rs, 2 * old.n + m)
                for b in range(SPT):
                    x = pe.matmul(bank[7][:, b * SEQ:(b + 1) * SEQ], cst(f"rep_{2 * b + m}"), WGT[:, :],
                                  start=True, stop=True)
                x.then_inc(A.rep, 1)

            def first_turn(t):
                first_norm_turn(pe, t)

            def step(t):
                nxt, old = t + 1, t + -1
                if t.real():
                    pe.wait_ge(n_a.lo, t.n + 1)
                    project(t, PROJ[:5], last_use)
                if old.real():
                    denominators(old)
                meanwhile(t, first_turn, (0, 1))
                if not t.real() and old.real():
                    numerator(old, 1)
                if t.real():
                    project(t, PROJ[5:10], last_use)
                if old.real():
                    weights(old, 0)
                if t.real():
                    project(t, PROJ[10:], last_use)
                if old.real():
                    weights(old, 1)
                    if t.real():
                        numerator(old, 1)
                    pe.wait_ge(A.y, old.n + 1)
                    for k in range(SUB):
                        cols = slice(k * P, (k + 1) * P)
                        pe.matmul(bank[4][:, cols], Y[:, old.p, cols], WOUT[:, :], start=True, stop=False)
                        x = pe.matmul(bank[4][:, cols], ONES[0:1, :], BROW[:, 0:C], start=False, stop=True)
                    x.then_inc(A.z, 1)
                meanwhile(t, first_turn, range(2, NT))
                if t.real():
                    numerator(t, 0)
                if nxt.real():
                    after(pe, n_a.lo, nxt.n)
                    norm_turn(pe, n_a, nxt, bank[0])

            pe.wait_ge(ld.ba, 80)
            pe.matmul(bank[6][:, 0:2 * MA], cst("rep_0")[0:HA, :], BAH[:, :, :].rearrange("h a m -> h (a m)"),
                      start=True, stop=True).then_inc(pr.ba, 1)
            pe.wait_ge(pr.la, 19)
            pe.wait_ge(pr.wout, 2)
            pe.wait_ge(pr.ones, 2)
            pe.wait_ge(pr.ba, 2)
            run_steps(pe, step)
            ffn_pe(pe, 0)

            SQ, SL, SK, SKL, SKONE, SID = 0, NJ, 2 * NJ, 2 * NJ + 1, 2 * NJ + 2, 2 * NJ + 3

            def rows(t, b, k):
                n = t.n * SPT + b
                g, half = (k, None) if k < NG else ((k - NG) // 2, (k - NG) % 2)
                q = QST[g * RG:(g + 1) * RG, t.p, :, b * SEQ:(b + 1) * SEQ]
                ks = KST[g * RG:(g + 1) * RG, t.p, b * SEQ:(b + 1) * SEQ]
                bk = bank[k % 2]
                after(pe, B.row_used, 12 * n + k - 1)
                if k < NG:
                    for j in range(NJ):
                        pe.matmul(bk[:, j * P:(j + 1) * P], q[:, j, 0:P], ks[:, 0:P], start=(j == 0), stop=False,
                                  skip_group_check=True)
                    m = pe.matmul(r3(bk, NJ), MASKB[:, 2, :], spread(MASKB[:, 0, :], NJ), start=False, stop=True,
                                  skip_group_check=True)
                else:
                    for j in range(2):
                        pe.matmul(bk[:, j * SEQ:(j + 1) * SEQ], q[:, 2 * half + j, P:SEQ], ks, start=(j == 0),
                                  stop=False, skip_group_check=True)
                    m = pe.matmul(r3(bk, 2)[:, :, P:SEQ], MASKB[:, 2, :], spread(MASKB[:, 0, :], 2), start=False,
                                  stop=True, skip_group_check=True)
                m.then_inc(B.row_ready, 1)

            def cols(o, p, ob, u):
                g = u // 2 if u < 8 else u - 8
                rg = slice(g * RG, (g + 1) * RG)
                bk = bank[2 + u % 2]
                after(pe, B.t_used, 2 * (UNITS * o + u - 1))
                if u < 8:
                    pe.matmul(bk, KST[rg, p, ob * SEQ:ob * SEQ + P], Q2[rg, ob, 2 * (u % 2):2 * (u % 2) + 2, :],
                              start=True, stop=False, skip_group_check=True)
                    m = pe.matmul(r3(bk, 2)[:, :, 0:P], MASKB[:, 2, :], spread(MASKB[:, 1, :], 2), start=False,
                                  stop=True, skip_group_check=True)
                else:
                    pe.matmul(bk, KST[rg, p, ob * SEQ + P:(ob + 1) * SEQ], Q2[rg, ob, :, P:SEQ], start=True,
                              stop=False, skip_group_check=True)
                    m = pe.matmul(r3(bk, NJ), MASKB[:, 2, :], spread(MASKB[:, 1, :], NJ), start=False, stop=True,
                                  skip_group_check=True)
                m.then_inc(B.t_ready, 1)

            def values(o, p, ob, u):
                if u < 2:
                    after(pe, B.os, 2 * o - 1 + u)
                pe.wait_ge(B.pl, UNITS * o + u + 1)
                at = VAT - RG * (u // 2 if u < 8 else u - 8)
                for i in range(2):
                    x = (PH, PL)[i][:, u % RING, :]
                    if u < 8:
                        m = pe.matmul(bank[4 + u % 2], VS[:, p, 2 * ob, at:at + P], x, start=(u < 2 and i == 0),
                                      stop=False, skip_group_check=True)
                    else:
                        for z in range(2):
                            m = pe.matmul(r3(bank[4 + z], 2)[:, :, P:SEQ], VS[:, p, 2 * ob + 1, at:at + P],
                                          r3(x, NJ)[:, 2 * z:2 * z + 2, :], start=False, stop=(u == UNITS - 1),
                                          skip_group_check=True)
                m.then_inc(B.pv, 1)

            def turn_sums(o, ob, a, more):
                if a == 0:
                    pe.wait_ge(B.os, 2 * (o + 1))
                    after(pe, B.done, o)
                    if more:
                        pe.wait_ge(B.q2_used, 2 * (o + 2))
                else:
                    pe.wait_ge(B.oc, 4 * o + 2)
                    pe.wait_ge(B.ro, 2 * o + 1)
                for j in range(NJ):
                    at = (j % 2) * SEQ + a * P
                    m = pe.transpose(bank[7][:, j * P:(j + 1) * P], OS[:, ob, j // 2, at:at + P], ident)
                m.then_inc(B.turn, 1)

            def turn_out(o, ob):
                pe.wait_ge(B.o, o + 1)
                for a in range(2):
                    m = pe.transpose(bank[7][:, a * P:(a + 1) * P], OB[:, ob, a, :], ident)
                m.then_inc(B.ot, 1)

            def project_out(o, ob):
                pe.wait_ge(B.otc, o + 1)
                for a in range(2):
                    dst = bank[7][:, a * P:(a + 1) * P]
                    pe.matmul(dst, OT[:, ob, a * P:(a + 1) * P], WOB[:, :], start=True, stop=False)
                    m = pe.matmul(dst, ONES[0:1, :], BROW[:, C:2 * C], start=False, stop=True)
                m.then_inc(B.out, 1)

            def stack2(o, p, ob, h):
                pe.wait_ge(B.nml, 2 * (o + 1))
                for x in range(2):
                    j = 2 * h + x
                    dst = bank[6 + h][:, x * SEQ:(x + 1) * SEQ]
                    pe.matmul(dst, SELR[:, SID, :], QST[:, p, j, ob * SEQ:(ob + 1) * SEQ], start=True, stop=False)
                    for a in range(2):
                        m = pe.matmul(dst[:, a * P:(a + 1) * P], NMP[:, ob, a, j, :], SELR[:, SID, :],
                                      start=False, stop=(a == 1))
                m.then_inc(B.q2_ready, 1)

            def project_b(nxt, i):
                pe.wait_ge(n_b.lo, n_b.base + nxt.n + 1)
                if i:
                    pe.wait_ge(b_used[BPROJ[i - 1]], nxt.n + 1)
                split_product(pe, bank[6], WBH[:, i, :], WBL[:, i, :], XH[:, nxt.p, :],
                              XL[:, nxt.p, :]).then_inc(b_ready[BPROJ[i]], 1)

            def project_v(nxt, subs):
                pe.wait_ge(b_used[BPROJ[-1]], nxt.n + 1)
                for k in subs:
                    dst = bank[6][:, k * DB:(k + 1) * DB]
                    c = slice(k * P, (k + 1) * P)
                    pe.matmul(dst, XH[:, nxt.p, c], WVH[:, :], start=True, stop=False)
                    pe.matmul(dst, XH[:, nxt.p, c], WVL[:, :], start=False, stop=False)
                    pe.matmul(dst, XL[:, nxt.p, c], WVH[:, :], start=False, stop=False)
                    m = pe.matmul(dst, ONES[0:1, :], BROW[:, 2 * C:], start=False, stop=True)
                if SUB - 1 in subs:
                    m.then_inc(B.v_ready, 1)

            def query_stack(nxt, j):
                pe.wait_ge(B.v_used, nxt.n + 1) if j == 0 else pe.wait_ge(B.st_used, NJ * nxt.n + j)
                pe.wait_ge(B.lo, 2 * nxt.n + 1)
                pe.matmul(bank[6], SELR[:, SQ + j, :], QKH[:, 0, :], start=True, stop=False)
                pe.matmul(bank[6], SELR[:, SL + j, :], QKL[:, 0, :], start=False, stop=True).then_inc(B.st_ready, 1)

            def key_stack(nxt):
                pe.wait_ge(B.st_used, NJ * (nxt.n + 1))
                pe.wait_ge(B.lo, 2 * (nxt.n + 1))
                pe.matmul(bank[6], SELR[:, SK, :], QKH[:, 1, :], start=True, stop=False)
                pe.matmul(bank[6], SELR[:, SKL, :], QKL[:, 1, :], start=False, stop=False)
                pe.matmul(bank[6], SELR[0:1, SKONE, :], ONESR[:, :], start=False, stop=True).then_inc(B.kst_ready, 1)

            def slot(t, b):
                nxt = t + 1
                n = t.n * SPT + b
                has1, has2 = live(t, b, 1), live(t, b, 2)
                for k in range(UNITS):
                    if t.real():
                        if (b, k) == (0, 0):
                            pe.wait_ge(B.kst_used, t.n + 1)
                            pe.wait_ge(B.st_used, NJ * (t.n + 1))
                        rows(t, b, k)
                    unit = unit_at(t, b, k, T_LAG)
                    if unit:
                        if k == T_LAG:
                            pe.wait_ge(B.q2_used, 2 * n)
                        cols(*unit)
                    if k == T_LAG - 1 and has1:
                        op = t.p if b == 1 else 1 - t.p
                        if b == 0 and t.real():
                            pe.wait_ge(B.kst_used, t.n + 1)
                        if b == 1 and nxt.real():
                            pe.wait_ge(b_used[BPROJ[-1]], nxt.n + 1)
                        stack2(n - 1, op, 1 - b, 0)
                        after(pe, B.done, n - 2)
                        stack2(n - 1, op, 1 - b, 1)
                    if nxt.real():
                        if k == 3 and has1:
                            pe.wait_ge(B.q2_used, 2 * n - 1)
                        if (b, k) == (0, 3):
                            if t.real():
                                pe.wait_ge(B.kst_used, t.n + 1)
                            norm_turn(pe, n_b, nxt, bank[6])
                        if b == 0 and k >= 5 and k % 2 == 1:
                            project_b(nxt, (k - 5) // 2)
                        if b == 1 and k in (3, 4):
                            project_v(nxt, range(2 * (k - 3), 2 * (k - 2)))
                        if b == 1 and 5 <= k < 5 + NJ:
                            query_stack(nxt, k - 5)
                        if (b, k) == (1, 10):
                            key_stack(nxt)
                    early = early_tile(t, b, k)
                    if early:
                        pe.wait_ge(B.row_used, UNITS * NSEQ)
                        after(pe, f[1].lo, f[1].base + early.n - 1 if early.n >= 2 else 0)
                        early_turn(pe, early, bank[early.p])
                    unit = unit_at(t, b, k, PV_LAG)
                    if unit:
                        values(*unit)
                    if has2:
                        if k == OUT_STEP:
                            turn_sums(n - 2, b, 0, has1)
                        if k == OUT_STEP + 1:
                            turn_sums(n - 2, b, 1, has1)
                        if k == OUT_STEP + 3:
                            turn_out(n - 2, b)
                        if k == OUT_STEP + 5:
                            project_out(n - 2, b)

            pe.wait_ge(f[0].done, NT)
            pe.wait_ge(pr.bqkr, 6)
            for k in range(4):
                m = pe.matmul(bank[7][:, k:k + 1], BQKR[0:1, k, :], ONES[0:1, 0:1], start=True, stop=True)
            m.then_inc(pr.bqk, 1)
            pe.wait_ge(pr.bqk, 2)
            pe.wait_ge(pr.selr, 2 * NJ + 4 + 3 + SUB)
            pe.wait_ge(pr.wb, 10)
            pe.wait_ge(pr.zero, 6)
            run_slots(pe, slot)
            ffn_pe(pe, 1)

        def ffn_dve(v, i):
            s = f[i]
            v.wait_ge(*ffn_starts[i])

            if i == 1:
                early_stats(v, LAST)
                early_apply(v, LAST)
                norm_lo(v, s, LAST, bank[6 + LAST.p], XTH[:, LAST.n, :], XTL[:, LAST.n, :])
            v.sem_inc(s.mul, 2)
            v.sem_inc(s.acc, 2)
            v.wait_ge(s.zero, 1)

            def mul(m, k):
                v.wait_ge(s.up, m * FC + k + 1)
                v.wait_ge(s.sil, m * FC + k + 3)
                v.wait_ge(s.d, m * FC + k + 1)
                v.tensor_tensor(HF[:, k, :], SG[:, k % 2, :], bank[2 + k % 2], ALU.mult).then_inc(s.mul, 1)

            def lo(m, k):
                v.wait_ge(s.hh, m * FC + k + 1)
                v.tensor_tensor(HL[:, k, :], HF[:, k, :], HH[:, k, :].bitcast(F32), ALU.subtract).then_inc(s.hl, 1)

            def add(m, t, p):
                v.wait_ge(s.d, (m + 2) * FC)
                v.tensor_tensor(YACC[:, t, :], YACC[:, t, :], bank[4 + p], ALU.add).then_inc(s.acc, 1)

            def tile(m, p, before):
                mul(m, 0)
                mul(m, 1)
                lo(m, 0)
                if before is not None:
                    add(m - 1, before, 1 - p)
                mul(m, 2)
                lo(m, 1)
                mul(m, 3)
                lo(m, 2)
                lo(m, 3)

            def residual(t):
                after(v, s.back, t.n + 1)
                v.tensor_tensor(X[:, t.n, :, :], X[:, t.n, :, :], by_sub(bank[6 + t.p]), ALU.add).then_inc(s.done, 1)

            def expert(e, u, before):
                first = (2 * e + u) * NT
                tile(first, 0, before)
                tile(first + 1, 1, 0)
                with v.Fori(1, NT // 2) as h:
                    tile(first + 2 * h, 0, 2 * h - 1)
                    tile(first + 2 * h + 1, 1, 2 * h)

            expert(0, 0, None)
            expert(0, 1, NT - 1)
            with v.Fori(1, NE // 2 - 1) as e:
                expert(e, 0, NT - 1)
                expert(e, 1, NT - 1)
            expert(NE // 2 - 1, 0, NT - 1)

            def last(t):
                tile((NE - 1) * NT + t.n, t.p, NT - 1 if isinstance(t.n, int) and t.n == 0 else t.n - 1)
                if (t + -2).real():
                    residual(t + -2)
                if i == 0 and isinstance(t.n, int) and t.n == 3:
                    v.wait_ge(s.done, 1)
                    norm_stats(v, n_b, Tile(0, 0))
            quads(v, last)
            if i == 0:
                norm_apply(v, n_b, Tile(0, 0))
            add(NE * NT - 1, NT - 1, 1)
            residual(LAST + -1)
            residual(LAST)

        @block.vector
        def _(v):
            def stats_a(t):
                if isinstance(t.n, int) and t.n < 2:
                    v.wait_ge((ld.x0, ld.x1)[t.n], 16)
                else:
                    v.wait_ge(ld.x, 16 * (NT - 2))
                norm_stats(v, n_a, t)

            v.wait_ge(ld.wa, 96)
            v.tensor_copy(LA[:, 0, :].rearrange("p (c h) -> p c h", c=DA),
                          WRAW[:, 5, :].rearrange("p (h c) -> p c h", c=DA)).then_inc(pr.wout, 1)
            stats_a(Tile(0, 0))
            v.wait_ge(pr.wtc, 6)
            v.memset(LA[:, 10:12, :], 0.0).then_inc(pr.la, 1)
            v.wait_ge(pr.la, 1)
            hd = lambda k: WT[:, k, :].rearrange("p (h d) -> p d h", d=DA)
            dh = lambda k: LA[:, k, :].rearrange("p (d h) -> p d h", d=DA)
            for k, w in ((0, 1), (2, 0)):
                v.tensor_copy(dh(k), hd(w)).then_inc(pr.la, 1)
                v.tensor_copy(dh(k + 1)[:, 0:2, :], hd(w)[:, 2:4, :]).then_inc(pr.la, 1)
                v.tensor_copy(dh(k + 1)[:, 2:4, :], hd(w)[:, 0:2, :]).then_inc(pr.la, 1)
            for c in range(DA):
                v.tensor_copy(dh(4 + c), spread(hd(2)[:, c, :], DA)).then_inc(pr.la, 1)
            for m in range(MA):
                hm = WT[:, 3, 0:HA * MA].rearrange("p (h m) -> p m h", m=MA)
                v.tensor_copy(dh(8 + m), spread(hm[:, m, :], DA)).then_inc(pr.la, 1)
            hm = WT[:, 4, 0:HA * MA].rearrange("p (h m) -> p m h", m=MA)
            for b in range(SPT):
                dst = LA[:, 10 + b, :].rearrange("p (b m h) -> p b m h", b=SPT, m=MA)
                for m in range(MA):
                    v.tensor_tensor(dst[:, b, m, :], hm[:, m, :], hm[:, 1 - m, :], ALU.subtract).then_inc(pr.la, 1)
            v.wait_ge(pr.la, 17)
            v.tensor_copy(LAH[:, :, :], LA[:, :, :]).then_inc(pr.la, 1)
            v.wait_ge(pr.la, 18)
            v.tensor_tensor(LAL[:, :, :], LA[:, :, :], LAH[:, :, :].bitcast(F32), ALU.subtract).then_inc(pr.la, 1)
            v.tensor_scalar(WOUT[:, :], WT[:, 5, :], 0.5, None, ALU.mult).then_inc(pr.wout, 1)
            v.wait_ge(pr.ba, 2)
            v.tensor_tensor(BMIXD[:, 0:1], BA[:, 1, 0:1], BA[:, 1, 1:2], ALU.subtract).then_inc(pr.bmix, 1)
            v.wait_ge(pr.bmix, 1)
            v.tensor_scalar(BMIXD[:, 1:2], BMIXD[:, 0:1], cst("sign"), None, ALU.mult).then_inc(pr.bmix, 1)

            def rope_part(t, k, name, table, dst):
                v.wait_ge(a_ready[name], t.n + 1)
                after(v, (A.u_k, A.u_q)[k], t.n)
                v.tensor_tensor(seqs(dst), seqs(bank[PBANK[name]]), spread(cst(table), SPT),
                                ALU.mult).then_inc(a_used[name], 1)

            def phi(t, k):
                v.wait_ge((A.re_k, A.re_q)[k], t.n + 1)
                if k == 0:
                    after(v, A.scan, 10 * t.n)
                else:
                    after(v, A.prod0, t.n - 1)
                    after(v, A.prod1, t.n - 1)
                v.scalar_tensor_tensor(KV[:, 4, :] if k == 0 else PQ[:, t.p, :], EX[:, k, :], 1.0, U[:, k, :],
                                       ALU.min, ALU.add).then_inc((A.phi_k, A.phi_q)[k], 1)

            def weighted(old, m):
                v.wait_ge(A.rs, 2 * old.n + m + 1)
                v.wait_ge(A.num, 2 * old.n + m + 1)
                after(v, A.y, old.n)
                v.tensor_tensor(AY[:, m, :], RS[:, m, :], bank[5 + m], ALU.mult).then_inc(A.ay, 1)

            def first_norm(t):
                first_norm_dve(v, t)

            def normalise_z(t):
                v.wait_ge(A.rstd2, t.n + 1)
                v.wait_ge(A.y, t.n + 1)
                for k in range(SUB):
                    v.tensor_scalar(ZN[:, k, :], Z[:, k, :], MV2[:, k, 0:1], RSTD2[:, k:k + 1], ALU.subtract,
                                    ALU.mult).then_inc(A.zn, 1)

            def scans(t, m):
                v.wait_ge(A.beta, t.n + 1)
                v.wait_ge(a_used["v3"], t.n + 1)
                after(v, A.den, t.n)
                after(v, A.num, 2 * (t.n - 1) + m + 1)
                for c in range(5):
                    v.tensor_tensor_scan(S[:, m, c, :], BETA[:, m, :], KV[:, c, :], 0.0, ALU.mult,
                                         ALU.add).then_inc(A.scan, 1)

            def step(t):
                nxt, old = t + 1, t + -1
                if t.real():
                    rope_part(t, 0, "k", "cos_a", R1[:, 0, :])
                    rope_part(t, 0, "ks", "sin_a", R2[:, 0, :])
                    rope_part(t, 1, "q", "cos_a", R1[:, 1, :])
                    rope_part(t, 1, "qs", "sin_a", R2[:, 1, :])
                if (t + -2).real():
                    normalise_z(t + -2)
                meanwhile(t, first_norm, (-1, 0, 1))
                if old.real():
                    v.wait_ge(A.den, old.n + 1)
                    v.tensor_scalar(DP[:, :], bank[4][:, 0:SEQ], DEN_EPS, None, ALU.add).then_inc(A.dp, 1)
                    v.wait_ge(A.dp, old.n + 1)
                    v.reciprocal(RC[:, :], DP[:, :]).then_inc(A.rc, 1)
                    v.wait_ge(A.rc, old.n + 1)
                    v.wait_ge(a_used["mx"], old.n + 1)
                    v.scalar_tensor_tensor(WGT[:, :], MIX[:, old.p, :], 1.0, RC[:, :], ALU.add,
                                           ALU.mult).then_inc(A.wgt, 1)
                if t.real():
                    phi(t, 0)
                    phi(t, 1)
                for c in range(DA):
                    if t.real():
                        v.wait_ge(A.phi_k, t.n + 1)
                        v.wait_ge(a_ready[f"v{c}"], t.n + 1)
                        v.tensor_tensor(KV[:, c, :], KV[:, 4, :], bank[PBANK[f"v{c}"]],
                                        ALU.mult).then_inc(a_used[f"v{c}"], 1)
                if old.real():
                    weighted(old, 0)
                if t.real():
                    scans(t, 0)
                if old.real():
                    weighted(old, 1)
                meanwhile(t, first_norm, (2,))
                if t.real():
                    v.wait_ge(A.scan, 10 * t.n + 5)
                    v.wait_ge(A.phi_q, t.n + 1)
                    v.tensor_tensor(S[:, 0, :, :], S[:, 0, :, :], spread(PQ[:, t.p, :], 5),
                                    ALU.mult).then_inc(A.prod0, 1)
                    scans(t, 1)
                if old.real():
                    v.wait_ge(A.z, old.n + 1)
                    after(v, A.zn, SUB * old.n)
                    v.tensor_tensor(Z[:, :, :], XN[:, old.p, :, :], by_sub(bank[4]), ALU.add).then_inc(A.zsum, 1)
                    v.wait_ge(A.zsum, old.n + 1)
                    after(v, A.mv2, SUB * old.n)
                    for k in range(SUB):
                        v.bn_stats(ST2[:, k, :], Z[:, k, :]).then_inc(A.st2, 1)
                    v.wait_ge(A.st2, SUB * (old.n + 1))
                    carry(v)
                    for k in range(SUB):
                        v.bn_aggr(MV2[:, k, :], ST2[:, k, :]).then_inc(A.mv2, 1)
                meanwhile(t, first_norm, (3, 4))
                if nxt.real():
                    after(v, A.zsum, nxt.n - 1)
                    norm_apply(v, n_a, nxt)
                if (t + 2).real():
                    stats_a(t + 2)
                if nxt.real():
                    after(v, a_ready["v3"], nxt.n - 1)
                    norm_lo(v, n_a, nxt, bank[0], XH[:, nxt.p, :], XL[:, nxt.p, :])

            v.wait_ge(pr.ones, 2)
            run_steps(v, step)
            normalise_z(LAST)
            for n in range(5, NT + 1):
                first_norm(Tile(n, n % 2))
            ffn_dve(v, 0)

            def maximum(t, b, k):
                n = t.n * SPT + b
                after(v, B.nml, 2 * (n - 1))
                v.wait_ge(B.row_ready, UNITS * n + k + 1)
                if k < NG:
                    dst, src = NM[:, b, 0, NJ * k:NJ * (k + 1)], r3(bank[k % 2], NJ)
                else:
                    h = 2 * (k - NG)
                    dst, src = NM[:, b, 1, h:h + 2], r3(bank[k % 2], 2)
                v.tensor_reduce(dst, src, AX.X, ALU.max, negate=True).then_inc(B.row_used, 1)

            def split_maxima(t, b):
                n = t.n * SPT + b
                v.wait_ge(B.row_used, UNITS * (n + 1))
                after(v, B.q2_ready, 2 * (n - 1))
                dst = lambda a, r: NMP[:, b, a, :, :].rearrange("p j (g r) -> p g j r", g=NG)[:, :, :, r]
                src = lambda a: NM[:, b, a, :].rearrange("p (g j) -> p g j", g=NG)
                for a in range(2):
                    v.tensor_copy(dst(a, 3 * DB), src(a)).then_inc(B.nmh, 1)
                v.wait_ge(B.nmh, 2 * (n + 1))
                for a in range(2):
                    v.tensor_tensor(dst(a, 3 * DB + 1), src(a), dst(a, 3 * DB).bitcast(F32),
                                    ALU.subtract).then_inc(B.nml, 1)

            def gather_sums(o, a):
                v.wait_ge(B.turn, 2 * o + a + 1)
                acc = bank[7].rearrange("p (j g r) -> p g j r", j=NJ, g=NG)
                after(v, B.o, o)
                ro = RO[:, a, :].rearrange("p (g j) -> p g j", g=NG)
                v.reciprocal(ro, acc[:, :, :, DB]).then_inc(B.ro, 1)
                v.wait_ge(B.ro, 2 * o + a + 1)
                ro = bass.AP(ro.tensor, ro.offset, [*ro.ap, [0, DB]])
                for i in range(2):
                    at = i * (DB + 1)
                    v.tensor_tensor(OC[:, i, a, :, :, :], acc[:, :, :, at:at + DB], ro, ALU.mult).then_inc(B.oc, 1)

            def normalise(o, ob):
                v.wait_ge(B.oc, 4 * (o + 1))
                after(v, B.ot, o - 1)
                oc = lambda i: OC[:, i, :, :, :, :].rearrange("p a g j c -> p (a g j c)")
                v.tensor_tensor(OB[:, ob, :, :].rearrange("p a c -> p (a c)"), oc(0), oc(1), ALU.add).then_inc(B.o, 1)

            def residual_b(n, t_n, b):
                v.wait_ge(B.out, n + 1)
                xs = X[:, t_n, 2 * b:2 * b + 2, :]
                v.tensor_tensor(xs, xs, bank[7][:, 0:2 * C].rearrange("p (a c) -> p a c", a=2),
                                ALU.add).then_inc(B.done, 1)

            def rope_b(t, k, name, table, dst, bias):
                v.wait_ge(b_ready[name], t.n + 1)
                after(v, (B.u_q, B.u_k)[k], t.n)
                v.scalar_tensor_tensor(seqs(dst), seqs(bank[6]), bias, spread(cst(table), SPT), ALU.add,
                                       ALU.mult).then_inc(b_used[name], 1)

            def split_b(nxt, i):
                v.wait_ge(B.hi, 2 * nxt.n + i + 1)
                after(v, B.kst_ready, nxt.n)
                v.tensor_tensor(QKL[:, i, :], QK[:, i, :], QKH[:, i, :].bitcast(F32), ALU.subtract).then_inc(B.lo, 1)

            def split_v(nxt):
                src = bank[6][:, 0:SUB * DB].rearrange("p (s c) -> p s c", s=SUB)
                part = lambda c: VS[:, nxt.p, :, VAT + c:VAT + c + DB]
                v.wait_ge(B.v_ready, nxt.n + 1)
                after(v, B.pv, 2 * UNITS * (nxt.n - 1))
                v.tensor_copy(part(0), src).then_inc(B.vhi, 1)
                v.wait_ge(B.vhi, nxt.n + 1)
                v.tensor_tensor(part(DB + 1), src, part(0).bitcast(F32),
                                ALU.subtract).then_inc(B.v_used, 1)

            def slot(t, b):
                nxt = t + 1
                n = t.n * SPT + b
                for k in range(UNITS):
                    if nxt.real():
                        if (b, k) == (0, 6):
                            rope_b(nxt, 0, "q", "cos_b", B1[:, 0, :], BQK[:, 0:1])
                        if (b, k) == (0, 8):
                            rope_b(nxt, 0, "qs", "sin_b", B2[:, 0, :], BQK[:, 1:2])
                        if (b, k) == (0, 10):
                            rope_b(nxt, 1, "k", "cos_b", B1[:, 1, :], BQK[:, 2:3])
                        if (b, k) == (1, 0):
                            rope_b(nxt, 1, "ks", "sin_b", B2[:, 1, :], BQK[:, 3:4])
                    if live(t, b, 2):
                        if k in (OUT_STEP + 1, OUT_STEP + 2):
                            gather_sums(n - 2, k - OUT_STEP - 1)
                        if k == OUT_STEP + 2:
                            normalise(n - 2, b)
                        if k == OUT_STEP + 6:
                            residual_b(n - 2, t.n - 1, b)
                    if t.real():
                        maximum(t, b, k)
                    if nxt.real():
                        if (b, k) == (0, 0) and t.real():
                            norm_apply(v, n_b, nxt)
                        if (b, k) == (0, 4):
                            after(v, B.v_ready, nxt.n - 1)
                            norm_lo(v, n_b, nxt, bank[6], XH[:, nxt.p, :], XL[:, nxt.p, :])
                        if (b, k) == (1, 2):
                            split_b(nxt, 0)
                        if (b, k) == (1, 4):
                            split_v(nxt)
                        if (b, k) == (1, 5):
                            split_b(nxt, 1)
                    if (t + 2).real() and (b, k) == (1, 10):
                        norm_stats(v, n_b, t + 2)
                    early = early_tile(t, b, k)
                    if early:
                        norm_lo(v, f[1], early, bank[early.p], XTH[:, early.n, :], XTL[:, early.n, :])
                    if (t + -2).real() and (b, k) == (0, 3):
                        early_stats(v, t + -2)
                    if (t + -2).real() and (b, k) == (0, 7):
                        early_apply(v, t + -2)
                if t.real():
                    split_maxima(t, b)

            v.wait_ge(f[0].done, NT)
            v.wait_ge(pr.zero, 6)
            v.wait_ge(pr.bqk, 2)
            run_slots(v, slot)
            ffn_dve(v, 1)


_INS = ["L0_attn_a_" + n for n in "x Wq Wk Wv Wbeta bbeta Wmix bmix Wout bout ln_g ln_b".split()] + \
       ["L0_attn_b_" + n for n in "Wq bq Wk bk Wv bv Wo bo".split()] + ["L0_ffn_" + n for n in "Wg Wu Wd".split()]


def kernel(**inputs):
    import numpy as _np
    import concourse.bacc as _bacc
    from concourse import mybir as _mybir
    from concourse.bass_utils import run_bass_kernel_spmd as _run

    nc = _bacc.Bacc("TRN2", target_bir_lowering=False, num_devices=1)
    arrays, args = {}, []
    for name in _INS:
        a = _np.ascontiguousarray(inputs[name])
        arrays[f"in_{name}_dram"] = a
        args.append(nc.dram_tensor(f"in_{name}_dram", a.shape, _mybir.dt.from_np(a.dtype), kind="ExternalInput").ap())
    tables = _np.concatenate(list(_C.values()), axis=1)
    arrays["in_tables_dram"] = tables
    args.append(nc.dram_tensor("in_tables_dram", tables.shape, _mybir.dt.float32, kind="ExternalInput").ap())
    shape = inputs["L0_attn_a_x"].shape
    args.append(nc.dram_tensor("out_0_dram", shape, _mybir.dt.float32, kind="ExternalOutput").ap())
    program(nc, *args)
    r = _run(nc, [arrays], core_ids=[0])
    return r.results[0]["out_0_dram"]
```
